# Optimizing a Trainium2 kernel written in Bass

```python
import numpy as np
import jax
import jax.numpy as jnp

def _softmax(x, axis=-1):
    return jax.nn.softmax(x, axis=axis)

def _gelu(x):
    return jax.nn.gelu(x, approximate=True)

def _silu(x):
    return jax.nn.silu(x)

def _sigmoid(x):
    return jax.nn.sigmoid(x)

def _layernorm(x, axis=-1, eps=1e-05):
    m = jnp.mean(x, axis=axis, keepdims=True)
    v = jnp.var(x, axis=axis, keepdims=True)
    return (x - m) / jnp.sqrt(v + eps)

def _scatter_add(tgt, idx, src, axis=0):
    return tgt.at[idx].add(src)

def _segment_sum(src, seg, n):
    return jax.ops.segment_sum(src, seg, n)
kernel_name = 'mk_recurrent_d2_jaxref_r8_f7e1cc'

def setup_inputs(seed: int=0):
    np.random.seed(seed)
    _w = jnp.asarray

    def _L0_attn_setup():
        import jax, jax.numpy as jnp
        import numpy as np
        D_MODEL = 256
        N_HEADS = 16
        HEAD_DIM = D_MODEL // N_HEADS
        BATCH = 2
        SEQ = 256

        def apply_rope(x):
            b, h, t, d = x.shape
            half = d // 2
            pos = jnp.arange(t, dtype=x.dtype)[:, None]
            inv_freq = 1.0 / 10000.0 ** (jnp.arange(half, dtype=x.dtype) / half)
            angles = pos * inv_freq[None, :]
            sin = jnp.sin(angles)[None, None]
            cos = jnp.cos(angles)[None, None]
            x1, x2 = (x[..., :half], x[..., half:])
            return jnp.concatenate([x1 * cos - x2 * sin, x1 * sin + x2 * cos], axis=-1)
        key = jax.random.key(seed)
        ks = jax.random.split(key, 5)
        scale = 1.0 / np.sqrt(D_MODEL)
        x = jax.random.normal(ks[0], (BATCH, SEQ, D_MODEL), dtype=jnp.float32)
        Wq = jax.random.normal(ks[1], (D_MODEL, D_MODEL), dtype=jnp.float32) * scale
        Wk = jax.random.normal(ks[2], (D_MODEL, D_MODEL), dtype=jnp.float32) * scale
        Wv = jax.random.normal(ks[3], (D_MODEL, D_MODEL), dtype=jnp.float32) * scale
        Wo = jax.random.normal(ks[4], (D_MODEL, D_MODEL), dtype=jnp.float32) * scale
        return {'x': x, 'Wq': Wq, 'Wk': Wk, 'Wv': Wv, 'Wo': Wo}
    _L0_attn_in = _L0_attn_setup()

    def _L0_ffn_setup():
        import jax, jax.numpy as jnp
        import numpy as np
        ALPHA = 1.702
        LIMIT = 7.0
        TOP_K = 4
        B, S, H = (1, 128, 256)
        E, D = (16, 256)
        key = jax.random.key(seed)
        ks = jax.random.split(key, 7)
        s = 0.02
        return {'hidden_states': jax.random.normal(ks[0], (B, S, H), dtype=jnp.float32), 'router_weight': jax.random.normal(ks[1], (E, H), dtype=jnp.float32) * s, 'router_bias': jax.random.normal(ks[2], (E,), dtype=jnp.float32) * s, 'gate_up_proj': jax.random.normal(ks[3], (E, H, 2 * D), dtype=jnp.float32) * s, 'gate_up_proj_bias': jax.random.normal(ks[4], (E, 2 * D), dtype=jnp.float32) * s, 'down_proj': jax.random.normal(ks[5], (E, D, H), dtype=jnp.float32) * s, 'down_proj_bias': jax.random.normal(ks[6], (E, H), dtype=jnp.float32) * s}
    _L0_ffn_in = _L0_ffn_setup()

    def _L1_attn_setup():
        import jax, jax.numpy as jnp
        import numpy as np
        B, N, E = (4, 512, 256)
        H_DIM = 256
        HEADS = 16
        DH = H_DIM // HEADS
        LN_EPS = 1e-05

        def _heads(t):
            b, n, _ = t.shape
            return t.reshape(b, n, HEADS, DH).transpose(0, 2, 1, 3)

        def _layernorm(x, g, b):
            mu = jnp.mean(x, axis=-1, keepdims=True)
            var = jnp.mean(jnp.square(x - mu), axis=-1, keepdims=True)
            return (x - mu) * jax.lax.rsqrt(var + LN_EPS) * g + b
        key = jax.random.key(seed)
        ks = jax.random.split(key, 10)
        s = 1.0 / np.sqrt(E)
        so = 1.0 / np.sqrt(H_DIM)
        return {'x': jax.random.normal(ks[0], (B, N, E), jnp.float32), 'Wqk': jax.random.normal(ks[1], (E, H_DIM), jnp.float32) * s, 'bqk': jnp.zeros((H_DIM,), jnp.float32), 'Wv': jax.random.normal(ks[2], (E, H_DIM), jnp.float32) * s, 'bv': jnp.zeros((H_DIM,), jnp.float32), 'Wu': jax.random.normal(ks[3], (E, H_DIM), jnp.float32) * s, 'bu': jnp.zeros((H_DIM,), jnp.float32), 'Wo': jax.random.normal(ks[4], (H_DIM, E), jnp.float32) * so, 'bo': jnp.zeros((E,), jnp.float32), 'ln_g': jnp.ones((H_DIM,), jnp.float32), 'ln_b': jnp.zeros((H_DIM,), jnp.float32)}
    _L1_attn_in = _L1_attn_setup()

    def _L1_ffn_setup():
        import jax, jax.numpy as jnp
        import numpy as np
        B, S, H = (1, 128, 256)
        E = 32
        K = 4
        I = 96
        SI = 512
        WSCALE = 0.02
        key = jax.random.key(seed)
        ks = jax.random.split(key, 8)
        inp = {'hidden_states': jax.random.normal(ks[0], (B, S, H), jnp.float32), 'router_w': jax.random.normal(ks[1], (H, E), jnp.float32) * WSCALE, 'w_gate': jax.random.normal(ks[2], (E, H, I), jnp.float32) * WSCALE, 'w_up': jax.random.normal(ks[3], (E, H, I), jnp.float32) * WSCALE, 'w_down': jax.random.normal(ks[4], (E, I, H), jnp.float32) * WSCALE, 'ws_gate': jax.random.normal(ks[5], (H, SI), jnp.float32) * WSCALE, 'ws_up': jax.random.normal(ks[6], (H, SI), jnp.float32) * WSCALE, 'ws_down': jax.random.normal(ks[7], (SI, H), jnp.float32) * WSCALE}
        return inp
    _L1_ffn_in = _L1_ffn_setup()
    _d = {'L0_attn_x': _L0_attn_in['x'], 'L0_attn_Wq': _L0_attn_in['Wq'], 'L0_attn_Wk': _L0_attn_in['Wk'], 'L0_attn_Wv': _L0_attn_in['Wv'], 'L0_attn_Wo': _L0_attn_in['Wo'], 'L0_ffn_router_weight': _L0_ffn_in['router_weight'], 'L0_ffn_router_bias': _L0_ffn_in['router_bias'], 'L0_ffn_gate_up_proj': _L0_ffn_in['gate_up_proj'], 'L0_ffn_gate_up_proj_bias': _L0_ffn_in['gate_up_proj_bias'], 'L0_ffn_down_proj': _L0_ffn_in['down_proj'], 'L0_ffn_down_proj_bias': _L0_ffn_in['down_proj_bias'], 'L1_attn_Wqk': _L1_attn_in['Wqk'], 'L1_attn_bqk': _L1_attn_in['bqk'], 'L1_attn_Wv': _L1_attn_in['Wv'], 'L1_attn_bv': _L1_attn_in['bv'], 'L1_attn_Wu': _L1_attn_in['Wu'], 'L1_attn_bu': _L1_attn_in['bu'], 'L1_attn_Wo': _L1_attn_in['Wo'], 'L1_attn_bo': _L1_attn_in['bo'], 'L1_attn_ln_g': _L1_attn_in['ln_g'], 'L1_attn_ln_b': _L1_attn_in['ln_b'], 'L1_ffn_router_w': _L1_ffn_in['router_w'], 'L1_ffn_w_gate': _L1_ffn_in['w_gate'], 'L1_ffn_w_up': _L1_ffn_in['w_up'], 'L1_ffn_w_down': _L1_ffn_in['w_down'], 'L1_ffn_ws_gate': _L1_ffn_in['ws_gate'], 'L1_ffn_ws_up': _L1_ffn_in['ws_up'], 'L1_ffn_ws_down': _L1_ffn_in['ws_down']}
    _x0 = _d['L0_attn_x']
    _d['L0_attn_x'] = jax.random.normal(jax.random.fold_in(jax.random.key(seed), 1), (4, 256, 256), dtype=_x0.dtype)
    del _x0
    return _d

def reference(L0_attn_x, L0_attn_Wq, L0_attn_Wk, L0_attn_Wv, L0_attn_Wo, L0_ffn_router_weight, L0_ffn_router_bias, L0_ffn_gate_up_proj, L0_ffn_gate_up_proj_bias, L0_ffn_down_proj, L0_ffn_down_proj_bias, L1_attn_Wqk, L1_attn_bqk, L1_attn_Wv, L1_attn_bv, L1_attn_Wu, L1_attn_bu, L1_attn_Wo, L1_attn_bo, L1_attn_ln_g, L1_attn_ln_b, L1_ffn_router_w, L1_ffn_w_gate, L1_ffn_w_up, L1_ffn_w_down, L1_ffn_ws_gate, L1_ffn_ws_up, L1_ffn_ws_down):

    def _L0_attn_ref(x, Wq, Wk, Wv, Wo):
        import jax, jax.numpy as jnp
        import numpy as np
        D_MODEL = 256
        N_HEADS = 16
        HEAD_DIM = D_MODEL // N_HEADS
        BATCH = 2
        SEQ = 256

        def apply_rope(x):
            b, h, t, d = x.shape
            half = d // 2
            pos = jnp.arange(t, dtype=x.dtype)[:, None]
            inv_freq = 1.0 / 10000.0 ** (jnp.arange(half, dtype=x.dtype) / half)
            angles = pos * inv_freq[None, :]
            sin = jnp.sin(angles)[None, None]
            cos = jnp.cos(angles)[None, None]
            x1, x2 = (x[..., :half], x[..., half:])
            return jnp.concatenate([x1 * cos - x2 * sin, x1 * sin + x2 * cos], axis=-1)
        b, t, _ = x.shape

        def proj(W):
            y = jnp.einsum('btd,ed->bte', x, W)
            return y.reshape(b, t, N_HEADS, HEAD_DIM).transpose(0, 2, 1, 3)
        q = apply_rope(proj(Wq))
        k = apply_rope(proj(Wk))
        v = proj(Wv)
        scores = jnp.einsum('bhqd,bhkd->bhqk', q, k) / np.sqrt(HEAD_DIM)
        causal = jnp.tril(jnp.ones((t, t), dtype=bool))
        scores = jnp.where(causal[None, None], scores, -jnp.inf)
        attn = jax.nn.softmax(scores, axis=-1)
        out = jnp.einsum('bhqk,bhkd->bhqd', attn, v)
        out = out.transpose(0, 2, 1, 3).reshape(b, t, D_MODEL)
        return jnp.einsum('btd,ed->bte', out, Wo)

    def _L0_ffn_ref(hidden_states, router_weight, router_bias, gate_up_proj, gate_up_proj_bias, down_proj, down_proj_bias):
        import jax, jax.numpy as jnp
        import numpy as np
        ALPHA = 1.702
        LIMIT = 7.0
        TOP_K = 4
        B, S, H = (1, 128, 256)
        E, D = (16, 256)
        batch, seq, hdim = hidden_states.shape
        x = hidden_states.reshape(-1, hdim)
        T = x.shape[0]
        logits = x @ router_weight.T + router_bias
        top_val, top_idx = jax.lax.top_k(logits, TOP_K)
        top_val = jax.nn.softmax(top_val, axis=-1)
        router_scores = jnp.zeros_like(logits).at[jnp.arange(T)[:, None], top_idx].set(top_val)
        gate_up = jnp.einsum('th,ehd->etd', x, gate_up_proj) + gate_up_proj_bias[:, None, :]
        gate = gate_up[..., ::2]
        up = gate_up[..., 1::2]
        gate = jnp.minimum(gate, LIMIT)
        up = jnp.clip(up, -LIMIT, LIMIT)
        glu = gate * jax.nn.sigmoid(gate * ALPHA)
        out = jnp.einsum('etd,edh->eth', (up + 1.0) * glu, down_proj) + down_proj_bias[:, None, :]
        out = out * router_scores.T[:, :, None]
        out = out.sum(axis=0)
        return out.reshape(batch, seq, hdim)

    def _L1_attn_ref(x, Wqk, bqk, Wv, bv, Wu, bu, Wo, bo, ln_g, ln_b):
        import jax, jax.numpy as jnp
        import numpy as np
        B, N, E = (4, 512, 256)
        H_DIM = 256
        HEADS = 16
        DH = H_DIM // HEADS
        LN_EPS = 1e-05

        def _heads(t):
            b, n, _ = t.shape
            return t.reshape(b, n, HEADS, DH).transpose(0, 2, 1, 3)

        def _layernorm(x, g, b):
            mu = jnp.mean(x, axis=-1, keepdims=True)
            var = jnp.mean(jnp.square(x - mu), axis=-1, keepdims=True)
            return (x - mu) * jax.lax.rsqrt(var + LN_EPS) * g + b
        q = x @ Wqk + bqk
        k = x @ Wqk + bqk
        v = jax.nn.silu(x @ Wv + bv)
        u = jax.nn.silu(x @ Wu + bu)
        q = jax.nn.elu(_heads(q))
        kh = jax.nn.elu(_heads(k))
        vh = _heads(v)
        kv = jnp.einsum('bhnd,bhne->bhde', kh, vh)
        out = jnp.einsum('bhnd,bhde->bhne', q, kv)
        out = out.transpose(0, 2, 1, 3).reshape(x.shape[0], x.shape[1], H_DIM)
        out = _layernorm(out, ln_g, ln_b)
        out = u * out
        return out @ Wo + bo

    def _L1_ffn_ref(hidden_states, router_w, w_gate, w_up, w_down, ws_gate, ws_up, ws_down):
        import jax, jax.numpy as jnp
        import numpy as np
        B, S, H = (1, 128, 256)
        E = 32
        K = 4
        I = 96
        SI = 512
        WSCALE = 0.02
        b, s, h = hidden_states.shape
        x = hidden_states.reshape(-1, h)
        T = x.shape[0]
        shared = jax.nn.silu(x @ ws_gate) * (x @ ws_up) @ ws_down
        logits = x @ router_w
        probs = jax.nn.softmax(logits.astype(jnp.float32), axis=-1)
        topw, topi = jax.lax.top_k(probs, K)
        topw = topw / jnp.sum(topw, axis=-1, keepdims=True)
        topw = topw.astype(hidden_states.dtype)
        combine = jnp.zeros((T, E), hidden_states.dtype).at[jnp.arange(T)[:, None], topi].add(topw)
        g = jnp.einsum('th,ehi->eti', x, w_gate)
        u = jnp.einsum('th,ehi->eti', x, w_up)
        hmid = jax.nn.silu(g) * u
        routed = jnp.einsum('eti,te,eih->th', hmid, combine, w_down)
        return (shared + routed).reshape(b, s, h)
    x = L0_attn_x
    xn = _layernorm(x, axis=-1)
    s = _L0_attn_ref(xn, L0_attn_Wq, L0_attn_Wk, L0_attn_Wv, L0_attn_Wo)
    g = _silu(_L0_ffn_ref(xn, L0_ffn_router_weight, L0_ffn_router_bias, L0_ffn_gate_up_proj, L0_ffn_gate_up_proj_bias, L0_ffn_down_proj, L0_ffn_down_proj_bias))
    x = x + s * g
    xn = _layernorm(x, axis=-1)
    s = _L1_attn_ref(xn, L1_attn_Wqk, L1_attn_bqk, L1_attn_Wv, L1_attn_bv, L1_attn_Wu, L1_attn_bu, L1_attn_Wo, L1_attn_bo, L1_attn_ln_g, L1_attn_ln_b)
    g = _silu(_L1_ffn_ref(xn, L1_ffn_router_w, L1_ffn_w_gate, L1_ffn_w_up, L1_ffn_w_down, L1_ffn_ws_gate, L1_ffn_ws_up, L1_ffn_ws_down))
    x = x + s * g
    return x

_drawn_inputs = setup_inputs


def setup_inputs(seed=0):
    import zlib

    import numpy as np

    out = dict(_drawn_inputs(seed))
    spreads = {'L1_attn_bqk': (0.0, 0.8),
     'L1_attn_bv': (0.0, 0.8),
     'L1_attn_bu': (0.0, 0.8),
     'L1_attn_bo': (0.0, 0.8),
     'L1_attn_ln_g': (1.0, 0.6),
     'L1_attn_ln_b': (0.0, 0.8)}
    factors = {'L0_attn_Wq': 8.0,
     'L0_attn_Wk': 8.0,
     'L0_attn_Wv': 8.0,
     'L0_attn_Wo': 8.0,
     'L0_ffn_router_weight': 8.0,
     'L0_ffn_router_bias': 8.0,
     'L0_ffn_gate_up_proj': 8.0,
     'L0_ffn_gate_up_proj_bias': 8.0,
     'L0_ffn_down_proj': 8.0,
     'L0_ffn_down_proj_bias': 8.0,
     'L1_attn_Wqk': 7.711,
     'L1_attn_Wv': 8.0,
     'L1_attn_Wu': 7.894,
     'L1_attn_Wo': 7.315,
     'L1_ffn_router_w': 8.0,
     'L1_ffn_w_gate': 8.0,
     'L1_ffn_w_up': 8.0,
     'L1_ffn_w_down': 8.0,
     'L1_ffn_ws_gate': 7.484,
     'L1_ffn_ws_up': 7.381,
     'L1_ffn_ws_down': 7.391}
    for name, (base, spread) in spreads.items():
        noise = np.random.default_rng([zlib.crc32(name.encode()), seed]).standard_normal(out[name].shape)
        drawn = base * np.exp(spread * noise) if base else spread * noise
        out[name] = jnp.asarray(drawn.astype(out[name].dtype))
    for name, factor in factors.items():
        out[name] = (out[name] * factor).astype(out[name].dtype)
    return out
```

```python
import concourse.bass as bass
from concourse import mybir
from contextlib import ExitStack

P = 128
D = 256
KD = D // P
TOK = 1024
NTT = TOK // P
TOPK = 4
HEADS, DH = 16, 16
BATCH, SEQ = 4, 256
PAIRS = 8
MASKED = -1.0e30

E0, F0 = 16, 256
E1, F1 = 32, 96
SH = 512
LIMIT, ALPHA = 7.0, 1.702
EPS = 1e-5


def tiles_needed(experts):
    n = TOK * TOPK // P + experts - 1
    return -(-n // 4) * 4


NT0, NT1 = tiles_needed(E0), tiles_needed(E1)

C_ID, C_IOTA, C_TOK, C_MASK, C_TRI, C_BD, C_COS, C_SIN, C_PMOD, C_END = (
    0, 128, 256, 264, 392, 520, 648, 680, 712, 713)


def constants():
    import numpy as np
    c = np.zeros((P, C_END), np.float32)
    p, f = np.arange(P)[:, None], np.arange(P)[None, :]
    c[:, C_ID:C_ID + P] = p == f
    c[:, C_IOTA:C_IOTA + P] = f
    c[:, C_TOK:C_TOK + NTT] = p + P * np.arange(NTT)[None, :]
    c[:, C_MASK:C_MASK + P] = np.where(f > p, MASKED, 0.0)
    c[:, C_TRI:C_TRI + P] = p < f
    c[:, C_BD:C_BD + P] = p // DH == f // DH
    half = DH // 2
    freq = (np.float32(1.0) / np.float32(10000.0) ** (np.arange(half, dtype=np.float32) / np.float32(half))).astype(np.float32)
    for t in range(SEQ // P):
        ang = ((p + t * P).astype(np.float32) * freq[None, :]).astype(np.float32)
        co, si = np.cos(ang), np.sin(ang)
        c[:, C_COS + DH * t:C_COS + DH * (t + 1)] = np.concatenate([co, co], axis=1)
        c[:, C_SIN + DH * t:C_SIN + DH * (t + 1)] = np.concatenate([-si, si], axis=1)
    c[:, C_PMOD:C_PMOD + 1] = p % 32
    return c


def build_program(nc, x, consts, wqkv0, wo0, wr0, rb0, gub0, dnb0, gu0, dn0,
                  wqvu1, b768, wo1, lnrow, bo1, wr1, gu1, dn1, wsgu, wsdn, out):
    f32, bf16, i32, u32 = mybir.dt.float32, mybir.dt.bfloat16, mybir.dt.int32, mybir.dt.uint32
    ALU, ACT, AX = mybir.AluOpType, mybir.ActivationFunctionType, mybir.AxisListType
    ctx = ExitStack()
    with ctx:
        def sb(name, shape, dt=f32):
            return ctx.enter_context(nc.sbuf_tensor(name, shape, dt))

        def sem(name):
            return ctx.enter_context(nc.semaphore(name))

        xn_dram = [nc.dram_tensor(f"xn_rows{n}", (TOK, D), f32, kind="Internal").ap() for n in (0, 1)]
        ys_dram = [nc.dram_tensor(f"sorted_rows{n}", (nt * P, D), f32, kind="Internal").ap()
                   for n, nt in ((0, NT0), (1, NT1))]

        cst = sb("cst", [P, C_END])
        ident = cst[:, C_ID:C_ID + P]
        iota = cst[:, C_IOTA:C_IOTA + P]
        tokid = cst[:, C_TOK:C_TOK + NTT]
        bdiag = cst[:, C_BD:C_BD + P]
        pmod = cst[:, C_PMOD:C_PMOD + 1]
        ident_bf = sb("ident_bf", [P, P], bf16)
        mask_bf = sb("mask_bf", [P, P], bf16)
        tri_bf = sb("tri_bf", [P, P], bf16)
        ones_bf = sb("ones_bf", [P, P], bf16)
        ones_e = sb("ones_e", [P, E1])

        big = sb("experts", [P, E0 * KD * 2 * F0 + E0 * KD * D])
        GU0 = E0 * KD * 2 * F0
        GU1 = E1 * KD * 2 * F1
        gu0_sb, dn0_sb = big[:, 0:GU0], big[:, GU0:]
        gu1_sb, dn1_sb = big[:, 0:GU1], big[0:F1, GU0:]
        wsgu_sb = big[:, GU1:GU1 + KD * 2 * SH].rearrange("p (k n) -> p k n", k=KD)
        off = GU1 + KD * 2 * SH
        wsdn_sb = big[:, off:off + 4 * D].rearrange("p (k n) -> p k n", k=4)
        off += 4 * D
        wo1_sb = big[:, off:off + KD * D].rearrange("p (k n) -> p k n", k=KD)
        off += KD * D
        lng_sb, bo1_sb = big[:, off:off + D], big[:, off + D:off + 2 * D]
        assert off + 2 * D <= GU0
        wqkv_sb = sb("wqkv", [P, KD, 3 * D])
        wo0_sb = sb("wo0", [P, KD, D])
        b768_sb = sb("b768", [P, 3 * D])
        lnb_sb = sb("lnb", [P, D])
        wr0_sb = sb("wr0", [P, KD, E0])
        wr1_sb = sb("wr1", [P, KD, E1])
        rb0_sb = sb("rb0", [P, E0])
        gub_bf = sb("gub_bf", [96, 2 * F0], bf16)
        dnb_bf = sb("dnb_bf", [96, D], bf16)

        xr = sb("xr", [P, NTT, D])
        xn = sb("xn", [P, NTT, D])

        att = sb("att", [P, 9856])
        qk_raw = att[:, 0:4096].rearrange("p (t n) -> p t n", t=NTT)
        v_aug = att[:, 4096:6272].rearrange("p (t h d) -> p t h d", t=NTT, h=HEADS)
        stage0 = 6272
        xnT0 = att[:, stage0:stage0 + 2048].rearrange("p (k t) -> p k t", k=KD)
        qst = att[:, 6272:7296].rearrange("p (t a n) -> p t a n", t=2, a=2)
        kst = att[:, 7296:7808].rearrange("p (t n) -> p t n", t=2)
        qTs = att[:, 7808:8832].rearrange("p (a g t) -> p a g t", a=2, g=2)
        kTs = att[:, 8832:9344].rearrange("p (g t) -> p g t", g=2)
        ost = att[:, 9344:9856].rearrange("p (t n) -> p t n", t=2)
        q1r, v1r, u1r = (att[:, 2048 * n:2048 * (n + 1)].rearrange("p (t n) -> p t n", t=NTT)
                         for n in range(3))
        kvb = att[:, 6144:6656].rearrange("p (s g n) -> p s g n", s=2, g=2)
        xnT1 = att[:, 6656:8704].rearrange("p (k t) -> p k t", k=KD)
        q1T = xn[:, :, :].rearrange("p t n -> p (t n)").rearrange("p (g t) -> p g t", g=2)

        til = sb("til", [P, 5120])
        xg = til[:, 0:1024].rearrange("p (s n) -> p s n", s=4)
        xgT = til[:, 1024:1536].rearrange("p (s k t) -> p s k t", s=2, k=KD)
        gbuf = til[:, 1536:2048].rearrange("p (s n) -> p s n", s=2)
        ubuf = til[:, 2048:2560].rearrange("p (s n) -> p s n", s=2)
        sig = til[:, 2560:3072].rearrange("p (s n) -> p s n", s=2)
        hbuf = til[:, 3072:3584].rearrange("p (s n) -> p s n", s=2)
        hT = til[:, 3584:4096].rearrange("p (s k t) -> p s k t", s=2, k=KD)
        ybuf = til[:, 4096:5120].rearrange("p (s n) -> p s n", s=4)
        pr = til[:, 0:1536].rearrange("p (s m n) -> p s m n", s=2, m=2)
        prT = til[:, 1536:3072].rearrange("p (s m n) -> p s m n", s=2, m=2)
        g0r = til[:, 3072:5120].rearrange("p (t n) -> p t n", t=NTT)
        shg = til[:, 0:2048].rearrange("p (m t) -> p m t", m=4)
        shs = til[:, 2048:3072].rearrange("p (s t) -> p s t", s=2)
        a1T = til[:, 3072:3584].rearrange("p (s k t) -> p s k t", s=2, k=KD)
        fbuf = til[:, 3584:4096].rearrange("p (s n) -> p s n", s=2)
        fsig = til[:, 4096:4608].rearrange("p (s n) -> p s n", s=2)

        rou = sb("rou", [P, 3584])
        oh = rou[:, 0:512].bitcast(bf16)
        sl4 = rou[:, 512:1536]
        amat = rou[:, 1536:2560].rearrange("p (s k n) -> p s k n", s=2, k=TOPK)
        bmat = rou[:, 2560:3584].rearrange("p (s k n) -> p s k n", s=2, k=TOPK)
        cg = rou[:, 0:2048].rearrange("p (s k n) -> p s k n", s=2, k=TOPK)
        csum = rou[:, 2048:2560]
        cf = rou[:, 2560:3072].rearrange("p (s n) -> p s n", s=2)
        rtmp = rou[:, 3072:3584].rearrange("p (h d) -> p h d", d=DH)
        gub_f, dnb_f, bsp = til[0:96, 0:512], til[0:96, 512:768], til[0:96, 768:1024].bitcast(bf16)
        sh1r = big[:, 0:2048].rearrange("p (t n) -> p t n", t=NTT)
        a1r = big[:, 2048:4096].rearrange("p (t n) -> p t n", t=NTT)
        s1r = big[:, 4096:6144].rearrange("p (t n) -> p t n", t=NTT)
        rowtmp = big[:, 6144:10240].rearrange("p (w t n) -> p w t n", w=2, t=NTT)

        bnst = sb("bnst", [P, NTT, 6])
        mv = sb("mv", [P, NTT, 2])
        sd = sb("sd", [P, NTT])
        rstd = sb("rstd", [P, NTT])
        lgt = sb("lgt", [P, NTT * E1])
        top = sb("top", [P, NTT, 8])
        topi = sb("topi", [P, NTT, 8], u32)
        topf = sb("topf", [P, NTT, TOPK])
        wraw = sb("wraw", [P, NTT, TOPK])
        wsum = sb("wsum", [P, NTT])
        wtop = sb("wtop", [P, NTT, TOPK])
        mcnt = sb("mcnt", [P, NTT * E1], bf16)
        nti = sb("nti", [P, E1], i32)
        nts = sb("nts", [P, E1])
        enda = sb("enda", [P, E1])
        base = sb("base", [P, E1])
        slotf = sb("slotf", [P, NTT * TOPK])
        sloti = sb("sloti", [P, NTT * TOPK], i32)
        slotu = [sb(f"slotu{n}", [P, NTT * TOPK], u32) for n in (0, 1)]
        tq = sb("tq", [P, NTT * TOPK], i32)
        tqf = sb("tqf", [P, NTT * TOPK])
        smf = sb("smf", [P, NTT * TOPK])
        gidx = sb("gidx", [P, NT1], u32)
        wtile = sb("wtile", [P, NT1])
        texf = sb("texf", [P, NT1])
        texi = sb("texi", [P, NT1], i32)
        selc = sb("selc", [96, NT0], bf16)
        idxs = sb("idxs", [P, 4], u32)
        idx4 = sb("idx4", [P, 2, TOPK], u32)
        mxs = sb("mxs", [P, 2, 4])
        rec = sb("rec", [P, 2, HEADS])

        ps = ctx.enter_context(nc.psum_tensor("ps", [P, 8, 512], f32))
        psf = ps[:, :, :].rearrange("p b n -> p (b n)")

        s_cst, s_x, s_wr, s_bias, s_wqkv, s_w0, s_w1, s_wqvu1, s_small1, s_tab1 = map(sem, (
            "cst_in", "x_in", "wr_in", "bias_in", "wqkv_in", "experts0_in", "experts1_in", "wqvu1_in",
            "small1_in", "tables1_in"))
        s_cbf = sem("casts_done")
        s_bsp = sem("bias_split_done")
        s_pool = sem("pool_chain")
        s_dve = sem("dve_chain")
        s_act = sem("act_chain")
        s_out = sem("out_stored")

        class Layer:

            def __init__(self, n):
                self.n, self.E, self.F, self.NT = n, (E0, E1)[n], (F0, F1)[n], (NT0, NT1)[n]
                self.KF, self.FP = -(-self.F // P), min(self.F, P)
                self.xnT = (xnT0, xnT1)[n]
                self.wr = (wr0_sb, wr1_sb)[n]
                self.ve_ready = sem(f"variances{n}")
                self.sd_ready = sem(f"deviations{n}")
                self.xn_ready = sem(f"xn_ready{n}")
                self.xn_stored = sem(f"xn_stored{n}")
                self.xT_done = sem(f"xnT_done{n}")
                self.xnT_ready = sem(f"xnT_ready{n}")
                self.qkv_done = sem(f"projected{n}")
                self.qkv_read = sem(f"projected_read{n}")
                self.logits_done = sem(f"logits_done{n}")
                self.wexp_in = sem(f"top_logits{n}")
                self.wexp_out = sem(f"top_exps{n}")
                self.m_ready = sem(f"choices{n}")
                self.rank_done = sem(f"ranks_done{n}")
                self.ab_ready = sem(f"onehots_ready{n}")
                self.ab_used = sem(f"onehots_used{n}")
                self.idx_ready = sem(f"tile_lists_ready{n}")
                self.icol = sem(f"index_column{n}")
                self.xg_full = [sem(f"gathered{n}_{j}") for j in range(4)]
                self.xgT_done = sem(f"gathered_turned{n}")
                self.xgT_ready = sem(f"xgT_ready{n}")
                self.gu_done = sem(f"gate_up_done{n}")
                self.g_ready = sem(f"gate_ready{n}")
                self.u_ready = sem(f"up_ready{n}")
                self.sig_ready = sem(f"sigmoid_ready{n}")
                self.h1_ready = sem(f"half_gated{n}")
                self.h_ready = sem(f"hidden_ready{n}")
                self.hT_done = sem(f"hidden_turned{n}")
                self.hT_ready = sem(f"hT_ready{n}")
                self.y_done = sem(f"down_done{n}")
                self.y_ready = sem(f"weighted_ready{n}")
                self.y_stored = [sem(f"weighted_stored{n}_{j}") for j in range(4)]
                self.icol4 = sem(f"index_rows{n}")
                self.cg_full = [sem(f"four_rows{n}_{j}") for j in range(2)]
                self.cg_read = sem(f"four_rows_read{n}")
                self.f_ready = sem(f"expert_sum_ready{n}")
                self.fsig_ready = sem(f"expert_sum_sigmoid{n}")
                self.g_done = sem(f"block_rows_ready{n}")

        L = [Layer(0), Layer(1)]
        s_rope, s_qkT, s_qkTr, s_sc, s_mx, s_sub, s_exp, s_pT, s_pTr, s_pv, s_rec, s_on, s_oT, s_oTr, s_wo, s_s = map(sem, (
            "rope_done", "qkT_done", "qkT_read", "scores_done", "max_ready", "shifted_ready", "probs_ready",
            "probsT_done", "probsT_ready", "pv_done", "recip_ready", "attn_ready", "attnT_done", "attnT_ready",
            "wo_done", "s_ready"))
        s_x1 = sem("x1_ready")
        s_rst = sem("rope_steps")
        s_vone = sem("v_ones_ready")
        s_here = sem("waits_taken")
        s_shrow, s_bn1, s_a1n = map(sem, ("shared_rows_read", "stats1_ready", "a1_gated"))
        s_z, s_e, s_row1, s_qT1, s_qT1r, s_kv, s_kvr, s_o1, s_ln1, s_sd1, s_a1, s_a1T, s_a1Tr, s_wo1, s_s1, s_shd, s_shsig, s_shr, s_sdn = map(sem, (
            "z_ready", "zfun_ready", "rows1_ready", "q1T_done", "q1T_ready", "kv_done", "kv_ready", "o1_done",
            "ln1_var", "ln1_sd", "a1_ready", "a1T_done", "a1T_ready", "wo1_done", "s1_ready",
            "shared_up_done", "shared_sig", "shared_ready", "shared_down_done"))

        def ge(eng, s, v):
            if not isinstance(v, int) or v > 0:
                eng.wait_ge(s, v)

        def run_tiles(eng, s, stages):
            def step(t, j, first, last):
                for n, stage in enumerate(stages):
                    if stage is not None and first >= n and last <= n:
                        stage(t - n, (j - n) % 4)

            for t in range(8):
                step(t, t % 4, t, 0)
            with eng.Fori(2, s.NT // 4) as g:
                for j in range(4):
                    step(g * 4 + j, j, 3, 0)
            for j in range(3):
                step(s.NT + j, j, 3, j + 1)

        block = ctx.enter_context(nc.Block())

        @block.sync
        def _(sp):
            sp.dma_start(xr[:, :, :], x.rearrange("(t p) d -> p t d", p=P)).then_inc(s_x, 16)
            sp.dma_start(cst[:, :], consts).then_inc(s_cst, 16)
            sp.dma_start(wr0_sb[:, :, :], wr0).then_inc(s_wr, 16)
            sp.dma_start(rb0_sb[:, :], rb0.partition_broadcast(P)).then_inc(s_wr, 16)
            sp.dma_start(wqkv_sb[:, :, :], wqkv0).then_inc(s_wqkv, 16)
            sp.dma_start(wo0_sb[:, :, :], wo0).then_inc(s_wqkv, 16)
            for j in range(3):
                sp.dma_start(gub_f[32 * j:32 * j + E0, :], gub0).then_inc(s_bias, 16)
                sp.dma_start(dnb_f[32 * j:32 * j + E0, :], dnb0).then_inc(s_bias, 16)
            sp.dma_start(wr1_sb[:, :, :], wr1).then_inc(s_small1, 16)
            sp.dma_start(b768_sb[:, :], b768.partition_broadcast(P)).then_inc(s_small1, 16)
            sp.dma_start(lnb_sb[:, :], lnrow[1:2, :].partition_broadcast(P)).then_inc(s_small1, 16)

            def store_xn(s):
                for i in range(NTT):
                    sp.wait_ge(s.xn_ready, i + 1)
                    sp.dma_start(xn_dram[s.n][i * P:(i + 1) * P, :], xn[:, i, :]).then_inc(s.xn_stored, 16)

            def store_tiles(s):
                rows = ys_dram[s.n].rearrange("(t p) d -> t p d", p=P)
                with sp.Fori(0, s.NT // 4) as g:
                    for j in range(4):
                        t = g * 4 + j
                        sp.wait_ge(s.y_ready, t + 1)
                        sp.dma_start(rows[t], ybuf[:, j, :]).then_inc(s.y_stored[j], 16)

            store_xn(L[0])
            sp.wait_ge(L[0].qkv_done, NTT)
            sp.dma_start(wqkv_sb[:, :, :], wqvu1).then_inc(s_wqvu1, 16)
            store_tiles(L[0])
            sp.wait_ge(L[0].y_done, NT0)
            for c in range(4):
                e = slice(c * 8, c * 8 + 8)
                sp.dma_start(gu1_sb.rearrange("p (e n) -> p e n", e=E1)[:, e, :], gu1[:, e, :]).then_inc(s_w1, 16)
                sp.dma_start(dn1_sb.rearrange("p (e n) -> p e n", e=E1)[:, e, :], dn1[:, e, :]).then_inc(s_w1, 16)
            sp.dma_start(wsgu_sb, wsgu).then_inc(s_tab1, 16)
            sp.dma_start(wsdn_sb, wsdn).then_inc(s_tab1, 16)
            sp.dma_start(wo1_sb, wo1).then_inc(s_tab1, 16)
            sp.dma_start(lng_sb, lnrow[0:1, :].partition_broadcast(P)).then_inc(s_tab1, 16)
            sp.dma_start(bo1_sb, bo1.partition_broadcast(P)).then_inc(s_tab1, 16)
            store_xn(L[1])
            store_tiles(L[1])
            for i in range(NTT):
                sp.wait_ge(L[1].g_done, i + 1)
                sp.dma_start(out[i * P:(i + 1) * P, :], xr[:, i, :]).then_inc(s_out, 16)
            sp.wait_ge(s_out, 16 * NTT)

        @block.gpsimd
        def _(po):
            chain = [0]

            def link(ins):
                chain[0] += 1
                ins.then_inc(s_pool, 1)
                po.wait_ge(s_pool, chain[0])

            def here():
                po.sem_inc(s_here, 1)

            def gather_tiles(s):
                ge(po, s.xn_stored, 16 * NTT)
                po.wait_ge(s.idx_ready, 1)

                def one(t, j):
                    if not isinstance(t, int) or t >= 4:
                        po.wait_ge(s.xgT_done, t - 3)
                    po.tensor_copy(idxs[:, j:j + 1], gidx[:, bass.ds(t, 1)]).then_inc(s.icol, 1)
                    po.wait_ge(s.icol, t + 1)
                    here()
                    po.indirect_dma_start(xg[:, j, :], None, xn_dram[s.n],
                                          bass.IndirectOffsetOnAxis(ap=idxs[:, j:j + 1], axis=0))\
                      .then_inc(s.xg_full[j], 16)

                for j in range(4):
                    one(j, j)
                with po.Fori(1, s.NT // 4) as g:
                    for j in range(4):
                        one(g * 4 + j, j)

            def gather_back(s, i, j):
                if not isinstance(i, int) or i >= 2:
                    po.wait_ge(s.cg_read, i - 1)
                po.tensor_copy(idx4[:, j, :], slotu[s.n][:, bass.ds(i * TOPK, TOPK)]).then_inc(s.icol4, 1)
                po.wait_ge(s.icol4, i + 1)
                here()
                for k in range(TOPK):
                    po.indirect_dma_start(cg[:, j, k, :], None, ys_dram[s.n],
                                          bass.IndirectOffsetOnAxis(ap=idx4[:, j, k:k + 1], axis=0))\
                      .then_inc(s.cg_full[j], 16)

            def tiles_stored(s):
                for j in range(4):
                    po.wait_ge(s.y_stored[j], 16 * (s.NT // 4))

            link(po.memset(gub_bf[:, :], 0.0))
            link(po.memset(dnb_bf[:, :], 0.0))
            po.wait_ge(s_bias, 96)
            for full, part, n in ((gub_f, gub_bf, 2 * F0), (dnb_f, dnb_bf, D)):
                for j in range(3):
                    rows = slice(32 * j, 32 * j + E0)
                    for m in range(j):
                        link(po.tensor_copy(bsp[rows, 0:n], full[rows, :]))
                        link(po.tensor_tensor(full[rows, :], full[rows, :], bsp[rows, 0:n], ALU.subtract))
                    link(po.tensor_copy(part[rows, :], full[rows, :]))
            po.engine_nop().then_inc(s_bsp, 1)

            gather_tiles(L[0])
            tiles_stored(L[0])
            po.wait_ge(L[0].qkv_read, 2 * NTT)
            link(po.memset(qst[:, :, :, :], 0.0))
            with po.Fori(0, BATCH) as b:
                po.wait_ge(s_qkT, b + 1)
                here()
                for tt in range(2):
                    ct = cst[:, C_COS + DH * tt:C_COS + DH * tt + DH]
                    st = cst[:, C_SIN + DH * tt:C_SIN + DH * tt + DH]
                    raw = qk_raw[:, bass.ds(b * 2 + tt, 1), :].rearrange("p o (h d) -> p (o h) d", d=DH)
                    half = DH // 2

                    def wide(a, lo, hi):
                        return a[:, lo:hi].unsqueeze(1).broadcast_to([P, 2 * HEADS, hi - lo])

                    po.tensor_tensor(rtmp[:, :, 0:half], raw[:, :, half:DH], wide(st, 0, half), ALU.mult).then_inc(s_rst, 1)
                    po.tensor_tensor(rtmp[:, :, half:DH], raw[:, :, 0:half], wide(st, half, DH), ALU.mult).then_inc(s_rst, 1)
                    po.wait_ge(s_rst, b * 6 + 3 * tt + 2)
                    here()
                    po.tensor_tensor(raw, raw, wide(ct, 0, DH), ALU.mult).then_inc(s_rst, 1)
                    po.wait_ge(s_rst, b * 6 + 3 * tt + 3)
                    here()
                    for a in range(2):
                        po.tensor_tensor(qst[:, tt, a, :].rearrange("p (g a d) -> p g a d", a=2, d=DH)[:, :, a, :],
                                         raw[:, a:HEADS:2, :], rtmp[:, a:HEADS:2, :], ALU.add).then_inc(s_rope, 1)
                    po.tensor_tensor(kst[:, tt, :].rearrange("p (h d) -> p h d", d=DH),
                                     raw[:, HEADS:, :], rtmp[:, HEADS:, :], ALU.add).then_inc(s_rope, 1)
                    po.wait_ge(s_rope, b * 6 + 3 * tt + 3)
                    here()
                po.wait_ge(L[0].cg_read, b * 2 + 1)
                for j in range(2):
                    po.tensor_copy(idx4[:, j, :], slotu[0][:, bass.ds(b * 2 * TOPK + j * TOPK, TOPK)]).then_inc(L[0].icol4, 1)
                    po.wait_ge(L[0].icol4, b * 2 + j + 1)
                    here()
                    for k in range(TOPK):
                        po.indirect_dma_start(cg[:, j, k, :], None, ys_dram[0],
                                              bass.IndirectOffsetOnAxis(ap=idx4[:, j, k:k + 1], axis=0))\
                          .then_inc(L[0].cg_full[j], 16)
            gather_tiles(L[1])
            tiles_stored(L[1])
            for i in range(NTT):
                gather_back(L[1], i, i % 2)

        @block.scalar
        def _(ac):
            ac.wait_ge(s_x, 16)
            for c in range(4):
                e = slice(c * 4, c * 4 + 4)
                ac.dma_start(gu0_sb.rearrange("p (e n) -> p e n", e=E0)[:, e, :], gu0[:, e, :]).then_inc(s_w0, 16)
                ac.dma_start(dn0_sb.rearrange("p (e n) -> p e n", e=E0)[:, e, :], dn0[:, e, :]).then_inc(s_w0, 16)

            def norm_and_turn(s):
                ac.wait_ge(s.ve_ready, 1)
                ac.activation(sd[:, :], sd[:, :], ACT.Sqrt).then_inc(s.sd_ready, 1)
                for i in range(NTT):
                    ac.wait_ge(s.xT_done, i + 1)
                    ac.activation(s.xnT[:, :, i * P:(i + 1) * P],
                                  ps[:, i % 2, 0:D].rearrange("p (k t) -> p k t", k=KD), ACT.Copy)\
                      .then_inc(s.xnT_ready, 1)

            def top_exp(s):
                ac.wait_ge(s.wexp_in, 1)
                ac.activation(wraw[:, :, :], wraw[:, :, :], ACT.Exp).then_inc(s.wexp_out, 1)

            def tiles(s):
                ac.wait_ge(s.idx_ready, 1)

                def turn(t, j):
                    ac.wait_ge(s.xgT_done, t + 1)
                    if not isinstance(t, int) or t >= 2:
                        ac.wait_ge(s.gu_done, t - 1)
                    ac.activation(xgT[:, j % 2, :, :], ps[:, j % 2, 0:D].rearrange("p (k t) -> p k t", k=KD), ACT.Copy)\
                      .then_inc(s.xgT_ready, 1)

                def gate(t, j):
                    if s.n == 0:
                        ac.wait_ge(s.g_ready, t + 1)
                        ac.activation(sig[:, j % 2, 0:s.F], gbuf[:, j % 2, :], ACT.Sigmoid, scale=ALPHA)\
                          .then_inc(s.sig_ready, 1)
                    else:
                        ac.wait_ge(s.gu_done, t + 1)
                        if not isinstance(t, int) or t >= 2:
                            ac.wait_ge(s.h_ready, t - 1)
                        ac.activation(sig[:, j % 2, 0:s.F], ps[:, 2 + j % 2, 0:s.F], ACT.Sigmoid)\
                          .then_inc(s.sig_ready, 1)

                def weigh(t, j):
                    ac.wait_ge(s.y_done, t + 1)
                    if not isinstance(t, int) or t >= 4:
                        ac.wait_ge(s.y_stored[j], (t - j) * 4)
                    ac.activation(ybuf[:, j, :], ps[:, 6 + j % 2, 0:D], ACT.Copy, scale=wtile[:, bass.ds(t, 1)])\
                      .then_inc(s.y_ready, 1)

                run_tiles(ac, s, (turn, gate, None, weigh))

            norm_and_turn(L[0])
            def qkv0(i):
                ac.wait_ge(L[0].qkv_done, i + 1)
                b0 = 4 + 2 * (i % 2)
                ac.activation(qk_raw[:, i, :], ps[:, b0, :], ACT.Copy).then_inc(L[0].qkv_read, 1)
                ac.activation(v_aug[:, i, :, 0:DH], ps[:, b0 + 1, 0:D].rearrange("p (h d) -> p h d", d=DH), ACT.Copy)\
                  .then_inc(L[0].qkv_read, 1)

            qkv0(0)
            top_exp(L[0])
            for i in range(1, NTT):
                qkv0(i)
            tiles(L[0])

            ac.sem_inc(s_s, 1)
            with ac.Fori(0, BATCH) as b:
                ac.wait_ge(s_qkT, b + 2)
                ac.activation(qTs[:, :, :, :], ps[:, 0:2, :].rearrange("p a (g t) -> p a g t", g=2), ACT.Copy).then_inc(s_qkTr, 1)

                def probs(p):
                    ac.wait_ge(s_sub, b * PAIRS + p + 1)
                    ac.activation(pr[:, p % 2, :, :], pr[:, p % 2, :, :], ACT.Exp, scale=float(DH) ** -0.5).then_inc(s_exp, 1)

                def probs_turned(p):
                    ac.wait_ge(s_pT, b * PAIRS + p + 1)
                    ac.activation(prT[:, p % 2, :, :], ps[:, 4:6, 0:384], ACT.Copy).then_inc(s_pTr, 1)

                probs(0)
                for p in range(PAIRS):
                    if p + 1 < PAIRS:
                        probs(p + 1)
                    probs_turned(p)
                ac.wait_ge(s_oT, b + 1)
                ac.activation(kTs[:, :, :], ps[:, 4, :].rearrange("p (g t) -> p g t", g=2), ACT.Copy).then_inc(s_oTr, 1)
                ac.wait_ge(s_wo, b + 1)
                ac.activation(xn[:, bass.ds(b * 2, 2), :], ps[:, 5, :].rearrange("p (t n) -> p t n", t=2), ACT.Copy).then_inc(s_s, 1)

            ac.wait_ge(L[0].f_ready, NTT)
            for i in range(NTT):
                ac.activation(rou[:, i * D:(i + 1) * D], g0r[:, i, :], ACT.Sigmoid).then_inc(L[0].fsig_ready, 1)

            norm_and_turn(L[1])

            def qvu1(i):
                ac.wait_ge(L[1].qkv_done, i + 1)
                b0 = 4 + 2 * (i % 2)
                ac.activation(att[:, 0:6144].rearrange("p (w t n) -> p w t n", w=3, t=NTT)[:, :, i, :],
                              psf[:, b0 * 512:b0 * 512 + 3 * D].rearrange("p (w n) -> p w n", w=3), ACT.Copy)\
                  .then_inc(L[1].qkv_read, 1)

            qvu1(0)
            top_exp(L[1])
            for i in range(1, NTT):
                qvu1(i)
            tiles(L[1])
            ac.wait_ge(s_z, 1)
            ac.activation(rowtmp[:, 0, :, :], v1r, ACT.Sigmoid).then_inc(s_e, 1)
            ac.wait_ge(s_z, 2)
            ac.activation(rowtmp[:, 1, :, :], u1r, ACT.Sigmoid).then_inc(s_e, 1)

            def shared(h, m):
                n = 4 * h + m
                ac.wait_ge(s_shd, n + 1)
                if n >= 2:
                    ac.wait_ge(s_shr, n - 1)
                ac.activation(shs[:, n % 2, :], ps[:, n % 2, :], ACT.Sigmoid).then_inc(s_shsig, 1)

            def shared_rows(h):
                for i in range(4 * h, 4 * h + 4):
                    ac.wait_ge(s_sdn, i + 1)
                    ac.activation(sh1r[:, i, :], ps[:, 4 + i % 2, 0:D], ACT.Copy).then_inc(s_shrow, 1)

            for h in range(2):
                for m in range(4):
                    shared(h, m)
                shared_rows(h)
            ac.wait_ge(s_z, 3)
            ac.activation(rowtmp[:, 0, :, :], q1r, ACT.Exp).then_inc(s_e, 1)
            for b in range(BATCH):
                ac.wait_ge(s_qT1, b + 1)
                ac.activation(q1T[:, :, b * SEQ:(b + 1) * SEQ], ps[:, b % 2, :].rearrange("p (g t) -> p g t", g=2), ACT.Copy)\
                  .then_inc(s_qT1r, 1)
                for i in (2 * b, 2 * b + 1):
                    ac.wait_ge(s_o1, i + 1)
                    ac.activation(a1r[:, i, :], ps[:, 2 + i % 2, 0:D], ACT.Copy).then_inc(s_a1, 1)
            ac.wait_ge(s_ln1, 1)
            ac.activation(sd[:, :], sd[:, :], ACT.Sqrt).then_inc(s_sd1, 1)
            for i in range(NTT):
                ac.wait_ge(s_a1T, i + 1)
                if i >= 2:
                    ac.wait_ge(s_wo1, i - 1)
                ac.activation(a1T[:, i % 2, :, :], ps[:, 4 + i % 2, 0:D].rearrange("p (k t) -> p k t", k=KD), ACT.Copy)\
                  .then_inc(s_a1Tr, 1)
            for i in range(NTT):
                ac.wait_ge(L[1].f_ready, i + 1)
                ac.activation(fsig[:, i % 2, :], fbuf[:, i % 2, :], ACT.Sigmoid).then_inc(L[1].fsig_ready, 1)

        @block.tensor
        def _(pe):
            def turn_and_route(s):
                pe.wait_ge(s_cst, 16)
                pe.wait_ge(s_wr if s.n == 0 else s_small1, 32 if s.n == 0 else 48)
                for i in range(NTT + 1):
                    if i < NTT:
                        pe.wait_ge(s.xn_ready, i + 1)
                        if i >= 2:
                            pe.wait_ge(s.xnT_ready, i - 1)
                        for k in range(KD):
                            mm = pe.transpose(ps[:, i % 2, k * P:(k + 1) * P], xn[:, i, k * P:(k + 1) * P], ident)
                        mm.then_inc(s.xT_done, 1)
                    if i >= 1:
                        pe.wait_ge(s.xnT_ready, i)
                        for k in range(KD):
                            mm = pe.matmul(ps[:, 2, (i - 1) * s.E:i * s.E], s.xnT[:, k, (i - 1) * P:i * P],
                                           s.wr[:, k, :], start=(k == 0), stop=(k == KD - 1))
                mm.then_inc(s.logits_done, 1)

            def project(s, i):
                if i == 0:
                    if s.n == 0:
                        pe.wait_ge(s_wqkv, 32)
                    else:
                        pe.wait_ge(s_wqvu1, 16)
                if i >= 2:
                    pe.wait_ge(s.qkv_read, (i - 1) * (2 if s.n == 0 else 1))
                b0 = 4 + 2 * (i % 2)
                for n0, n1 in ((0, 512), (512, 768)):
                    for k in range(KD):
                        mm = pe.matmul(psf[:, b0 * 512 + n0:b0 * 512 + n1], s.xnT[:, k, i * P:(i + 1) * P],
                                       wqkv_sb[:, k, n0:n1], start=(k == 0), stop=(k == KD - 1))
                mm.then_inc(s.qkv_done, 1)

            def rank(s):
                pe.wait_ge(s.m_ready, 1)
                pe.wait_ge(s_cbf, 4)
                cnt = mcnt[:, 0:NTT * s.E].rearrange("p (t e) -> p t e", e=s.E)
                out3 = ps[:, 3, 0:NTT * s.E].rearrange("p (t e) -> p t e", e=s.E)
                pe.matmul(out3, tri_bf[:, :], cnt, start=True, stop=False)
                for j in range(NTT - 1):
                    n = NTT - 1 - j
                    pe.matmul(out3[:, j + 1:NTT, :], ones_bf[:, :], cnt[:, j, :].unsqueeze(1).broadcast_to([P, n, s.E]),
                              start=False, stop=(j == NTT - 2))
                for j in range(NTT):
                    mm = pe.matmul(ps[:, 3, 256:256 + s.E], ones_bf[:, :], cnt[:, j, :], start=(j == 0), stop=(j == NTT - 1))
                mm.then_inc(s.rank_done, 1)

            def place(s, i):
                pe.wait_ge(s.ab_ready, i + 1)
                for k in range(TOPK):
                    mm = pe.matmul(ps[:, 2, 0:2 * s.NT], amat[:, i % 2, k, :], bmat[:, i % 2, k, 0:2 * s.NT],
                                   start=(i == 0 and k == 0), stop=(i == NTT - 1 and k == TOPK - 1))
                mm.then_inc(s.ab_used, 1)

            def tiles(s):
                pe.wait_ge(s.idx_ready, 1)
                pe.wait_ge(s.qkv_read, NTT * (2 if s.n == 0 else 1))
                if s.n == 0:
                    pe.wait_ge(s_w0, 128)
                    pe.wait_ge(s_bsp, 1)
                else:
                    pe.wait_ge(s_w1, 128)
                    pe.wait_ge(s_tab1, 80)
                gu, dn = ((gu0_sb, dn0_sb), (gu1_sb, dn1_sb))[s.n]

                def turn(t, j):
                    pe.wait_ge(s.xg_full[j], (t + (4 - j)) * 4)
                    if not isinstance(t, int) or t >= 2:
                        pe.wait_ge(s.xgT_ready, t - 1)
                    for k in range(KD):
                        mm = pe.transpose(ps[:, j % 2, k * P:(k + 1) * P], xg[:, j, k * P:(k + 1) * P], ident)
                    mm.then_inc(s.xgT_done, 1)

                def up(t, j):
                    e = pe.value_load(texi[0:1, bass.ds(t, 1)], min_val=0, max_val=s.E - 1)
                    if not isinstance(t, int) or t >= 2:
                        pe.wait_ge(s.h_ready, t - 1)
                    b0, w = 2 + j % 2, 2 * s.F
                    if s.n == 0:
                        pe.matmul(ps[:, b0, 0:w], selc[:, bass.ds(t, 1)].broadcast_to([96, P]), gub_bf[:, :],
                                  start=True, stop=False)
                    pe.wait_ge(s.xgT_ready, t + 1)
                    for k in range(KD):
                        mm = pe.matmul(ps[:, b0, 0:w], xgT[:, j % 2, k, :], gu[:, bass.ds(e * (KD * w) + k * w, w)],
                                       start=(s.n == 1 and k == 0), stop=(k == KD - 1))
                    mm.then_inc(s.gu_done, 1)

                def turn_h(t, j):
                    pe.wait_ge(s.h_ready, t + 1)
                    if not isinstance(t, int) or t >= 2:
                        pe.wait_ge(s.hT_ready, t - 1)
                    for k in range(s.KF):
                        mm = pe.transpose(ps[0:s.FP, 4 + j % 2, k * P:(k + 1) * P], hbuf[:, j % 2, k * s.FP:(k + 1) * s.FP], ident)
                    mm.then_inc(s.hT_done, 1)

                def down(t, j):
                    e = pe.value_load(texi[0:1, bass.ds(t, 1)], min_val=0, max_val=s.E - 1)
                    if not isinstance(t, int) or t >= 2:
                        pe.wait_ge(s.y_ready, t - 1)
                    if s.n == 0:
                        pe.matmul(ps[:, 6 + j % 2, 0:D], selc[:, bass.ds(t, 1)].broadcast_to([96, P]), dnb_bf[:, :],
                                  start=True, stop=False)
                    pe.wait_ge(s.hT_ready, t + 1)
                    for k in range(s.KF):
                        mm = pe.matmul(ps[:, 6 + j % 2, 0:D], hT[0:s.FP, j % 2, k, :],
                                       dn[0:s.FP, bass.ds(e * (s.KF * D) + k * D, D)],
                                       start=(s.n == 1 and k == 0), stop=(k == s.KF - 1))
                    mm.then_inc(s.y_done, 1)

                run_tiles(pe, s, (turn, up, turn_h, down))

            turn_and_route(L[0])
            project(L[0], 0)
            project(L[0], 1)
            rank(L[0])
            for i in range(2, 5):
                project(L[0], i)
            for i in range(NTT):
                place(L[0], i)
                if i in (1, 3, 5):
                    project(L[0], 5 + i // 2)
            tiles(L[0])

            pe.wait_ge(L[0].y_ready, NT0)
            pe.wait_ge(s_vone, 1)
            pe.sem_inc(s_qkT, 1)
            with pe.Fori(0, BATCH) as b:
                pe.wait_ge(s_rope, b * 6 + 6)
                for tt in range(2):
                    for g in range(2):
                        for a in range(2):
                            pe.transpose(ps[:, a, g * SEQ + tt * P:g * SEQ + (tt + 1) * P], qst[:, tt, a, g * P:(g + 1) * P], ident)
                        mm = pe.transpose(ps[:, 2, g * SEQ + tt * P:g * SEQ + (tt + 1) * P], kst[:, tt, g * P:(g + 1) * P], ident)
                mm.then_inc(s_qkT, 1)
                pe.wait_ge(s_qkTr, b * 2 + 2)

                def heads(p):
                    g, a, r = p // 4, p % 2, 2 * (p % 4 // 2)
                    return [(g, a, r + m, 8 * g + 2 * (r + m) + a) for m in range(2)]

                def scores(p):
                    if p >= 2:
                        pe.wait_ge(s_sub, b * PAIRS + p - 1)
                    for m, (g, a, r, h) in enumerate(heads(p)):
                        bank = ps[:, 2 * (p % 2) + m, :]
                        rows = slice(32 * r, 32 * r + 32)
                        pe.matmul(bank[:, 0:P], qTs[rows, a, g, 0:P], kTs[rows, g, 0:P], start=True, stop=False)
                        pe.matmul(bank[:, 0:P], ident_bf[:, :], mask_bf[:, :], start=False, stop=True)
                        pe.matmul(bank[:, P:3 * P], qTs[rows, a, g, P:2 * P], kTs[rows, g, :], start=True, stop=False)
                        mm = pe.matmul(bank[:, 2 * P:3 * P], ident_bf[:, :], mask_bf[:, :], start=False, stop=True)
                    mm.then_inc(s_sc, 1)

                def turn_probs(p):
                    pe.wait_ge(s_exp, b * PAIRS + p + 1)
                    if p == 0:
                        pe.wait_ge(s_s, b + 1)
                    for m in range(2):
                        for n in range(3):
                            mm = pe.transpose(ps[:, 4 + m, n * P:(n + 1) * P], pr[:, p % 2, m, n * P:(n + 1) * P], ident)
                    mm.then_inc(s_pT, 1)

                def attend(p):
                    pe.wait_ge(s_pTr, b * PAIRS + p + 1)
                    for m, (g, a, r, h) in enumerate(heads(p)):
                        o = slice(h * (DH + 1), (h + 1) * (DH + 1))
                        v = [v_aug[:, bass.ds(b * 2 + tt, 1), h, :].rearrange("p o d -> p (o d)") for tt in range(2)]
                        pe.matmul(ps[:, 6, o], prT[:, p % 2, m, 0:P], v[0], start=True, stop=True)
                        pe.matmul(ps[:, 7, o], prT[:, p % 2, m, P:2 * P], v[0], start=True, stop=False)
                        mm = pe.matmul(ps[:, 7, o], prT[:, p % 2, m, 2 * P:3 * P], v[1], start=False, stop=True)
                    if p == PAIRS - 1:
                        mm.then_inc(s_pv, 1)

                scores(0)
                scores(1)
                for p in range(PAIRS):
                    turn_probs(p)
                    if p + 2 < PAIRS:
                        scores(p + 2)
                    attend(p)
                pe.wait_ge(s_on, b + 1)
                for g in range(2):
                    for tt in range(2):
                        mm = pe.transpose(ps[:, 4, g * SEQ + tt * P:g * SEQ + (tt + 1) * P], ost[:, tt, g * P:(g + 1) * P], ident)
                mm.then_inc(s_oT, 1)
                pe.wait_ge(s_oTr, b + 1)
                for tt in range(2):
                    for k in range(KD):
                        mm = pe.matmul(ps[:, 5, tt * D:(tt + 1) * D], kTs[:, k, tt * P:(tt + 1) * P], wo0_sb[:, k, :],
                                       start=(k == 0), stop=(k == KD - 1))
                mm.then_inc(s_wo, 1)

            pe.wait_ge(s_s, BATCH + 1)
            pe.wait_ge(s_sub, BATCH * PAIRS)
            turn_and_route(L[1])
            project(L[1], 0)
            project(L[1], 1)
            rank(L[1])
            for i in range(2, 5):
                project(L[1], i)
            for i in range(NTT):
                place(L[1], i)
                if i in (1, 3, 5):
                    project(L[1], 5 + i // 2)
            tiles(L[1])

            pe.wait_ge(L[1].y_ready, NT1)
            for h in range(2):
                toks = slice(h * 512, (h + 1) * 512)
                for m in range(4):
                    n = 4 * h + m
                    if n >= 2:
                        pe.wait_ge(s_shr, n - 1)
                    for w in range(2):
                        for k in range(KD):
                            mm = pe.matmul(ps[:, n % 2 + 2 * w, :], wsgu_sb[:, k, w * SH + m * P:w * SH + (m + 1) * P],
                                           L[1].xnT[:, k, toks], start=(k == 0), stop=(k == KD - 1))
                    mm.then_inc(s_shd, 1)
                pe.wait_ge(s_shr, 4 * h + 4)
                for i in range(4 * h, 4 * h + 4):
                    if i >= 2:
                        pe.wait_ge(s_shrow, i - 1)
                    for m in range(4):
                        mm = pe.matmul(ps[:, 4 + i % 2, 0:D], shg[:, m, (i % 4) * P:(i % 4 + 1) * P], wsdn_sb[:, m, :],
                                       start=(m == 0), stop=(m == 3))
                    mm.then_inc(s_sdn, 1)

            pe.wait_ge(s_row1, 2)
            for b in range(BATCH):
                for g in range(2):
                    for tt in range(2):
                        i = 2 * b + tt
                        mm = pe.transpose(ps[:, b % 2, g * SEQ + tt * P:g * SEQ + (tt + 1) * P], q1r[:, i, g * P:(g + 1) * P], ident) \
                            if b < 2 or not (g == 0 and tt == 0) else None
                        if mm is None:
                            pe.wait_ge(s_qT1r, b - 1)
                            mm = pe.transpose(ps[:, b % 2, 0:P], q1r[:, i, 0:P], ident)
                mm.then_inc(s_qT1, 1)
                if b >= 2:
                    pe.wait_ge(s_kvr, b - 1)
                for g in range(2):
                    for tt in range(2):
                        i = 2 * b + tt
                        mm = pe.matmul(ps[:, 6 + b % 2, g * P:(g + 1) * P], q1r[:, i, g * P:(g + 1) * P], v1r[:, i, g * P:(g + 1) * P],
                                       start=(tt == 0), stop=(tt == 1))
                mm.then_inc(s_kv, 1)
                pe.wait_ge(s_kvr, b + 1)
                pe.wait_ge(s_qT1r, b + 1)
                for tt in range(2):
                    i = 2 * b + tt
                    if i >= 2:
                        pe.wait_ge(s_a1, i - 1)
                        pe.wait_ge(s_bn1, i - 1)
                    for g in range(2):
                        mm = pe.matmul(ps[:, 2 + i % 2, g * P:(g + 1) * P], q1T[:, g, i * P:(i + 1) * P], kvb[:, b % 2, g, :],
                                       start=True, stop=True)
                    mm.then_inc(s_o1, 1)
            pe.wait_ge(s_shrow, NTT)
            for i in range(NTT + 1):
                if i < NTT:
                    pe.wait_ge(s_a1n, i + 1)
                    if i >= 2:
                        pe.wait_ge(s_a1Tr, i - 1)
                    for k in range(KD):
                        mm = pe.transpose(ps[:, 4 + i % 2, k * P:(k + 1) * P], a1r[:, i, k * P:(k + 1) * P], ident)
                    mm.then_inc(s_a1T, 1)
                if i >= 1:
                    pe.wait_ge(s_a1Tr, i)
                    if i >= 3:
                        pe.wait_ge(s_s1, i - 2)
                    for k in range(KD):
                        mm = pe.matmul(ps[:, 6 + (i - 1) % 2, 0:D], a1T[:, (i - 1) % 2, k, :], wo1_sb[:, k, :],
                                       start=(k == 0), stop=(k == KD - 1))
                    mm.then_inc(s_wo1, 1)

        @block.vector
        def _(ve):
            chain = [0]

            def link(ins):
                chain[0] += 1
                ins.then_inc(s_dve, 1)
                ve.wait_ge(s_dve, chain[0])

            def normalise(s):
                for i in range(NTT):
                    if s.n == 0 or i == 0:
                        pass
                    ins = ve.bn_stats(bnst[:, i, :], xr[:, i, :])
                link(ins)
                for i in range(NTT):
                    ins = ve.bn_aggr(mv[:, i, :], bnst[:, i, :])
                link(ins)
                ve.tensor_scalar(sd[:, :], mv[:, :, 1], EPS, None, ALU.add).then_inc(s.ve_ready, 1)
                ve.wait_ge(s.sd_ready, 1)
                link(ve.reciprocal(rstd[:, :], sd[:, :]))
                for i in range(NTT):
                    ve.tensor_scalar(xn[:, i, :], xr[:, i, :], mv[:, i, 0:1], rstd[:, i:i + 1], ALU.subtract, ALU.mult)\
                      .then_inc(s.xn_ready, 1)

            def route(s):
                E, NT = s.E, s.NT
                lg = lgt[:, 0:NTT * E].rearrange("p (t e) -> p t e", e=E)
                ohv = oh[:, 0:NTT * TOPK * E].rearrange("p (t k e) -> p t k e", t=NTT, e=E) if NTT * TOPK * E <= 1024 else None
                s4 = sl4[:, 0:NTT * TOPK * E].rearrange("p (t k e) -> p t k e", t=NTT, e=E)
                ve.wait_ge(s.logits_done, 1)
                out_l = ps[:, 2, 0:NTT * E].rearrange("p (t e) -> p t e", e=E)
                if s.n == 0:
                    link(ve.tensor_tensor(lg, out_l, rb0_sb[:, :].unsqueeze(1).broadcast_to([P, NTT, E]), ALU.add))
                else:
                    link(ve.tensor_copy(lg, out_l))
                for i in range(NTT):
                    ins = ve.max(top[:, i, :], lg[:, i, :])
                link(ins)
                ve.tensor_tensor(wraw[:, :, :], top[:, :, 0:TOPK], top[:, :, 0:1].broadcast_to([P, NTT, TOPK]), ALU.subtract)\
                  .then_inc(s.wexp_in, 1)
                for i in range(NTT):
                    ins = ve.max_index(topi[:, i, :], top[:, i, :], lg[:, i, :])
                link(ins)
                link(ve.tensor_copy(topf[:, :, :], topi[:, :, 0:TOPK]))
                oh2 = oh[:, 0:NTT * TOPK * E].rearrange("p (n e) -> p n e", e=E)
                link(ve.tensor_tensor(oh2, iota[:, 0:E].unsqueeze(1).broadcast_to([P, NTT * TOPK, E]),
                                      topf[:, :, :].rearrange("p t k -> p (t k)").unsqueeze(2).broadcast_to([P, NTT * TOPK, E]),
                                      ALU.is_equal))
                with nc.allow_low_precision("zeros and ones: a token's four experts differ"):
                    ve.tensor_reduce(mcnt[:, 0:NTT * E].rearrange("p (t e) -> p t e", e=E), ohv.rearrange("p t k e -> p t e k"),
                                     AX.X, ALU.add).then_inc(s.m_ready, 1)
                ve.wait_ge(s.wexp_out, 1)
                link(ve.tensor_reduce(wsum[:, :], wraw[:, :, :], AX.X, ALU.add))
                link(ve.reciprocal(wsum[:, :], wsum[:, :]))
                link(ve.tensor_tensor(wtop[:, :, :], wraw[:, :, :], wsum[:, :].unsqueeze(2).broadcast_to([P, NTT, TOPK]), ALU.mult))
                ve.wait_ge(s.rank_done, 1)
                link(ve.tensor_scalar(nti[:, 0:E], ps[:, 3, 256:256 + E], float(P - 1), None, ALU.add))
                link(ve.tensor_scalar(nti[:, 0:E], nti[:, 0:E], 7, 7, ALU.arith_shift_right, ALU.logical_shift_left))
                link(ve.tensor_copy(nts[:, 0:E], nti[:, 0:E]))
                link(ve.tensor_tensor_scan(enda[:, 0:E], ones_e[:, 0:E], nts[:, 0:E], 0.0, ALU.mult, ALU.add))
                link(ve.tensor_tensor(base[:, 0:E], enda[:, 0:E], nts[:, 0:E], ALU.subtract))
                link(ve.tensor_tensor(lg, ps[:, 3, 0:NTT * E].rearrange("p (t e) -> p t e", e=E),
                                      base[:, 0:E].unsqueeze(1).broadcast_to([P, NTT, E]), ALU.add))
                link(ve.tensor_tensor(s4, ohv, lg.unsqueeze(2).broadcast_to([P, NTT, TOPK, E]), ALU.mult))
                link(ve.tensor_reduce(slotf[:, :], s4.rearrange("p t k e -> p (t k) e"), AX.X, ALU.add))
                ve.tensor_copy(slotu[s.n][:, :], slotf[:, :])
                link(ve.tensor_copy(sloti[:, :], slotf[:, :]))
                ve.tensor_scalar(tq[:, :], sloti[:, :], 7, None, ALU.arith_shift_right)
                link(ve.tensor_scalar(sloti[:, :], sloti[:, :], P - 1, None, ALU.bitwise_and))
                ve.tensor_copy(tqf[:, :], tq[:, :])
                link(ve.tensor_copy(smf[:, :], sloti[:, :]))
                for i in range(NTT):
                    if i >= 2:
                        ve.wait_ge(s.ab_used, i - 1)
                    pick = slice(i * TOPK, (i + 1) * TOPK)
                    ve.tensor_tensor(amat[:, i % 2, :, :], iota.unsqueeze(1).broadcast_to([P, TOPK, P]),
                                     smf[:, pick].unsqueeze(2).broadcast_to([P, TOPK, P]), ALU.is_equal)
                    bm = bmat[:, i % 2, :, :]
                    link(ve.tensor_tensor(bm[:, :, 0:NT], iota[:, 0:NT].unsqueeze(1).broadcast_to([P, TOPK, NT]),
                                          tqf[:, pick].unsqueeze(2).broadcast_to([P, TOPK, NT]), ALU.is_equal))
                    link(ve.tensor_tensor(bm[:, :, NT:2 * NT], bm[:, :, 0:NT], wtop[:, i, :].unsqueeze(2).broadcast_to([P, TOPK, NT]), ALU.mult))
                    ve.tensor_scalar(bm[:, :, 0:NT], bm[:, :, 0:NT], tokid[:, i:i + 1], None, ALU.mult).then_inc(s.ab_ready, 1)
                half = NT // 2
                for q in range(2):
                    sl = sl4[:, 0:half * E].rearrange("p (t e) -> p t e", e=E)
                    link(ve.scalar_tensor_tensor(out=sl, in0=iota[:, q * half:(q + 1) * half].unsqueeze(2).broadcast_to([P, half, E]),
                                                 scalar=float(P), in1=enda[:, 0:E].unsqueeze(1).broadcast_to([P, half, E]),
                                                 op0=ALU.mult, op1=ALU.is_ge))
                    link(ve.tensor_reduce(texf[:, q * half:(q + 1) * half], sl, AX.X, ALU.add))
                link(ve.tensor_scalar(texf[:, 0:NT], texf[:, 0:NT], float(E - 1), None, ALU.min))
                link(ve.tensor_copy(texi[:, 0:NT], texf[:, 0:NT]))
                if s.n == 0:
                    link(ve.tensor_scalar(selc[:, :], texf[0:96, 0:NT], pmod[0:96, :], None, ALU.is_equal))
                ve.wait_ge(s.ab_used, NTT)
                link(ve.tensor_copy(gidx[:, 0:NT], ps[:, 2, 0:NT]))
                ve.tensor_copy(wtile[:, 0:NT], ps[:, 2, NT:2 * NT]).then_inc(s.idx_ready, 1)

            def tiles(s):
                F = s.F

                def gate(t, j):
                    ve.wait_ge(s.gu_done, t + 1)
                    g, u = ps[:, 2 + j % 2, 0:F], ps[:, 2 + j % 2, F:2 * F]
                    if s.n == 0:
                        ve.tensor_scalar(gbuf[:, j % 2, :], g, LIMIT, None, ALU.min).then_inc(s.g_ready, 1)
                        ve.tensor_scalar(ubuf[:, j % 2, :], u, LIMIT, -LIMIT, ALU.min, ALU.max).then_inc(s.u_ready, 1)
                        ve.wait_ge(s.u_ready, t + 1)
                        ve.scalar_tensor_tensor(out=ubuf[:, j % 2, :], in0=ubuf[:, j % 2, :], scalar=1.0, in1=gbuf[:, j % 2, :],
                                                op0=ALU.add, op1=ALU.mult).then_inc(s.h1_ready, 1)
                        ve.wait_ge(s.h1_ready, t + 1)
                        ve.wait_ge(s.sig_ready, t + 1)
                    else:
                        ve.wait_ge(s.sig_ready, t + 1)
                        ve.tensor_tensor(gbuf[:, j % 2, 0:F], sig[:, j % 2, 0:F], g, ALU.mult).then_inc(s.h1_ready, 1)
                        ve.wait_ge(s.h1_ready, t + 1)
                    if not isinstance(t, int) or t >= 2:
                        ve.wait_ge(s.hT_done, t - 1)
                    if s.n == 0:
                        ve.tensor_tensor(hbuf[:, j % 2, :], ubuf[:, j % 2, :], sig[:, j % 2, :], ALU.mult).then_inc(s.h_ready, 1)
                    else:
                        ve.tensor_tensor(hbuf[:, j % 2, 0:F], gbuf[:, j % 2, 0:F], u, ALU.mult).then_inc(s.h_ready, 1)

                def turned(t, j):
                    ve.wait_ge(s.hT_done, t + 1)
                    if not isinstance(t, int) or t >= 2:
                        ve.wait_ge(s.y_done, t - 1)
                    ve.tensor_copy(hT[0:s.FP, j % 2, 0:s.KF, :],
                                   ps[0:s.FP, 4 + j % 2, 0:s.KF * P].rearrange("p (k t) -> p k t", t=P)).then_inc(s.hT_ready, 1)

                run_tiles(ve, s, (None, gate, turned, None))

            ve.memset(ones_bf[:, :], 1.0).then_inc(s_cbf, 1)
            ve.memset(v_aug[:, :, :, DH:DH + 1], 1.0).then_inc(s_vone, 1)
            link(ve.memset(ones_e[:, :], 1.0))
            ve.wait_ge(s_cst, 16)
            for dst, c in ((ident_bf, C_ID), (mask_bf, C_MASK), (tri_bf, C_TRI)):
                ve.tensor_copy(dst[:, :], cst[:, c:c + P]).then_inc(s_cbf, 1)
            ve.wait_ge(s_x, 16)
            ve.wait_ge(s_wr, 32)
            normalise(L[0])
            route(L[0])
            tiles(L[0])

            ve.sem_inc(L[0].cg_read, 1)
            with ve.Fori(0, BATCH) as b:
                ve.wait_ge(s_qkT, b + 2)
                ve.tensor_copy(kTs[:, :, :], ps[:, 2, :].rearrange("p (g t) -> p g t", g=2)).then_inc(s_qkTr, 1)
                for p in range(PAIRS):
                    pi = b * PAIRS + p
                    s2 = p % 2
                    two = ps[:, 2 * s2:2 * s2 + 2, :]
                    ve.wait_ge(s_sc, pi + 1)
                    ve.tensor_reduce(mxs[:, s2, 0:2], two[:, :, 0:P], AX.X, ALU.max).then_inc(s_mx, 1)
                    ve.tensor_reduce(mxs[:, s2, 2:4], two[:, :, P:3 * P], AX.X, ALU.max).then_inc(s_mx, 1)
                    ve.wait_ge(s_mx, pi * 2 + 2)
                    ve.tensor_tensor(pr[:, s2, :, 0:P], two[:, :, 0:P],
                                     mxs[:, s2, 0:2].unsqueeze(2).broadcast_to([P, 2, P]), ALU.subtract)
                    ve.tensor_tensor(pr[:, s2, :, P:3 * P], two[:, :, P:3 * P],
                                     mxs[:, s2, 2:4].unsqueeze(2).broadcast_to([P, 2, 2 * P]), ALU.subtract).then_inc(s_sub, 1)
                ve.wait_ge(s_pv, b + 1)
                o = ps[:, 6:8, 0:HEADS * (DH + 1)].rearrange("p t (h d) -> p t h d", h=HEADS)
                ve.reciprocal(rec[:, :, :], o[:, :, :, DH]).then_inc(s_rec, 1)
                ve.wait_ge(s_rec, b + 1)
                ve.tensor_tensor(ost[:, :, :].rearrange("p t (h d) -> p t h d", h=HEADS), o[:, :, :, 0:DH],
                                 rec[:, :, :].unsqueeze(3).broadcast_to([P, 2, HEADS, DH]), ALU.mult).then_inc(s_on, 1)
                for j in range(2):
                    ve.wait_ge(L[0].cg_full[j], b * 64 + 64)
                    if j == 1:
                        ve.wait_ge(L[0].f_ready, b * 2 + 1)
                    ve.tensor_tensor(csum.rearrange("p (k n) -> p k n", k=2), cg[:, j, 0:2, :], cg[:, j, 2:4, :], ALU.add)\
                      .then_inc(L[0].cg_read, 1)
                    ve.wait_ge(L[0].cg_read, b * 2 + j + 2)
                    ve.tensor_tensor(g0r[:, bass.ds(b * 2 + j, 1), :].rearrange("p o n -> p (o n)"), csum[:, 0:D], csum[:, D:2 * D], ALU.add)\
                      .then_inc(L[0].f_ready, 1)
                ve.wait_ge(L[0].f_ready, b * 2 + 2)

            ve.wait_ge(s_s, BATCH + 1)
            for i in range(NTT):
                ve.wait_ge(L[0].fsig_ready, i + 1)
                link(ve.tensor_tensor(g0r[:, i, :], g0r[:, i, :], rou[:, i * D:(i + 1) * D], ALU.mult))
                link(ve.tensor_tensor(g0r[:, i, :], g0r[:, i, :], xn[:, i, :], ALU.mult))
                link(ve.tensor_tensor(xr[:, i, :], xr[:, i, :], g0r[:, i, :], ALU.add))
            normalise(L[1])
            route(L[1])
            tiles(L[1])

            def table(lo):
                return b768_sb[:, lo:lo + D].unsqueeze(1).broadcast_to([P, NTT, D])

            ve.wait_ge(L[1].qkv_read, NTT)
            ve.wait_ge(s_small1, 48)
            ve.tensor_tensor(v1r, v1r, table(D), ALU.add).then_inc(s_z, 1)
            ve.tensor_tensor(u1r, u1r, table(2 * D), ALU.add).then_inc(s_z, 1)
            ve.tensor_tensor(q1r, q1r, table(0), ALU.add).then_inc(s_z, 1)
            ve.wait_ge(s_z, 3)
            ve.wait_ge(s_e, 1)
            ve.tensor_tensor(v1r, v1r, rowtmp[:, 0, :, :], ALU.mult).then_inc(s_row1, 1)
            ve.wait_ge(s_e, 2)
            link(ve.tensor_tensor(u1r, u1r, rowtmp[:, 1, :, :], ALU.mult))

            def shared(h, m):
                n = 4 * h + m
                ve.wait_ge(s_shsig, n + 1)
                if h == 1 and m == 0:
                    ve.wait_ge(s_sdn, 4)
                link(ve.tensor_tensor(shs[:, n % 2, :], shs[:, n % 2, :], ps[:, n % 2, :], ALU.mult))
                ve.tensor_tensor(shg[:, m, :], shs[:, n % 2, :], ps[:, 2 + n % 2, :], ALU.mult).then_inc(s_shr, 1)

            for h in range(2):
                for m in range(4):
                    shared(h, m)
            ve.wait_ge(s_e, 3)
            link(ve.tensor_scalar(rowtmp[:, 0, :, :], rowtmp[:, 0, :, :], 1.0, -1.0, ALU.min, ALU.add))
            ve.scalar_tensor_tensor(out=q1r, in0=q1r, scalar=0.0, in1=rowtmp[:, 0, :, :], op0=ALU.max, op1=ALU.add)\
              .then_inc(s_row1, 1)

            def stats(i):
                ve.wait_ge(s_o1, i + 1)
                ve.wait_ge(s_a1, i + 1)
                ve.bn_stats(bnst[:, i, :], ps[:, 2 + i % 2, 0:D]).then_inc(s_bn1, 1)

            for b in range(BATCH):
                ve.wait_ge(s_kv, b + 1)
                if b >= 2:
                    ve.wait_ge(s_o1, 2 * b - 2)
                ve.tensor_tensor(kvb[:, b % 2, :, :], ps[:, 6 + b % 2, 0:D].rearrange("p (g n) -> p g n", g=2),
                                 bdiag.unsqueeze(1).broadcast_to([P, 2, P]), ALU.mult).then_inc(s_kvr, 1)
                stats(2 * b)
                stats(2 * b + 1)
            ve.wait_ge(s_bn1, NTT)
            for i in range(NTT):
                ins = ve.bn_aggr(mv[:, i, :], bnst[:, i, :])
            link(ins)
            ve.tensor_scalar(sd[:, :], mv[:, :, 1], EPS, None, ALU.add).then_inc(s_ln1, 1)
            ve.wait_ge(s_sd1, 1)
            link(ve.reciprocal(rstd[:, :], sd[:, :]))
            for i in range(NTT):
                link(ve.tensor_scalar(a1r[:, i, :], a1r[:, i, :], mv[:, i, 0:1], rstd[:, i:i + 1], ALU.subtract, ALU.mult))
                link(ve.tensor_tensor(a1r[:, i, :], a1r[:, i, :], lng_sb, ALU.mult))
                link(ve.tensor_tensor(a1r[:, i, :], a1r[:, i, :], lnb_sb[:, :], ALU.add))
                ve.tensor_tensor(a1r[:, i, :], a1r[:, i, :], u1r[:, i, :], ALU.mult).then_inc(s_a1n, 1)
                if i >= 2:
                    ve.wait_ge(s_wo1, i - 1)
                    ve.tensor_tensor(s1r[:, i - 2, :], ps[:, 6 + i % 2, 0:D], bo1_sb, ALU.add).then_inc(s_s1, 1)
            for i in (NTT - 2, NTT - 1):
                ve.wait_ge(s_wo1, i + 1)
                ve.tensor_tensor(s1r[:, i, :], ps[:, 6 + i % 2, 0:D], bo1_sb, ALU.add).then_inc(s_s1, 1)
            ve.wait_ge(s_s1, NTT)
            ve.wait_ge(s_shrow, NTT)
            for i in range(NTT):
                j = i % 2
                ve.wait_ge(L[1].cg_full[j], 64 * (i // 2 + 1))
                ve.tensor_tensor(csum.rearrange("p (k n) -> p k n", k=2), cg[:, j, 0:2, :], cg[:, j, 2:4, :], ALU.add)\
                  .then_inc(L[1].cg_read, 1)
                ve.wait_ge(L[1].cg_read, i + 1)
                link(ve.tensor_tensor(fbuf[:, j, :], csum[:, 0:D], csum[:, D:2 * D], ALU.add))
                link(ve.tensor_tensor(fbuf[:, j, :], fbuf[:, j, :], sh1r[:, i, :], ALU.add, ))
                ve.engine_nop().then_inc(L[1].f_ready, 1)
                link(ve.tensor_tensor(s1r[:, i, :], s1r[:, i, :], fbuf[:, j, :], ALU.mult))
                ve.wait_ge(L[1].fsig_ready, i + 1)
                link(ve.tensor_tensor(s1r[:, i, :], s1r[:, i, :], fsig[:, j, :], ALU.mult))
                ve.tensor_tensor(xr[:, i, :], xr[:, i, :], s1r[:, i, :], ALU.add).then_inc(L[1].g_done, 1)


def kernel(**inputs):
    import numpy as np
    import concourse.bacc as bacc
    from concourse.bass_utils import run_bass_kernel_spmd

    a = {k: np.asarray(v) for k, v in inputs.items()}

    def rows(w):
        return np.ascontiguousarray(w.reshape(-1, P, w.shape[-1]).transpose(1, 0, 2))

    def experts(w):
        e, h, n = w.shape
        p = min(h, P)
        return np.ascontiguousarray(w.reshape(e, h // p, p, n).transpose(2, 0, 1, 3).reshape(p, e, -1))

    def apart(w):
        return np.concatenate([w[..., ::2], w[..., 1::2]], axis=-1)

    arrays = dict(
        x=a["L0_attn_x"].reshape(TOK, D),
        consts=constants(),
        wqkv0=rows(np.concatenate([a["L0_attn_Wq"].T, a["L0_attn_Wk"].T, a["L0_attn_Wv"].T], axis=1)),
        wo0=rows(a["L0_attn_Wo"].T),
        wr0=rows(a["L0_ffn_router_weight"].T),
        rb0=a["L0_ffn_router_bias"].reshape(1, E0),
        gub0=apart(a["L0_ffn_gate_up_proj_bias"]),
        dnb0=a["L0_ffn_down_proj_bias"],
        gu0=experts(apart(a["L0_ffn_gate_up_proj"])),
        dn0=experts(a["L0_ffn_down_proj"]),
        wqvu1=rows(np.concatenate([a["L1_attn_Wqk"], a["L1_attn_Wv"], a["L1_attn_Wu"]], axis=1)),
        b768=np.concatenate([a["L1_attn_bqk"], a["L1_attn_bv"], a["L1_attn_bu"]]).reshape(1, 3 * D),
        wo1=rows(a["L1_attn_Wo"]),
        lnrow=np.stack([a["L1_attn_ln_g"], a["L1_attn_ln_b"]]),
        bo1=a["L1_attn_bo"].reshape(1, D),
        wr1=rows(a["L1_ffn_router_w"]),
        gu1=experts(np.concatenate([a["L1_ffn_w_gate"], a["L1_ffn_w_up"]], axis=-1)),
        dn1=experts(a["L1_ffn_w_down"]),
        wsgu=rows(np.concatenate([a["L1_ffn_ws_gate"], a["L1_ffn_ws_up"]], axis=1)),
        wsdn=rows(a["L1_ffn_ws_down"]),
    )
    arrays = {k: np.ascontiguousarray(v) for k, v in arrays.items()}
    nc = bacc.Bacc("TRN2", target_bir_lowering=False, num_devices=1)
    args = [nc.dram_tensor("in_" + k, v.shape, mybir.dt.from_np(v.dtype), kind="ExternalInput").ap() for k, v in arrays.items()]
    args.append(nc.dram_tensor("out", (TOK, D), mybir.dt.float32, kind="ExternalOutput").ap())
    build_program(nc, *args)
    r = run_bass_kernel_spmd(nc, [{"in_" + k: v for k, v in arrays.items()}], core_ids=[0])
    return r.results[0]["out"].reshape(BATCH, SEQ, D)
```

```python
import concourse.bass as bass
from concourse import mybir
from contextlib import ExitStack

P = 128
D = 256
KD = D // P
TOK = 1024
NTT = TOK // P
TOPK = 4
HEADS, DH = 16, 16
BATCH, SEQ = 4, 256
HALF = 8
MASKED = 1.0e30

E0, F0 = 16, 256
E1, F1 = 32, 96
SH = 512
LIMIT, ALPHA = 7.0, 1.702
EPS = 1e-5


def tiles_needed(experts):
    n = TOK * TOPK // P + experts - 1
    return -(-n // 4) * 4


NT0, NT1 = tiles_needed(E0), tiles_needed(E1)

C_ID, C_IOTA, C_TOK, C_MASK, C_TRI, C_BD, C_COS, C_SIN, C_PMOD, C_END = (
    0, 128, 256, 264, 392, 520, 648, 712, 776, 777)


def constants():
    import numpy as np
    c = np.zeros((P, C_END), np.float32)
    p, f = np.arange(P)[:, None], np.arange(P)[None, :]
    c[:, C_ID:C_ID + P] = p == f
    c[:, C_IOTA:C_IOTA + P] = f
    c[:, C_TOK:C_TOK + NTT] = p + P * np.arange(NTT)[None, :]
    c[:, C_MASK:C_MASK + P] = np.where(f > p, MASKED, 0.0)
    c[:, C_TRI:C_TRI + P] = p < f
    c[:, C_BD:C_BD + P] = p // DH == f // DH
    half = DH // 2
    freq = (np.float32(1.0) / np.float32(10000.0) ** (np.arange(half, dtype=np.float32) / np.float32(half))).astype(np.float32)
    for t in range(SEQ // P):
        ang = ((p + t * P).astype(np.float32) * freq[None, :]).astype(np.float32)
        co, si = np.cos(ang), np.sin(ang)
        for w, scale in ((0, -np.float32(DH) ** -0.5), (1, 1.0)):
            at = 2 * DH * t + DH * w
            c[:, C_COS + at:C_COS + at + DH] = np.concatenate([co, co], axis=1) * np.float32(scale)
            c[:, C_SIN + at:C_SIN + at + DH] = np.concatenate([-si, si], axis=1) * np.float32(scale)
    c[:, C_PMOD:C_PMOD + 1] = p % 32
    return c


def build_program(nc, x, consts, wqkv0, wo0, wr0, rb0, gub0, dnb0, gu0, dn0,
                  wqvu1, b768, wo1, lnrow, bo1, wr1, gu1, dn1, wsgu, wsdn, out):
    f32, f32r, bf16, i32, u32 = mybir.dt.float32, mybir.dt.float32r, mybir.dt.bfloat16, mybir.dt.int32, mybir.dt.uint32
    ALU, ACT, AX = mybir.AluOpType, mybir.ActivationFunctionType, mybir.AxisListType
    ctx = ExitStack()
    with ctx:
        def sb(name, shape, dt=f32):
            return ctx.enter_context(nc.sbuf_tensor(name, shape, dt))

        def sem(name):
            return ctx.enter_context(nc.semaphore(name))

        xn_dram = [nc.dram_tensor(f"xn_rows{n}", (TOK, D), f32, kind="Internal").ap() for n in (0, 1)]
        ys_dram = [nc.dram_tensor(f"sorted_rows{n}", (nt * P, D), f32, kind="Internal").ap()
                   for n, nt in ((0, NT0), (1, NT1))]

        cst = sb("cst", [P, C_END])
        ident = cst[:, C_ID:C_ID + P]
        iota = cst[:, C_IOTA:C_IOTA + P]
        tokid = cst[:, C_TOK:C_TOK + NTT]
        bdiag = cst[:, C_BD:C_BD + P]
        pmod = cst[:, C_PMOD:C_PMOD + 1]
        ident_bf = sb("ident_bf", [P, P], bf16)
        mask_bf = sb("mask_bf", [P, P], bf16)
        tri_bf = sb("tri_bf", [P, P], bf16)
        ones_bf = sb("ones_bf", [P, P], bf16)
        ones_e = sb("ones_e", [P, E1])

        big = sb("experts", [P, E0 * KD * 2 * F0 + E0 * KD * D])
        GU0 = E0 * KD * 2 * F0
        GU1 = E1 * KD * 2 * F1
        gu0_sb, dn0_sb = big[:, 0:GU0], big[:, GU0:]
        gu1_sb, dn1_sb = big[:, 0:GU1], big[0:F1, GU0:]
        wsgu_sb = big[:, GU1:GU1 + KD * 2 * SH].rearrange("p (k n) -> p k n", k=KD)
        off = GU1 + KD * 2 * SH
        wsdn_sb = big[:, off:off + 4 * D].rearrange("p (k n) -> p k n", k=4)
        off += 4 * D
        wo1_sb = big[:, off:off + KD * D].rearrange("p (k n) -> p k n", k=KD)
        off += KD * D
        lng_sb, bo1_sb = big[:, off:off + D], big[:, off + D:off + 2 * D]
        assert off + 2 * D <= GU0
        wqkv_sb = sb("wqkv", [P, KD, 3 * D])
        wo0_sb = sb("wo0", [P, KD, D])
        b768_sb = sb("b768", [P, 3 * D])
        lnb_sb = sb("lnb", [P, D])
        wr0_sb = sb("wr0", [P, KD, E0])
        wr1_sb = sb("wr1", [P, KD, E1])
        rb0_sb = sb("rb0", [P, E0])
        gub_bf = sb("gub_bf", [96, 2 * F0], bf16)
        dnb_bf = sb("dnb_bf", [96, D], bf16)

        xr = sb("xr", [P, NTT, D])
        xn = sb("xn", [P, NTT, D])

        att = sb("att", [P, 8192])
        til = sb("til", [P, 5120])
        qk_raw = att[:, 0:4096].rearrange("p (t n) -> p t n", t=NTT)
        v_rows = att[:, 4096:6144].rearrange("p (t n) -> p t n", t=NTT)
        xnT0 = att[:, 6144:8192].rearrange("p (k t) -> p k t", k=KD)
        parts = [a.rearrange("p (t w h n) -> p t w h n", t=2, w=2, h=HALF) for a in (att[:, 6144:8192], til[:, 0:2048])]
        ost = xn[:, 6:7, :].rearrange("p o (t n) -> p (o t) n", t=2)
        q1r, v1r, u1r = (att[:, 2048 * n:2048 * (n + 1)].rearrange("p (t n) -> p t n", t=NTT)
                         for n in range(3))
        kvb = til[:, 4608:5120].rearrange("p (s g n) -> p s g n", s=2, g=2)
        xnT1 = att[:, 6144:8192].rearrange("p (k t) -> p k t", k=KD)
        q1T = xn[:, :, :].rearrange("p t n -> p (t n)").rearrange("p (g t) -> p g t", g=2)

        xg = til[:, 0:1024].rearrange("p (s n) -> p s n", s=4)
        xgT = til[:, 1024:1536].rearrange("p (s k t) -> p s k t", s=2, k=KD)
        gbuf = til[:, 1536:2048].rearrange("p (s n) -> p s n", s=2)
        ubuf = til[:, 2048:2560].rearrange("p (s n) -> p s n", s=2)
        sig = til[:, 2560:3072].rearrange("p (s n) -> p s n", s=2)
        hbuf = til[:, 3072:3584].rearrange("p (s n) -> p s n", s=2)
        hT = til[:, 3584:4096].rearrange("p (s k t) -> p s k t", s=2, k=KD)
        ybuf = til[:, 4096:5120].rearrange("p (s n) -> p s n", s=4)
        pr = til[:, 2048:2816].rearrange("p (s n) -> p s n", s=2)
        prT = til[:, 2816:3584].rearrange("p (s n) -> p s n", s=2)
        otb = til[:, 3584:4096]
        oTs = xn[:, 4:6, :]
        fsum = til[:, 4608:5120].rearrange("p (t n) -> p t n", t=2)
        ftanh = xn[:, 0:2, :]
        fsil = xn[:, 2:4, :]
        shg = til[:, 0:2048].rearrange("p (m t) -> p m t", m=4)
        shs = til[:, 2048:3072].rearrange("p (s t) -> p s t", s=2)
        a1T = til[:, 3072:3584].rearrange("p (s k t) -> p s k t", s=2, k=KD)
        fbuf = til[:, 3584:4096].rearrange("p (s n) -> p s n", s=2)
        fsig = til[:, 4096:4608].rearrange("p (s n) -> p s n", s=2)

        rou = sb("rou", [P, 3584])
        oh = rou[:, 0:512].bitcast(bf16)
        sl4 = rou[:, 512:1536]
        amat = rou[:, 1536:2560].rearrange("p (s k n) -> p s k n", s=2, k=TOPK)
        bmat = rou[:, 2560:3584].rearrange("p (s k n) -> p s k n", s=2, k=TOPK)
        cg = rou[:, 0:2048].rearrange("p (s k n) -> p s k n", s=2, k=TOPK)
        csum0 = til[:, 4096:4608]
        csum = rou[:, 2048:2560]
        vst = rou[:, 2048:3072].rearrange("p (s t h d) -> p s t h d", s=2, t=2, h=HALF)
        cf = rou[:, 2560:3072].rearrange("p (s n) -> p s n", s=2)
        rtmp = rou[:, 3072:3584].rearrange("p (w h d) -> p w h d", w=2, d=DH)
        gub_f, dnb_f, bsp = til[0:96, 0:512], til[0:96, 512:768], til[0:96, 768:1024].bitcast(bf16)
        sh1r = big[:, 0:2048].rearrange("p (t n) -> p t n", t=NTT)
        a1r = big[:, 2048:4096].rearrange("p (t n) -> p t n", t=NTT)
        s1r = big[:, 4096:6144].rearrange("p (t n) -> p t n", t=NTT)
        rowtmp = big[:, 6144:10240].rearrange("p (w t n) -> p w t n", w=2, t=NTT)

        bnst = sb("bnst", [P, NTT, 6])
        mv = sb("mv", [P, NTT, 2])
        sd = sb("sd", [P, NTT])
        rstd = sb("rstd", [P, NTT])
        lgt = sb("lgt", [P, NTT * E1])
        top = sb("top", [P, NTT, 8])
        topi = sb("topi", [P, NTT, 8], u32)
        topf = sb("topf", [P, NTT, TOPK])
        wraw = sb("wraw", [P, NTT, TOPK])
        wsum = sb("wsum", [P, NTT])
        wtop = sb("wtop", [P, NTT, TOPK])
        mcnt = sb("mcnt", [P, NTT * E1], bf16)
        nti = sb("nti", [P, E1], i32)
        nts = sb("nts", [P, E1])
        enda = sb("enda", [P, E1])
        base = sb("base", [P, E1])
        slotf = sb("slotf", [P, NTT * TOPK])
        sloti = sb("sloti", [P, NTT * TOPK], i32)
        slotu = [sb(f"slotu{n}", [P, NTT * TOPK], u32) for n in (0, 1)]
        tq = sb("tq", [P, NTT * TOPK], i32)
        tqf = sb("tqf", [P, NTT * TOPK])
        smf = sb("smf", [P, NTT * TOPK])
        gidx = sb("gidx", [P, NT1], u32)
        wtile = sb("wtile", [P, NT1])
        texf = sb("texf", [P, NT1])
        texi = sb("texi", [P, NT1], i32)
        selc = sb("selc", [96, NT0], bf16)
        idxs = sb("idxs", [P, 4], u32)
        idx4 = sb("idx4", [P, 2, TOPK], u32)
        stk = sb("stk", [P, 2, 2, SEQ])
        mxs = sb("mxs", [P, 4, 2])
        rec = sb("rec", [P, 2, HALF])

        ps = ctx.enter_context(nc.psum_tensor("ps", [P, 8, 512], f32))
        psf = ps[:, :, :].rearrange("p b n -> p (b n)")

        s_cst, s_x, s_wr, s_bias, s_wqkv, s_w0, s_w1, s_wqvu1, s_small1, s_tab1 = map(sem, (
            "cst_in", "x_in", "wr_in", "bias_in", "wqkv_in", "experts0_in", "experts1_in", "wqvu1_in",
            "small1_in", "tables1_in"))
        s_cbf = sem("casts_done")
        s_bsp = sem("bias_split_done")
        s_pool = sem("pool_chain")
        s_dve = sem("dve_chain")
        s_act = sem("act_chain")
        s_out = sem("out_stored")

        class Layer:

            def __init__(self, n):
                self.n, self.E, self.F, self.NT = n, (E0, E1)[n], (F0, F1)[n], (NT0, NT1)[n]
                self.KF, self.FP = -(-self.F // P), min(self.F, P)
                self.xnT = (xnT0, xnT1)[n]
                self.wr = (wr0_sb, wr1_sb)[n]
                self.ve_ready = sem(f"variances{n}")
                self.sd_ready = sem(f"deviations{n}")
                self.xn_ready = sem(f"xn_ready{n}")
                self.xn_stored = sem(f"xn_stored{n}")
                self.xT_done = sem(f"xnT_done{n}")
                self.xnT_ready = sem(f"xnT_ready{n}")
                self.qkv_done = sem(f"projected{n}")
                self.qkv_read = sem(f"projected_read{n}")
                self.logits_done = sem(f"logits_done{n}")
                self.wexp_in = sem(f"top_logits{n}")
                self.wexp_out = sem(f"top_exps{n}")
                self.m_ready = sem(f"choices{n}")
                self.rank_done = sem(f"ranks_done{n}")
                self.ab_ready = sem(f"onehots_ready{n}")
                self.ab_used = sem(f"onehots_used{n}")
                self.idx_ready = sem(f"tile_lists_ready{n}")
                self.icol = sem(f"index_column{n}")
                self.xg_full = [sem(f"gathered{n}_{j}") for j in range(4)]
                self.xgT_done = sem(f"gathered_turned{n}")
                self.xgT_ready = sem(f"xgT_ready{n}")
                self.gu_done = sem(f"gate_up_done{n}")
                self.g_ready = sem(f"gate_ready{n}")
                self.u_ready = sem(f"up_ready{n}")
                self.sig_ready = sem(f"sigmoid_ready{n}")
                self.h1_ready = sem(f"half_gated{n}")
                self.h_ready = sem(f"hidden_ready{n}")
                self.hT_done = sem(f"hidden_turned{n}")
                self.hT_ready = sem(f"hT_ready{n}")
                self.y_done = sem(f"down_done{n}")
                self.y_ready = sem(f"weighted_ready{n}")
                self.y_stored = [sem(f"weighted_stored{n}_{j}") for j in range(4)]
                self.icol4 = sem(f"index_rows{n}")
                self.cg_full = [sem(f"four_rows{n}_{j}") for j in range(2)]
                self.cg_read = sem(f"four_rows_read{n}")
                self.f_ready = sem(f"expert_sum_ready{n}")
                self.fsig_ready = sem(f"expert_sum_sigmoid{n}")
                self.g_done = sem(f"block_rows_ready{n}")

        L = [Layer(0), Layer(1)]
        (s_rope, s_hl, s_hi, s_vst, s_vz, s_stkT, s_stk, s_sc, s_mx, s_exp, s_pT, s_pTr, s_pv, s_otr, s_oa, s_rec, s_on,
         s_oT, s_oTr, s_wo, s_s, s_fp, s_f, s_fe, s_sil) = map(sem, (
            "rope_done", "parts_ready", "high_parts_ready", "v_columns_ready", "v_zeros_ready", "stack_turned",
            "stack_ready", "scores_done", "min_ready", "probs_ready", "probsT_done", "probsT_ready", "half_attended",
            "attnT_read", "attn_turned_back", "recip_ready", "attn_ready", "attnT_done", "attnT_ready",
            "wo_done", "s_read", "pair_sums", "expert_sum", "half_tanh", "gated"))
        s_x1 = sem("x1_ready")
        s_rst = sem("rope_steps")
        s_here = sem("waits_taken")
        s_shrow, s_bn1, s_a1n = map(sem, ("shared_rows_read", "stats1_ready", "a1_gated"))
        s_z, s_e, s_row1, s_qT1, s_qT1r, s_kv, s_kvr, s_o1, s_ln1, s_sd1, s_a1, s_a1T, s_a1Tr, s_wo1, s_s1, s_shd, s_shsig, s_shr, s_sdn = map(sem, (
            "z_ready", "zfun_ready", "rows1_ready", "q1T_done", "q1T_ready", "kv_done", "kv_ready", "o1_done",
            "ln1_var", "ln1_sd", "a1_ready", "a1T_done", "a1T_ready", "wo1_done", "s1_ready",
            "shared_up_done", "shared_sig", "shared_ready", "shared_down_done"))

        def ge(eng, s, v):
            if not isinstance(v, int) or v > 0:
                eng.wait_ge(s, v)

        def run_steps(eng, total, body, first, rounds, stages):
            def step(u, g):
                for lag, every, work in stages:
                    v = u - lag
                    if v % every or (g is None and not 0 <= v < total):
                        continue
                    count = body // every
                    if g is None:
                        work(v // every, v // every % count)
                    else:
                        assert 0 <= v and v + body * (rounds - 1) < total
                        work(g * count + v // every, v // every % count)

            lags = [lag for lag, _, _ in stages]
            for u in range(min(lags), first):
                step(u, None)
            with eng.Fori(0, rounds) as g:
                for c in range(body):
                    step(first + c, g)
            for u in range(first + body * rounds, total + max(lags)):
                step(u, None)

        def run_tiles(eng, s, stages):
            run_steps(eng, s.NT, 4, 8, s.NT // 4 - 2, [(n, 1, stage) for n, stage in enumerate(stages) if stage])

        def run_heads(eng, stages):
            run_steps(eng, BATCH * HEADS, HEADS, 12, BATCH - 1, stages)

        block = ctx.enter_context(nc.Block())

        @block.sync
        def _(sp):
            sp.dma_start(xr[:, :, :], x.rearrange("(t p) d -> p t d", p=P)).then_inc(s_x, 16)
            sp.dma_start(cst[:, :], consts).then_inc(s_cst, 16)
            sp.dma_start(wr0_sb[:, :, :], wr0).then_inc(s_wr, 16)
            sp.dma_start(rb0_sb[:, :], rb0.partition_broadcast(P)).then_inc(s_wr, 16)
            sp.dma_start(wqkv_sb[:, :, :], wqkv0).then_inc(s_wqkv, 16)
            sp.dma_start(wo0_sb[:, :, :], wo0).then_inc(s_wqkv, 16)
            for j in range(3):
                sp.dma_start(gub_f[32 * j:32 * j + E0, :], gub0).then_inc(s_bias, 16)
                sp.dma_start(dnb_f[32 * j:32 * j + E0, :], dnb0).then_inc(s_bias, 16)
            sp.dma_start(wr1_sb[:, :, :], wr1).then_inc(s_small1, 16)
            sp.dma_start(b768_sb[:, :], b768.partition_broadcast(P)).then_inc(s_small1, 16)
            sp.dma_start(lnb_sb[:, :], lnrow[1:2, :].partition_broadcast(P)).then_inc(s_small1, 16)

            def store_xn(s):
                for i in range(NTT):
                    sp.wait_ge(s.xn_ready, i + 1)
                    sp.dma_start(xn_dram[s.n][i * P:(i + 1) * P, :], xn[:, i, :]).then_inc(s.xn_stored, 16)

            def store_tiles(s):
                rows = ys_dram[s.n].rearrange("(t p) d -> t p d", p=P)
                with sp.Fori(0, s.NT // 4) as g:
                    for j in range(4):
                        t = g * 4 + j
                        sp.wait_ge(s.y_ready, t + 1)
                        sp.dma_start(rows[t], ybuf[:, j, :]).then_inc(s.y_stored[j], 16)

            store_xn(L[0])
            sp.wait_ge(L[0].qkv_done, NTT)
            sp.dma_start(wqkv_sb[:, :, :], wqvu1).then_inc(s_wqvu1, 16)
            store_tiles(L[0])
            sp.wait_ge(L[0].y_done, NT0)
            for c in range(8):
                sp.wait_ge(s_f, c + 1)
                e = slice(c * 4, c * 4 + 4)
                sp.dma_start(gu1_sb.rearrange("p (e n) -> p e n", e=E1)[:, e, :], gu1[:, e, :]).then_inc(s_w1, 16)
                sp.dma_start(dn1_sb.rearrange("p (e n) -> p e n", e=E1)[:, e, :], dn1[:, e, :]).then_inc(s_w1, 16)
            sp.dma_start(wsgu_sb, wsgu).then_inc(s_tab1, 16)
            sp.dma_start(wsdn_sb, wsdn).then_inc(s_tab1, 16)
            sp.dma_start(wo1_sb, wo1).then_inc(s_tab1, 16)
            sp.dma_start(lng_sb, lnrow[0:1, :].partition_broadcast(P)).then_inc(s_tab1, 16)
            sp.dma_start(bo1_sb, bo1.partition_broadcast(P)).then_inc(s_tab1, 16)
            store_xn(L[1])
            store_tiles(L[1])
            for i in range(NTT):
                sp.wait_ge(L[1].g_done, i + 1)
                sp.dma_start(out[i * P:(i + 1) * P, :], xr[:, i, :]).then_inc(s_out, 16)
            sp.wait_ge(s_out, 16 * NTT)

        @block.gpsimd
        def _(po):
            chain = [0]

            def link(ins):
                chain[0] += 1
                ins.then_inc(s_pool, 1)
                po.wait_ge(s_pool, chain[0])

            def here():
                po.sem_inc(s_here, 1)

            def gather_tiles(s):
                ge(po, s.xn_stored, 16 * NTT)
                po.wait_ge(s.idx_ready, 1)

                def one(t, j):
                    if not isinstance(t, int) or t >= 4:
                        po.wait_ge(s.xgT_done, t - 3)
                    po.tensor_copy(idxs[:, j:j + 1], gidx[:, bass.ds(t, 1)]).then_inc(s.icol, 1)
                    po.wait_ge(s.icol, t + 1)
                    here()
                    po.indirect_dma_start(xg[:, j, :], None, xn_dram[s.n],
                                          bass.IndirectOffsetOnAxis(ap=idxs[:, j:j + 1], axis=0))\
                      .then_inc(s.xg_full[j], 16)

                def four(g):
                    for j in range(4):
                        one(g * 4 + j, j)

                four(0)
                mixed = BATCH if s.n == 0 else 0
                if s.n == 0:
                    po.memset(vst[:, :, :, :, DH:DH + 1], 1.0).then_inc(s_vz, 1)
                    po.memset(vst[:, :, :, :, DH + 1:], 0.0).then_inc(s_vz, 1)
                    po.wait_ge(s.qkv_read, 2 * NTT)
                    here()
                    with po.Fori(0, mixed) as g:
                        four(g * 2 + 1)
                        rotate(g * 2, 0, g * 2)
                        four(g * 2 + 2)
                        rotate(g * 2 + 1, 1, g * 2 + 1)
                with po.Fori(0, s.NT // 4 - 1 - 2 * mixed) as g:
                    four(g + 1 + 2 * mixed)

            def rotate(i, tt, n):
                ct, st = (cst[:, c + 2 * DH * tt:c + 2 * DH * (tt + 1)].rearrange("p (w d) -> p w d", w=2) for c in (C_COS, C_SIN))
                raw = qk_raw[:, bass.ds(i, 1), :].rearrange("p o (w h d) -> p (o w) h d", w=2, d=DH)
                half = DH // 2

                def wide(a, lo, hi):
                    return a[:, :, lo:hi].unsqueeze(2).broadcast_to([P, 2, HEADS, hi - lo])

                po.tensor_tensor(rtmp[:, :, :, 0:half], raw[:, :, :, half:DH], wide(st, 0, half), ALU.mult).then_inc(s_rst, 1)
                po.tensor_tensor(rtmp[:, :, :, half:DH], raw[:, :, :, 0:half], wide(st, half, DH), ALU.mult).then_inc(s_rst, 1)
                po.wait_ge(s_rst, n * 3 + 2)
                here()
                po.tensor_tensor(raw, raw, wide(ct, 0, DH), ALU.mult).then_inc(s_rst, 1)
                po.wait_ge(s_rst, n * 3 + 3)
                here()
                po.tensor_tensor(raw, raw, rtmp[:, :, :, :], ALU.add).then_inc(s_rope, 1)
                po.wait_ge(s_rope, n + 1)
                here()

            def gather_back(s, i, j):
                if not isinstance(i, int) or i >= 2:
                    po.wait_ge(s.cg_read, i - 1)
                po.tensor_copy(idx4[:, j, :], slotu[s.n][:, bass.ds(i * TOPK, TOPK)]).then_inc(s.icol4, 1)
                po.wait_ge(s.icol4, i + 1)
                here()
                for k in range(TOPK):
                    po.indirect_dma_start(cg[:, j, k, :], None, ys_dram[s.n],
                                          bass.IndirectOffsetOnAxis(ap=idx4[:, j, k:k + 1], axis=0))\
                      .then_inc(s.cg_full[j], 16)

            def tiles_stored(s):
                for j in range(4):
                    po.wait_ge(s.y_stored[j], 16 * (s.NT // 4))

            link(po.memset(gub_bf[:, :], 0.0))
            link(po.memset(dnb_bf[:, :], 0.0))
            po.wait_ge(s_bias, 96)
            for full, part, n in ((gub_f, gub_bf, 2 * F0), (dnb_f, dnb_bf, D)):
                for j in range(3):
                    rows = slice(32 * j, 32 * j + E0)
                    for m in range(j):
                        link(po.tensor_copy(bsp[rows, 0:n], full[rows, :]))
                        link(po.tensor_tensor(full[rows, :], full[rows, :], bsp[rows, 0:n], ALU.subtract))
                    link(po.tensor_copy(part[rows, :], full[rows, :]))
            po.engine_nop().then_inc(s_bsp, 1)

            gather_tiles(L[0])

            def one(shape):
                a = ones_e[:, 0:1]
                for _ in shape[2:]:
                    a = a.unsqueeze(1)
                return a.broadcast_to(shape)

            def split(b, j):
                if not isinstance(b, int):
                    po.wait_ge(s_stkT, b * 8 + 4 * j - 4)
                    here()
                raw = [qk_raw[:, bass.ds(b * 2 + tt, 1), :].rearrange("p o (w h d) -> p (o w) h d", w=2, d=DH)
                       [:, :, HALF * j:HALF * (j + 1), :] for tt in range(2)]

                def places(tt, w, part):
                    a = parts[j][:, tt, w, :, :]
                    if w == 0:
                        return a.rearrange("p h (r c d) -> p h r c d", r=2, c=2)[:, :, :, part, :]
                    return a.rearrange("p h (c r d) -> p h c r d", r=2, c=2)[:, :, part, :, :]

                def twice(a):
                    return a.unsqueeze(2).broadcast_to([P, HALF, 2, DH])

                for tt in range(2):
                    for w in range(2):
                        po.tensor_tensor(places(tt, w, 0).bitcast(f32r), twice(raw[tt][:, w, :, :]), one([P, HALF, 2, DH]), ALU.mult)\
                          .then_inc(s_hi, 1)
                po.wait_ge(s_hi, b * 8 + 4 * j + 4)
                here()
                for tt in range(2):
                    for w in range(2):
                        ins = po.tensor_tensor(places(tt, w, 1).bitcast(f32r), twice(raw[tt][:, w, :, :]),
                                               places(tt, w, 0), ALU.subtract)
                ins.then_inc(s_hl, 1)

            def values(b, j):
                if not isinstance(b, int) or b > 0:
                    po.wait_ge(s_pv, b * 2 + j)
                    here()
                po.tensor_tensor(vst[:, j, :, :, 0:DH], v_rows[:, bass.ds(b * 2, 2), HALF * DH * j:HALF * DH * (j + 1)]
                                 .rearrange("p t (h d) -> p t h d", d=DH), one([P, 2, HALF, DH]), ALU.mult).then_inc(s_vst, 1)

            def fetch(b, j):
                po.tensor_copy(idx4[:, j, :], slotu[0][:, bass.ds(b * 2 * TOPK + j * TOPK, TOPK)]).then_inc(L[0].icol4, 1)
                po.wait_ge(L[0].icol4, b * 2 + j + 1)
                here()
                for k in range(TOPK):
                    po.indirect_dma_start(cg[:, j, k, :], None, ys_dram[0],
                                          bass.IndirectOffsetOnAxis(ap=idx4[:, j, k:k + 1], axis=0))                      .then_inc(L[0].cg_full[j], 16)

            def total(b, j):
                if j == 0 and not (isinstance(b, int) and b == 0):
                    po.wait_ge(s_sil, b)
                po.wait_ge(L[0].cg_full[j], b * 64 + 64)
                here()
                po.tensor_tensor(csum0.rearrange("p (k n) -> p k n", k=2), cg[:, j, 0:2, :], cg[:, j, 2:4, :], ALU.add)                  .then_inc(s_fp, 1)
                po.wait_ge(s_fp, b * 2 + j + 1)
                here()
                po.tensor_tensor(fsum[:, j, :], csum0[:, 0:D], csum0[:, D:2 * D], ALU.add).then_inc(s_f, 1)
                po.wait_ge(s_f, b * 2 + j + 1)
                here()

            split(0, 0)
            values(0, 0)
            po.wait_ge(L[0].y_ready, NT0)
            split(0, 1)
            tiles_stored(L[0])
            with po.Fori(0, BATCH - 1) as b:
                fetch(b, 0)
                fetch(b, 1)
                values(b, 1)
                split(b + 1, 0)
                total(b, 0)
                values(b + 1, 0)
                split(b + 1, 1)
                total(b, 1)
            b = BATCH - 1
            fetch(b, 0)
            fetch(b, 1)
            values(b, 1)
            total(b, 0)
            total(b, 1)

            gather_tiles(L[1])
            tiles_stored(L[1])
            for i in range(NTT):
                gather_back(L[1], i, i % 2)

        @block.scalar
        def _(ac):
            ac.wait_ge(s_x, 16)
            for c in range(4):
                e = slice(c * 4, c * 4 + 4)
                ac.dma_start(gu0_sb.rearrange("p (e n) -> p e n", e=E0)[:, e, :], gu0[:, e, :]).then_inc(s_w0, 16)
                ac.dma_start(dn0_sb.rearrange("p (e n) -> p e n", e=E0)[:, e, :], dn0[:, e, :]).then_inc(s_w0, 16)

            def norm_and_turn(s):
                ac.wait_ge(s.ve_ready, 1)
                ac.activation(sd[:, :], sd[:, :], ACT.Sqrt).then_inc(s.sd_ready, 1)
                for i in range(NTT):
                    ac.wait_ge(s.xT_done, i + 1)
                    ac.activation(s.xnT[:, :, i * P:(i + 1) * P],
                                  ps[:, i % 2, 0:D].rearrange("p (k t) -> p k t", k=KD), ACT.Copy)\
                      .then_inc(s.xnT_ready, 1)

            def top_exp(s):
                ac.wait_ge(s.wexp_in, 1)
                ac.activation(wraw[:, :, :], wraw[:, :, :], ACT.Exp).then_inc(s.wexp_out, 1)

            def tiles(s):
                ac.wait_ge(s.idx_ready, 1)

                def turn(t, j):
                    ac.wait_ge(s.xgT_done, t + 1)
                    if not isinstance(t, int) or t >= 2:
                        ac.wait_ge(s.gu_done, t - 1)
                    ac.activation(xgT[:, j % 2, :, :], ps[:, j % 2, 0:D].rearrange("p (k t) -> p k t", k=KD), ACT.Copy)\
                      .then_inc(s.xgT_ready, 1)

                def gate(t, j):
                    if s.n == 0:
                        ac.wait_ge(s.g_ready, t + 1)
                        ac.activation(sig[:, j % 2, 0:s.F], gbuf[:, j % 2, :], ACT.Sigmoid, scale=ALPHA)\
                          .then_inc(s.sig_ready, 1)
                    else:
                        ac.wait_ge(s.gu_done, t + 1)
                        if not isinstance(t, int) or t >= 2:
                            ac.wait_ge(s.h_ready, t - 1)
                        ac.activation(sig[:, j % 2, 0:s.F], ps[:, 2 + j % 2, 0:s.F], ACT.Sigmoid)\
                          .then_inc(s.sig_ready, 1)

                def weigh(t, j):
                    ac.wait_ge(s.y_done, t + 1)
                    if not isinstance(t, int) or t >= 4:
                        ac.wait_ge(s.y_stored[j], (t - j) * 4)
                    ac.activation(ybuf[:, j, :], ps[:, 6 + j % 2, 0:D], ACT.Copy, scale=wtile[:, bass.ds(t, 1)])\
                      .then_inc(s.y_ready, 1)

                run_tiles(ac, s, (turn, gate, None, weigh))

            norm_and_turn(L[0])
            def qkv0(i):
                ac.wait_ge(L[0].qkv_done, i + 1)
                b0 = 4 + 2 * (i % 2)
                ac.activation(qk_raw[:, i, :], ps[:, b0, :], ACT.Copy).then_inc(L[0].qkv_read, 1)
                ac.activation(v_rows[:, i, :], ps[:, b0 + 1, 0:D], ACT.Copy).then_inc(L[0].qkv_read, 1)

            qkv0(0)
            top_exp(L[0])
            for i in range(1, NTT):
                qkv0(i)
            tiles(L[0])

            def stack(n, j):
                ac.wait_ge(s_stkT, n + 1)
                ac.activation(stk[:, j % 2, :, :].bitcast(f32r), ps[:, 0, :].rearrange("p (w t) -> p w t", w=2), ACT.Copy)                  .then_inc(s_stk, 1)

            def probs(h, j):
                ac.wait_ge(s_mx, h * 2 + 2)
                if not isinstance(h, int) or h >= 2:
                    ac.wait_ge(s_pT, h - 1)
                for tt, cols in ((0, slice(0, P)), (1, slice(P, 3 * P))):
                    ins = ac.activation(pr[:, j % 2, cols], ps[:, 1 + j % 2, cols], ACT.Exp,
                                        bias=mxs[:, j % 4, tt:tt + 1], scale=-1.0)
                ins.then_inc(s_exp, 1)

            def turned0(n, j):
                ac.wait_ge(s_oT, n + 1)
                ac.activation(oTs[:, j, :], ps[:, 7, 0:SEQ], ACT.Copy).then_inc(s_oTr, 1)

            def gate_tanh(b, j):
                ac.wait_ge(s_f, b * 2 + 2)
                ac.activation(ftanh, fsum, ACT.Tanh, scale=0.5).then_inc(s_fe, 1)

            run_heads(ac, [(-4, 2, stack), (-2, 1, probs), (12, HALF, turned0), (18, HEADS, gate_tanh)])

            norm_and_turn(L[1])

            def qvu1(i):
                ac.wait_ge(L[1].qkv_done, i + 1)
                b0 = 4 + 2 * (i % 2)
                ac.activation(att[:, 0:6144].rearrange("p (w t n) -> p w t n", w=3, t=NTT)[:, :, i, :],
                              psf[:, b0 * 512:b0 * 512 + 3 * D].rearrange("p (w n) -> p w n", w=3), ACT.Copy)\
                  .then_inc(L[1].qkv_read, 1)

            qvu1(0)
            top_exp(L[1])
            for i in range(1, NTT):
                qvu1(i)
            tiles(L[1])
            ac.wait_ge(s_z, 1)
            ac.activation(rowtmp[:, 0, :, :], v1r, ACT.Sigmoid).then_inc(s_e, 1)
            ac.wait_ge(s_z, 2)
            ac.activation(rowtmp[:, 1, :, :], u1r, ACT.Sigmoid).then_inc(s_e, 1)

            def shared(h, m):
                n = 4 * h + m
                ac.wait_ge(s_shd, n + 1)
                if n >= 2:
                    ac.wait_ge(s_shr, n - 1)
                ac.activation(shs[:, n % 2, :], ps[:, n % 2, :], ACT.Sigmoid).then_inc(s_shsig, 1)

            def shared_rows(h):
                for i in range(4 * h, 4 * h + 4):
                    ac.wait_ge(s_sdn, i + 1)
                    ac.activation(sh1r[:, i, :], ps[:, 4 + i % 2, 0:D], ACT.Copy).then_inc(s_shrow, 1)

            for h in range(2):
                for m in range(4):
                    shared(h, m)
                shared_rows(h)
            ac.wait_ge(s_z, 3)
            ac.activation(rowtmp[:, 0, :, :], q1r, ACT.Exp).then_inc(s_e, 1)
            for b in range(BATCH):
                ac.wait_ge(s_qT1, b + 1)
                ac.activation(q1T[:, :, b * SEQ:(b + 1) * SEQ], ps[:, b % 2, :].rearrange("p (g t) -> p g t", g=2), ACT.Copy)\
                  .then_inc(s_qT1r, 1)
                for i in (2 * b, 2 * b + 1):
                    ac.wait_ge(s_o1, i + 1)
                    ac.activation(a1r[:, i, :], ps[:, 2 + i % 2, 0:D], ACT.Copy).then_inc(s_a1, 1)
            ac.wait_ge(s_ln1, 1)
            ac.activation(sd[:, :], sd[:, :], ACT.Sqrt).then_inc(s_sd1, 1)
            for i in range(NTT):
                ac.wait_ge(s_a1T, i + 1)
                if i >= 2:
                    ac.wait_ge(s_wo1, i - 1)
                ac.activation(a1T[:, i % 2, :, :], ps[:, 4 + i % 2, 0:D].rearrange("p (k t) -> p k t", k=KD), ACT.Copy)\
                  .then_inc(s_a1Tr, 1)
            for i in range(NTT):
                ac.wait_ge(L[1].f_ready, i + 1)
                ac.activation(fsig[:, i % 2, :], fbuf[:, i % 2, :], ACT.Sigmoid).then_inc(L[1].fsig_ready, 1)

        @block.tensor
        def _(pe):
            def turn_and_route(s):
                pe.wait_ge(s_cst, 16)
                pe.wait_ge(s_wr if s.n == 0 else s_small1, 32 if s.n == 0 else 48)
                for i in range(NTT + 1):
                    if i < NTT:
                        pe.wait_ge(s.xn_ready, i + 1)
                        if i >= 2:
                            pe.wait_ge(s.xnT_ready, i - 1)
                        for k in range(KD):
                            mm = pe.transpose(ps[:, i % 2, k * P:(k + 1) * P], xn[:, i, k * P:(k + 1) * P], ident)
                        mm.then_inc(s.xT_done, 1)
                    if i >= 1:
                        pe.wait_ge(s.xnT_ready, i)
                        for k in range(KD):
                            mm = pe.matmul(ps[:, 2, (i - 1) * s.E:i * s.E], s.xnT[:, k, (i - 1) * P:i * P],
                                           s.wr[:, k, :], start=(k == 0), stop=(k == KD - 1))
                mm.then_inc(s.logits_done, 1)

            def project(s, i):
                if i == 0:
                    if s.n == 0:
                        pe.wait_ge(s_wqkv, 32)
                    else:
                        pe.wait_ge(s_wqvu1, 16)
                if i >= 2:
                    pe.wait_ge(s.qkv_read, (i - 1) * (2 if s.n == 0 else 1))
                b0 = 4 + 2 * (i % 2)
                for n0, n1 in ((0, 512), (512, 768)):
                    for k in range(KD):
                        mm = pe.matmul(psf[:, b0 * 512 + n0:b0 * 512 + n1], s.xnT[:, k, i * P:(i + 1) * P],
                                       wqkv_sb[:, k, n0:n1], start=(k == 0), stop=(k == KD - 1))
                mm.then_inc(s.qkv_done, 1)

            def rank(s):
                pe.wait_ge(s.m_ready, 1)
                pe.wait_ge(s_cbf, 4)
                cnt = mcnt[:, 0:NTT * s.E].rearrange("p (t e) -> p t e", e=s.E)
                out3 = ps[:, 3, 0:NTT * s.E].rearrange("p (t e) -> p t e", e=s.E)
                pe.matmul(out3, tri_bf[:, :], cnt, start=True, stop=False)
                for j in range(NTT - 1):
                    n = NTT - 1 - j
                    pe.matmul(out3[:, j + 1:NTT, :], ones_bf[:, :], cnt[:, j, :].unsqueeze(1).broadcast_to([P, n, s.E]),
                              start=False, stop=(j == NTT - 2))
                for j in range(NTT):
                    mm = pe.matmul(ps[:, 3, 256:256 + s.E], ones_bf[:, :], cnt[:, j, :], start=(j == 0), stop=(j == NTT - 1))
                mm.then_inc(s.rank_done, 1)

            def place(s, i):
                pe.wait_ge(s.ab_ready, i + 1)
                for k in range(TOPK):
                    mm = pe.matmul(ps[:, 2, 0:2 * s.NT], amat[:, i % 2, k, :], bmat[:, i % 2, k, 0:2 * s.NT],
                                   start=(i == 0 and k == 0), stop=(i == NTT - 1 and k == TOPK - 1))
                mm.then_inc(s.ab_used, 1)

            def tiles(s):
                pe.wait_ge(s.idx_ready, 1)
                pe.wait_ge(s.qkv_read, NTT * (2 if s.n == 0 else 1))
                if s.n == 0:
                    pe.wait_ge(s_w0, 128)
                    pe.wait_ge(s_bsp, 1)
                else:
                    pe.wait_ge(s_w1, 256)
                    pe.wait_ge(s_tab1, 80)
                gu, dn = ((gu0_sb, dn0_sb), (gu1_sb, dn1_sb))[s.n]

                def turn(t, j):
                    pe.wait_ge(s.xg_full[j], (t + (4 - j)) * 4)
                    if not isinstance(t, int) or t >= 2:
                        pe.wait_ge(s.xgT_ready, t - 1)
                    for k in range(KD):
                        mm = pe.transpose(ps[:, j % 2, k * P:(k + 1) * P], xg[:, j, k * P:(k + 1) * P], ident)
                    mm.then_inc(s.xgT_done, 1)

                def up(t, j):
                    e = pe.value_load(texi[0:1, bass.ds(t, 1)], min_val=0, max_val=s.E - 1)
                    if not isinstance(t, int) or t >= 2:
                        pe.wait_ge(s.h_ready, t - 1)
                    b0, w = 2 + j % 2, 2 * s.F
                    if s.n == 0:
                        pe.matmul(ps[:, b0, 0:w], selc[:, bass.ds(t, 1)].broadcast_to([96, P]), gub_bf[:, :],
                                  start=True, stop=False)
                    pe.wait_ge(s.xgT_ready, t + 1)
                    for k in range(KD):
                        mm = pe.matmul(ps[:, b0, 0:w], xgT[:, j % 2, k, :], gu[:, bass.ds(e * (KD * w) + k * w, w)],
                                       start=(s.n == 1 and k == 0), stop=(k == KD - 1))
                    mm.then_inc(s.gu_done, 1)

                def turn_h(t, j):
                    pe.wait_ge(s.h_ready, t + 1)
                    if not isinstance(t, int) or t >= 2:
                        pe.wait_ge(s.hT_ready, t - 1)
                    for k in range(s.KF):
                        mm = pe.transpose(ps[0:s.FP, 4 + j % 2, k * P:(k + 1) * P], hbuf[:, j % 2, k * s.FP:(k + 1) * s.FP], ident)
                    mm.then_inc(s.hT_done, 1)

                def down(t, j):
                    e = pe.value_load(texi[0:1, bass.ds(t, 1)], min_val=0, max_val=s.E - 1)
                    if not isinstance(t, int) or t >= 2:
                        pe.wait_ge(s.y_ready, t - 1)
                    if s.n == 0:
                        pe.matmul(ps[:, 6 + j % 2, 0:D], selc[:, bass.ds(t, 1)].broadcast_to([96, P]), dnb_bf[:, :],
                                  start=True, stop=False)
                    pe.wait_ge(s.hT_ready, t + 1)
                    for k in range(s.KF):
                        mm = pe.matmul(ps[:, 6 + j % 2, 0:D], hT[0:s.FP, j % 2, k, :],
                                       dn[0:s.FP, bass.ds(e * (s.KF * D) + k * D, D)],
                                       start=(s.n == 1 and k == 0), stop=(k == s.KF - 1))
                    mm.then_inc(s.y_done, 1)

                run_tiles(pe, s, (turn, up, turn_h, down))

            turn_and_route(L[0])
            project(L[0], 0)
            project(L[0], 1)
            rank(L[0])
            for i in range(2, 5):
                project(L[0], i)
            for i in range(NTT):
                place(L[0], i)
                if i in (1, 3, 5):
                    project(L[0], 5 + i // 2)
            tiles(L[0])

            pe.wait_ge(L[0].y_ready, NT0)
            pe.wait_ge(s_vz, 2)
            pe.sem_inc(s_pv, 1)

            def stack_ready(n, j):
                pe.wait_ge(s_hl, n + 1)

            def turn_stack(n, j):
                if not isinstance(n, int) or n >= 1:
                    pe.wait_ge(s_stk, n)
                half, h = j // 4, 2 * (j % 4)
                for tt in range(2):
                    q, k = (parts[half][:, tt, w, h:h + 2, :].rearrange("p h n -> p (h n)") for w in range(2))
                    pe.transpose(ps[:, 0, tt * P:(tt + 1) * P], q, ident)
                    mm = pe.transpose(ps[:, 0, SEQ + tt * P:SEQ + (tt + 1) * P], k, ident)
                mm.then_inc(s_stkT, 1)

            def stack_in(n, j):
                pe.wait_ge(s_stk, n + 1)

            def scores(h, j):
                if not isinstance(h, int) or h >= 2:
                    pe.wait_ge(s_exp, h - 1)
                bank = ps[:, 1 + j % 2, :]
                rows = slice(64 * (j % 2), 64 * (j % 2) + 64)
                q, k = (stk[rows, j // 2 % 2, w, :].bitcast(f32r) for w in range(2))
                pe.matmul(bank[:, 0:P], q[:, 0:P], k[:, 0:P], start=True, stop=False)
                pe.matmul(bank[:, 0:P], ident_bf[:, :], mask_bf[:, :], start=False, stop=True)
                pe.matmul(bank[:, P:3 * P], q[:, P:2 * P], k[:, :], start=True, stop=False)
                pe.matmul(bank[:, 2 * P:3 * P], ident_bf[:, :], mask_bf[:, :], start=False, stop=True).then_inc(s_sc, 1)

            def turn_probs(h, j):
                if isinstance(h, int) and h >= BATCH * HEADS - 2:
                    pe.wait_ge(s_exp, h + 1)
                for n in range(3):
                    mm = pe.transpose(ps[:, 3 + j % 2, n * P:(n + 1) * P], pr[:, j % 2, n * P:(n + 1) * P], ident)
                mm.then_inc(s_pT, 1)

            def values_in(n, j):
                pe.wait_ge(s_vst, n + 1)

            def attend(h, j):
                pe.wait_ge(s_pTr, h + 1)
                half, m = j // HALF, j % HALF
                o = ps[32 * (m % 4):32 * (m % 4) + 32, 5 + half, (m // 4) * SEQ:(m // 4 + 1) * SEQ]
                pe.matmul(o, vst[:, half, 0, m, :], prT[:, j % 2, 0:SEQ], start=True, stop=False)
                mm = pe.matmul(o[:, P:SEQ], vst[:, half, 1, m, :], prT[:, j % 2, SEQ:3 * P], start=False, stop=True)
                if m == HALF - 1:
                    mm.then_inc(s_pv, 1)

            def residual_read(b, j):
                pe.wait_ge(s_s, b + 1)

            def turn_back(n, j):
                pe.wait_ge(s_otr, n + 1)
                if not isinstance(n, int) or n >= 1:
                    pe.wait_ge(s_oTr, n)
                for tt in range(2):
                    for g in range(2):
                        mm = pe.transpose(ps[:, 7, tt * SEQ + g * P:tt * SEQ + (g + 1) * P], otb[:, g * SEQ + tt * P:g * SEQ + (tt + 1) * P], ident)
                mm.then_inc(s_oa, 1)

            def turn_rows(n, j):
                pe.wait_ge(s_on, n + 1)
                for tt in range(2):
                    mm = pe.transpose(ps[:, 7, tt * P:(tt + 1) * P], ost[:, tt, :], ident)
                mm.then_inc(s_oT, 1)

            def project0(b, j):
                pe.wait_ge(s_oTr, b * 2 + 2)
                for tt in range(2):
                    for k in range(KD):
                        mm = pe.matmul(ps[:, 7, tt * D:(tt + 1) * D], oTs[:, k, tt * P:(tt + 1) * P], wo0_sb[:, k, :],
                                       start=(k == 0), stop=(k == KD - 1))
                mm.then_inc(s_wo, 1)

            run_heads(pe, [(-4, HALF, stack_ready), (-4, 2, turn_stack), (-2, 2, stack_in), (-2, 1, scores), (0, 1, turn_probs),
                           (1, HALF, values_in), (1, 1, attend), (26, HEADS, residual_read), (10, HALF, turn_back),
                           (12, HALF, turn_rows), (22, HEADS, project0)])

            pe.wait_ge(s_s, BATCH)
            turn_and_route(L[1])
            project(L[1], 0)
            project(L[1], 1)
            rank(L[1])
            for i in range(2, 5):
                project(L[1], i)
            for i in range(NTT):
                place(L[1], i)
                if i in (1, 3, 5):
                    project(L[1], 5 + i // 2)
            tiles(L[1])

            pe.wait_ge(L[1].y_ready, NT1)
            for h in range(2):
                toks = slice(h * 512, (h + 1) * 512)
                for m in range(4):
                    n = 4 * h + m
                    if n >= 2:
                        pe.wait_ge(s_shr, n - 1)
                    for w in range(2):
                        for k in range(KD):
                            mm = pe.matmul(ps[:, n % 2 + 2 * w, :], wsgu_sb[:, k, w * SH + m * P:w * SH + (m + 1) * P],
                                           L[1].xnT[:, k, toks], start=(k == 0), stop=(k == KD - 1))
                    mm.then_inc(s_shd, 1)
                pe.wait_ge(s_shr, 4 * h + 4)
                for i in range(4 * h, 4 * h + 4):
                    if i >= 2:
                        pe.wait_ge(s_shrow, i - 1)
                    for m in range(4):
                        mm = pe.matmul(ps[:, 4 + i % 2, 0:D], shg[:, m, (i % 4) * P:(i % 4 + 1) * P], wsdn_sb[:, m, :],
                                       start=(m == 0), stop=(m == 3))
                    mm.then_inc(s_sdn, 1)

            pe.wait_ge(s_row1, 2)
            for b in range(BATCH):
                for g in range(2):
                    for tt in range(2):
                        i = 2 * b + tt
                        mm = pe.transpose(ps[:, b % 2, g * SEQ + tt * P:g * SEQ + (tt + 1) * P], q1r[:, i, g * P:(g + 1) * P], ident) \
                            if b < 2 or not (g == 0 and tt == 0) else None
                        if mm is None:
                            pe.wait_ge(s_qT1r, b - 1)
                            mm = pe.transpose(ps[:, b % 2, 0:P], q1r[:, i, 0:P], ident)
                mm.then_inc(s_qT1, 1)
                if b >= 2:
                    pe.wait_ge(s_kvr, b - 1)
                for g in range(2):
                    for tt in range(2):
                        i = 2 * b + tt
                        mm = pe.matmul(ps[:, 6 + b % 2, g * P:(g + 1) * P], q1r[:, i, g * P:(g + 1) * P], v1r[:, i, g * P:(g + 1) * P],
                                       start=(tt == 0), stop=(tt == 1))
                mm.then_inc(s_kv, 1)
                pe.wait_ge(s_kvr, b + 1)
                pe.wait_ge(s_qT1r, b + 1)
                for tt in range(2):
                    i = 2 * b + tt
                    if i >= 2:
                        pe.wait_ge(s_a1, i - 1)
                        pe.wait_ge(s_bn1, i - 1)
                    for g in range(2):
                        mm = pe.matmul(ps[:, 2 + i % 2, g * P:(g + 1) * P], q1T[:, g, i * P:(i + 1) * P], kvb[:, b % 2, g, :],
                                       start=True, stop=True)
                    mm.then_inc(s_o1, 1)
            pe.wait_ge(s_shrow, NTT)
            for i in range(NTT + 1):
                if i < NTT:
                    pe.wait_ge(s_a1n, i + 1)
                    if i >= 2:
                        pe.wait_ge(s_a1Tr, i - 1)
                    for k in range(KD):
                        mm = pe.transpose(ps[:, 4 + i % 2, k * P:(k + 1) * P], a1r[:, i, k * P:(k + 1) * P], ident)
                    mm.then_inc(s_a1T, 1)
                if i >= 1:
                    pe.wait_ge(s_a1Tr, i)
                    if i >= 3:
                        pe.wait_ge(s_s1, i - 2)
                    for k in range(KD):
                        mm = pe.matmul(ps[:, 6 + (i - 1) % 2, 0:D], a1T[:, (i - 1) % 2, k, :], wo1_sb[:, k, :],
                                       start=(k == 0), stop=(k == KD - 1))
                    mm.then_inc(s_wo1, 1)

        @block.vector
        def _(ve):
            chain = [0]

            def link(ins):
                chain[0] += 1
                ins.then_inc(s_dve, 1)
                ve.wait_ge(s_dve, chain[0])

            def normalise(s):
                for i in range(NTT):
                    if s.n == 0 or i == 0:
                        pass
                    ins = ve.bn_stats(bnst[:, i, :], xr[:, i, :])
                link(ins)
                for i in range(NTT):
                    ins = ve.bn_aggr(mv[:, i, :], bnst[:, i, :])
                link(ins)
                ve.tensor_scalar(sd[:, :], mv[:, :, 1], EPS, None, ALU.add).then_inc(s.ve_ready, 1)
                ve.wait_ge(s.sd_ready, 1)
                link(ve.reciprocal(rstd[:, :], sd[:, :]))
                for i in range(NTT):
                    ve.tensor_scalar(xn[:, i, :], xr[:, i, :], mv[:, i, 0:1], rstd[:, i:i + 1], ALU.subtract, ALU.mult)\
                      .then_inc(s.xn_ready, 1)

            def route(s):
                E, NT = s.E, s.NT
                lg = lgt[:, 0:NTT * E].rearrange("p (t e) -> p t e", e=E)
                ohv = oh[:, 0:NTT * TOPK * E].rearrange("p (t k e) -> p t k e", t=NTT, e=E) if NTT * TOPK * E <= 1024 else None
                s4 = sl4[:, 0:NTT * TOPK * E].rearrange("p (t k e) -> p t k e", t=NTT, e=E)
                ve.wait_ge(s.logits_done, 1)
                out_l = ps[:, 2, 0:NTT * E].rearrange("p (t e) -> p t e", e=E)
                if s.n == 0:
                    link(ve.tensor_tensor(lg, out_l, rb0_sb[:, :].unsqueeze(1).broadcast_to([P, NTT, E]), ALU.add))
                else:
                    link(ve.tensor_copy(lg, out_l))
                for i in range(NTT):
                    ins = ve.max(top[:, i, :], lg[:, i, :])
                link(ins)
                ve.tensor_tensor(wraw[:, :, :], top[:, :, 0:TOPK], top[:, :, 0:1].broadcast_to([P, NTT, TOPK]), ALU.subtract)\
                  .then_inc(s.wexp_in, 1)
                for i in range(NTT):
                    ins = ve.max_index(topi[:, i, :], top[:, i, :], lg[:, i, :])
                link(ins)
                link(ve.tensor_copy(topf[:, :, :], topi[:, :, 0:TOPK]))
                oh2 = oh[:, 0:NTT * TOPK * E].rearrange("p (n e) -> p n e", e=E)
                link(ve.tensor_tensor(oh2, iota[:, 0:E].unsqueeze(1).broadcast_to([P, NTT * TOPK, E]),
                                      topf[:, :, :].rearrange("p t k -> p (t k)").unsqueeze(2).broadcast_to([P, NTT * TOPK, E]),
                                      ALU.is_equal))
                with nc.allow_low_precision("zeros and ones: a token's four experts differ"):
                    ve.tensor_reduce(mcnt[:, 0:NTT * E].rearrange("p (t e) -> p t e", e=E), ohv.rearrange("p t k e -> p t e k"),
                                     AX.X, ALU.add).then_inc(s.m_ready, 1)
                ve.wait_ge(s.wexp_out, 1)
                link(ve.tensor_reduce(wsum[:, :], wraw[:, :, :], AX.X, ALU.add))
                link(ve.reciprocal(wsum[:, :], wsum[:, :]))
                link(ve.tensor_tensor(wtop[:, :, :], wraw[:, :, :], wsum[:, :].unsqueeze(2).broadcast_to([P, NTT, TOPK]), ALU.mult))
                ve.wait_ge(s.rank_done, 1)
                link(ve.tensor_scalar(nti[:, 0:E], ps[:, 3, 256:256 + E], float(P - 1), None, ALU.add))
                link(ve.tensor_scalar(nti[:, 0:E], nti[:, 0:E], 7, 7, ALU.arith_shift_right, ALU.logical_shift_left))
                link(ve.tensor_copy(nts[:, 0:E], nti[:, 0:E]))
                link(ve.tensor_tensor_scan(enda[:, 0:E], ones_e[:, 0:E], nts[:, 0:E], 0.0, ALU.mult, ALU.add))
                link(ve.tensor_tensor(base[:, 0:E], enda[:, 0:E], nts[:, 0:E], ALU.subtract))
                link(ve.tensor_tensor(lg, ps[:, 3, 0:NTT * E].rearrange("p (t e) -> p t e", e=E),
                                      base[:, 0:E].unsqueeze(1).broadcast_to([P, NTT, E]), ALU.add))
                link(ve.tensor_tensor(s4, ohv, lg.unsqueeze(2).broadcast_to([P, NTT, TOPK, E]), ALU.mult))
                link(ve.tensor_reduce(slotf[:, :], s4.rearrange("p t k e -> p (t k) e"), AX.X, ALU.add))
                ve.tensor_copy(slotu[s.n][:, :], slotf[:, :])
                link(ve.tensor_copy(sloti[:, :], slotf[:, :]))
                ve.tensor_scalar(tq[:, :], sloti[:, :], 7, None, ALU.arith_shift_right)
                link(ve.tensor_scalar(sloti[:, :], sloti[:, :], P - 1, None, ALU.bitwise_and))
                ve.tensor_copy(tqf[:, :], tq[:, :])
                link(ve.tensor_copy(smf[:, :], sloti[:, :]))
                for i in range(NTT):
                    if i >= 2:
                        ve.wait_ge(s.ab_used, i - 1)
                    pick = slice(i * TOPK, (i + 1) * TOPK)
                    ve.tensor_tensor(amat[:, i % 2, :, :], iota.unsqueeze(1).broadcast_to([P, TOPK, P]),
                                     smf[:, pick].unsqueeze(2).broadcast_to([P, TOPK, P]), ALU.is_equal)
                    bm = bmat[:, i % 2, :, :]
                    link(ve.tensor_tensor(bm[:, :, 0:NT], iota[:, 0:NT].unsqueeze(1).broadcast_to([P, TOPK, NT]),
                                          tqf[:, pick].unsqueeze(2).broadcast_to([P, TOPK, NT]), ALU.is_equal))
                    link(ve.tensor_tensor(bm[:, :, NT:2 * NT], bm[:, :, 0:NT], wtop[:, i, :].unsqueeze(2).broadcast_to([P, TOPK, NT]), ALU.mult))
                    ve.tensor_scalar(bm[:, :, 0:NT], bm[:, :, 0:NT], tokid[:, i:i + 1], None, ALU.mult).then_inc(s.ab_ready, 1)
                half = NT // 2
                for q in range(2):
                    sl = sl4[:, 0:half * E].rearrange("p (t e) -> p t e", e=E)
                    link(ve.scalar_tensor_tensor(out=sl, in0=iota[:, q * half:(q + 1) * half].unsqueeze(2).broadcast_to([P, half, E]),
                                                 scalar=float(P), in1=enda[:, 0:E].unsqueeze(1).broadcast_to([P, half, E]),
                                                 op0=ALU.mult, op1=ALU.is_ge))
                    link(ve.tensor_reduce(texf[:, q * half:(q + 1) * half], sl, AX.X, ALU.add))
                link(ve.tensor_scalar(texf[:, 0:NT], texf[:, 0:NT], float(E - 1), None, ALU.min))
                link(ve.tensor_copy(texi[:, 0:NT], texf[:, 0:NT]))
                if s.n == 0:
                    link(ve.tensor_scalar(selc[:, :], texf[0:96, 0:NT], pmod[0:96, :], None, ALU.is_equal))
                ve.wait_ge(s.ab_used, NTT)
                link(ve.tensor_copy(gidx[:, 0:NT], ps[:, 2, 0:NT]))
                ve.tensor_copy(wtile[:, 0:NT], ps[:, 2, NT:2 * NT]).then_inc(s.idx_ready, 1)

            def tiles(s):
                F = s.F

                def gate(t, j):
                    ve.wait_ge(s.gu_done, t + 1)
                    g, u = ps[:, 2 + j % 2, 0:F], ps[:, 2 + j % 2, F:2 * F]
                    if s.n == 0:
                        ve.tensor_scalar(gbuf[:, j % 2, :], g, LIMIT, None, ALU.min).then_inc(s.g_ready, 1)
                        ve.tensor_scalar(ubuf[:, j % 2, :], u, LIMIT, -LIMIT, ALU.min, ALU.max).then_inc(s.u_ready, 1)
                        ve.wait_ge(s.u_ready, t + 1)
                        ve.scalar_tensor_tensor(out=ubuf[:, j % 2, :], in0=ubuf[:, j % 2, :], scalar=1.0, in1=gbuf[:, j % 2, :],
                                                op0=ALU.add, op1=ALU.mult).then_inc(s.h1_ready, 1)
                        ve.wait_ge(s.h1_ready, t + 1)
                        ve.wait_ge(s.sig_ready, t + 1)
                    else:
                        ve.wait_ge(s.sig_ready, t + 1)
                        ve.tensor_tensor(gbuf[:, j % 2, 0:F], sig[:, j % 2, 0:F], g, ALU.mult).then_inc(s.h1_ready, 1)
                        ve.wait_ge(s.h1_ready, t + 1)
                    if not isinstance(t, int) or t >= 2:
                        ve.wait_ge(s.hT_done, t - 1)
                    if s.n == 0:
                        ve.tensor_tensor(hbuf[:, j % 2, :], ubuf[:, j % 2, :], sig[:, j % 2, :], ALU.mult).then_inc(s.h_ready, 1)
                    else:
                        ve.tensor_tensor(hbuf[:, j % 2, 0:F], gbuf[:, j % 2, 0:F], u, ALU.mult).then_inc(s.h_ready, 1)

                def turned(t, j):
                    ve.wait_ge(s.hT_done, t + 1)
                    if not isinstance(t, int) or t >= 2:
                        ve.wait_ge(s.y_done, t - 1)
                    ve.tensor_copy(hT[0:s.FP, j % 2, 0:s.KF, :],
                                   ps[0:s.FP, 4 + j % 2, 0:s.KF * P].rearrange("p (k t) -> p k t", t=P)).then_inc(s.hT_ready, 1)

                run_tiles(ve, s, (None, gate, turned, None))

            ve.memset(ones_bf[:, :], 1.0).then_inc(s_cbf, 1)
            link(ve.memset(ones_e[:, :], 1.0))
            ve.wait_ge(s_cst, 16)
            for dst, c in ((ident_bf, C_ID), (mask_bf, C_MASK), (tri_bf, C_TRI)):
                ve.tensor_copy(dst[:, :], cst[:, c:c + P]).then_inc(s_cbf, 1)
            ve.wait_ge(s_x, 16)
            ve.wait_ge(s_wr, 32)
            normalise(L[0])
            route(L[0])
            tiles(L[0])

            def smallest(h, j):
                ve.wait_ge(s_sc, h + 1)
                for tt, cols in ((0, slice(0, P)), (1, slice(P, 3 * P))):
                    ve.tensor_reduce(mxs[:, j % 4, tt:tt + 1], ps[:, 1 + j % 2, cols], AX.X, ALU.min).then_inc(s_mx, 1)

            def probs_turned(h, j):
                ve.wait_ge(s_pT, h + 1)
                ve.tensor_copy(prT[:, j % 2, :], ps[:, 3 + j % 2, 0:3 * P]).then_inc(s_pTr, 1)

            def attended(n, j):
                ve.wait_ge(s_pv, n + 2)
                ve.tensor_copy(otb, ps[:, 5 + j, :]).then_inc(s_otr, 1)

            def scale_rows(n, j):
                ve.wait_ge(s_oa, n + 1)
                o = ps[:, 7, :].rearrange("p (t h d) -> p t h d", t=2, d=32)
                ve.reciprocal(rec[:, :, :], o[:, :, :, DH]).then_inc(s_rec, 1)
                ve.wait_ge(s_rec, n + 1)
                ve.tensor_tensor(ost.rearrange("p t (h d) -> p t h d", d=DH), o[:, :, :, 0:DH],
                                 rec[:, :, :].unsqueeze(3).broadcast_to([P, 2, HALF, DH]), ALU.mult).then_inc(s_on, 1)

            def gate0(b, j):
                ve.wait_ge(s_fe, b + 1)
                ve.scalar_tensor_tensor(out=fsil, in0=ftanh, scalar=1.0, in1=fsum, op0=ALU.add, op1=ALU.mult).then_inc(s_sil, 1)

            def residual(b, j):
                ve.wait_ge(s_sil, b + 1)
                ve.wait_ge(s_wo, b + 1)
                ve.scalar_tensor_tensor(out=fsil, in0=fsil, scalar=0.5, in1=ps[:, 7, :].rearrange("p (t n) -> p t n", t=2),
                                        op0=ALU.mult, op1=ALU.mult).then_inc(s_s, 1)
                ve.wait_ge(s_s, b + 1)
                rows = xr[:, bass.ds(b * 2, 2), :]
                ve.tensor_tensor(rows, rows, fsil, ALU.add).then_inc(s_x1, 1)

            run_heads(ve, [(-2, 1, smallest), (0, 1, probs_turned), (HALF, HALF, attended), (10, HALF, scale_rows),
                           (19, HEADS, gate0), (22, HEADS, residual)])
            ve.wait_ge(s_x1, BATCH)
            normalise(L[1])
            route(L[1])
            tiles(L[1])

            def table(lo):
                return b768_sb[:, lo:lo + D].unsqueeze(1).broadcast_to([P, NTT, D])

            ve.wait_ge(L[1].qkv_read, NTT)
            ve.wait_ge(s_small1, 48)
            ve.tensor_tensor(v1r, v1r, table(D), ALU.add).then_inc(s_z, 1)
            ve.tensor_tensor(u1r, u1r, table(2 * D), ALU.add).then_inc(s_z, 1)
            ve.tensor_tensor(q1r, q1r, table(0), ALU.add).then_inc(s_z, 1)
            ve.wait_ge(s_z, 3)
            ve.wait_ge(s_e, 1)
            ve.tensor_tensor(v1r, v1r, rowtmp[:, 0, :, :], ALU.mult).then_inc(s_row1, 1)
            ve.wait_ge(s_e, 2)
            link(ve.tensor_tensor(u1r, u1r, rowtmp[:, 1, :, :], ALU.mult))

            def shared(h, m):
                n = 4 * h + m
                ve.wait_ge(s_shsig, n + 1)
                if h == 1 and m == 0:
                    ve.wait_ge(s_sdn, 4)
                link(ve.tensor_tensor(shs[:, n % 2, :], shs[:, n % 2, :], ps[:, n % 2, :], ALU.mult))
                ve.tensor_tensor(shg[:, m, :], shs[:, n % 2, :], ps[:, 2 + n % 2, :], ALU.mult).then_inc(s_shr, 1)

            for h in range(2):
                for m in range(4):
                    shared(h, m)
            ve.wait_ge(s_e, 3)
            link(ve.tensor_scalar(rowtmp[:, 0, :, :], rowtmp[:, 0, :, :], 1.0, -1.0, ALU.min, ALU.add))
            ve.scalar_tensor_tensor(out=q1r, in0=q1r, scalar=0.0, in1=rowtmp[:, 0, :, :], op0=ALU.max, op1=ALU.add)\
              .then_inc(s_row1, 1)

            def stats(i):
                ve.wait_ge(s_o1, i + 1)
                ve.wait_ge(s_a1, i + 1)
                ve.bn_stats(bnst[:, i, :], ps[:, 2 + i % 2, 0:D]).then_inc(s_bn1, 1)

            for j in (2, 3):
                ve.wait_ge(L[1].y_stored[j], 4 * NT1)
            for b in range(BATCH):
                ve.wait_ge(s_kv, b + 1)
                if b >= 2:
                    ve.wait_ge(s_o1, 2 * b - 2)
                ve.tensor_tensor(kvb[:, b % 2, :, :], ps[:, 6 + b % 2, 0:D].rearrange("p (g n) -> p g n", g=2),
                                 bdiag.unsqueeze(1).broadcast_to([P, 2, P]), ALU.mult).then_inc(s_kvr, 1)
                stats(2 * b)
                stats(2 * b + 1)
            ve.wait_ge(s_bn1, NTT)
            for i in range(NTT):
                ins = ve.bn_aggr(mv[:, i, :], bnst[:, i, :])
            link(ins)
            ve.tensor_scalar(sd[:, :], mv[:, :, 1], EPS, None, ALU.add).then_inc(s_ln1, 1)
            ve.wait_ge(s_sd1, 1)
            link(ve.reciprocal(rstd[:, :], sd[:, :]))
            for i in range(NTT):
                link(ve.tensor_scalar(a1r[:, i, :], a1r[:, i, :], mv[:, i, 0:1], rstd[:, i:i + 1], ALU.subtract, ALU.mult))
                link(ve.tensor_tensor(a1r[:, i, :], a1r[:, i, :], lng_sb, ALU.mult))
                link(ve.tensor_tensor(a1r[:, i, :], a1r[:, i, :], lnb_sb[:, :], ALU.add))
                ve.tensor_tensor(a1r[:, i, :], a1r[:, i, :], u1r[:, i, :], ALU.mult).then_inc(s_a1n, 1)
                if i >= 2:
                    ve.wait_ge(s_wo1, i - 1)
                    ve.tensor_tensor(s1r[:, i - 2, :], ps[:, 6 + i % 2, 0:D], bo1_sb, ALU.add).then_inc(s_s1, 1)
            for i in (NTT - 2, NTT - 1):
                ve.wait_ge(s_wo1, i + 1)
                ve.tensor_tensor(s1r[:, i, :], ps[:, 6 + i % 2, 0:D], bo1_sb, ALU.add).then_inc(s_s1, 1)
            ve.wait_ge(s_s1, NTT)
            ve.wait_ge(s_shrow, NTT)
            for i in range(NTT):
                j = i % 2
                ve.wait_ge(L[1].cg_full[j], 64 * (i // 2 + 1))
                ve.tensor_tensor(csum.rearrange("p (k n) -> p k n", k=2), cg[:, j, 0:2, :], cg[:, j, 2:4, :], ALU.add)\
                  .then_inc(L[1].cg_read, 1)
                ve.wait_ge(L[1].cg_read, i + 1)
                link(ve.tensor_tensor(fbuf[:, j, :], csum[:, 0:D], csum[:, D:2 * D], ALU.add))
                link(ve.tensor_tensor(fbuf[:, j, :], fbuf[:, j, :], sh1r[:, i, :], ALU.add, ))
                ve.engine_nop().then_inc(L[1].f_ready, 1)
                link(ve.tensor_tensor(s1r[:, i, :], s1r[:, i, :], fbuf[:, j, :], ALU.mult))
                ve.wait_ge(L[1].fsig_ready, i + 1)
                link(ve.tensor_tensor(s1r[:, i, :], s1r[:, i, :], fsig[:, j, :], ALU.mult))
                ve.tensor_tensor(xr[:, i, :], xr[:, i, :], s1r[:, i, :], ALU.add).then_inc(L[1].g_done, 1)


def kernel(**inputs):
    import numpy as np
    import concourse.bacc as bacc
    from concourse.bass_utils import run_bass_kernel_spmd

    a = {k: np.asarray(v) for k, v in inputs.items()}

    def rows(w):
        return np.ascontiguousarray(w.reshape(-1, P, w.shape[-1]).transpose(1, 0, 2))

    def experts(w):
        e, h, n = w.shape
        p = min(h, P)
        return np.ascontiguousarray(w.reshape(e, h // p, p, n).transpose(2, 0, 1, 3).reshape(p, e, -1))

    def apart(w):
        return np.concatenate([w[..., ::2], w[..., 1::2]], axis=-1)

    arrays = dict(
        x=a["L0_attn_x"].reshape(TOK, D),
        consts=constants(),
        wqkv0=rows(np.concatenate([a["L0_attn_Wq"].T, a["L0_attn_Wk"].T, a["L0_attn_Wv"].T], axis=1)),
        wo0=rows(a["L0_attn_Wo"].T),
        wr0=rows(a["L0_ffn_router_weight"].T),
        rb0=a["L0_ffn_router_bias"].reshape(1, E0),
        gub0=apart(a["L0_ffn_gate_up_proj_bias"]),
        dnb0=a["L0_ffn_down_proj_bias"],
        gu0=experts(apart(a["L0_ffn_gate_up_proj"])),
        dn0=experts(a["L0_ffn_down_proj"]),
        wqvu1=rows(np.concatenate([a["L1_attn_Wqk"], a["L1_attn_Wv"], a["L1_attn_Wu"]], axis=1)),
        b768=np.concatenate([a["L1_attn_bqk"], a["L1_attn_bv"], a["L1_attn_bu"]]).reshape(1, 3 * D),
        wo1=rows(a["L1_attn_Wo"]),
        lnrow=np.stack([a["L1_attn_ln_g"], a["L1_attn_ln_b"]]),
        bo1=a["L1_attn_bo"].reshape(1, D),
        wr1=rows(a["L1_ffn_router_w"]),
        gu1=experts(np.concatenate([a["L1_ffn_w_gate"], a["L1_ffn_w_up"]], axis=-1)),
        dn1=experts(a["L1_ffn_w_down"]),
        wsgu=rows(np.concatenate([a["L1_ffn_ws_gate"], a["L1_ffn_ws_up"]], axis=1)),
        wsdn=rows(a["L1_ffn_ws_down"]),
    )
    arrays = {k: np.ascontiguousarray(v) for k, v in arrays.items()}
    nc = bacc.Bacc("TRN2", target_bir_lowering=False, num_devices=1)
    args = [nc.dram_tensor("in_" + k, v.shape, mybir.dt.from_np(v.dtype), kind="ExternalInput").ap() for k, v in arrays.items()]
    args.append(nc.dram_tensor("out", (TOK, D), mybir.dt.float32, kind="ExternalOutput").ap())
    build_program(nc, *args)
    r = run_bass_kernel_spmd(nc, [{"in_" + k: v for k, v in arrays.items()}], core_ids=[0])
    return r.results[0]["out"].reshape(BATCH, SEQ, D)
```

```python
import concourse.bass as bass
from concourse import mybir
from contextlib import ExitStack

P = 128
D = 256
KD = D // P
TOK = 1024
NTT = TOK // P
TOPK = 4
HEADS, DH = 16, 16
BATCH, SEQ = 4, 256
HALF = 8
MASKED = 1.0e30

E0, F0 = 16, 256
E1, F1 = 32, 96
SH = 512
LIMIT, ALPHA = 7.0, 1.702
EPS = 1e-5


def tiles_needed(experts):
    return TOK * TOPK // P + experts - 1


NT0, NT1 = tiles_needed(E0), tiles_needed(E1)

C_ID, C_IOTA, C_TOK, C_MASK, C_TRI, C_BD, C_COS, C_SIN, C_PMOD, C_END = (
    0, 128, 256, 264, 392, 520, 648, 712, 776, 777)


def constants():
    import numpy as np
    c = np.zeros((P, C_END), np.float32)
    p, f = np.arange(P)[:, None], np.arange(P)[None, :]
    c[:, C_ID:C_ID + P] = p == f
    c[:, C_IOTA:C_IOTA + P] = f
    c[:, C_TOK:C_TOK + NTT] = p + P * np.arange(NTT)[None, :]
    c[:, C_MASK:C_MASK + P] = np.where(f > p, MASKED, 0.0)
    c[:, C_TRI:C_TRI + P] = p < f
    c[:, C_BD:C_BD + P] = p // DH == f // DH
    half = DH // 2
    freq = (np.float32(1.0) / np.float32(10000.0) ** (np.arange(half, dtype=np.float32) / np.float32(half))).astype(np.float32)
    for t in range(SEQ // P):
        ang = ((p + t * P).astype(np.float32) * freq[None, :]).astype(np.float32)
        co, si = np.cos(ang), np.sin(ang)
        for w, scale in ((0, -np.float32(DH) ** -0.5), (1, 1.0)):
            at = 2 * DH * t + DH * w
            c[:, C_COS + at:C_COS + at + DH] = np.concatenate([co, co], axis=1) * np.float32(scale)
            c[:, C_SIN + at:C_SIN + at + DH] = np.concatenate([-si, si], axis=1) * np.float32(scale)
    c[:, C_PMOD:C_PMOD + 1] = p % 32
    return c


def build_program(nc, x, consts, wqkv0, wo0, wr0, rb0, gub0, dnb0, gu0, dn0,
                  wqvu1, b768, wo1, lnrow, bo1, wr1, gu1, dn1, wsgu, wsdn, out):
    f32, f32r, bf16, i32, u32 = mybir.dt.float32, mybir.dt.float32r, mybir.dt.bfloat16, mybir.dt.int32, mybir.dt.uint32
    ALU, ACT, AX = mybir.AluOpType, mybir.ActivationFunctionType, mybir.AxisListType
    ctx = ExitStack()
    with ctx:
        def sb(name, shape, dt=f32):
            return ctx.enter_context(nc.sbuf_tensor(name, shape, dt))

        def sem(name):
            return ctx.enter_context(nc.semaphore(name))

        xn_dram = [nc.dram_tensor(f"xn_rows{n}", (TOK, D), f32, kind="Internal").ap() for n in (0, 1)]
        ys_dram = [nc.dram_tensor(f"sorted_rows{n}", (nt * P, D), f32, kind="Internal").ap()
                   for n, nt in ((0, NT0), (1, NT1))]

        cst = sb("cst", [P, C_END])
        ident = cst[:, C_ID:C_ID + P]
        iota = cst[:, C_IOTA:C_IOTA + P]
        tokid = cst[:, C_TOK:C_TOK + NTT]
        bdiag = cst[:, C_BD:C_BD + P]
        pmod = cst[:, C_PMOD:C_PMOD + 1]
        ident_bf = sb("ident_bf", [P, P], bf16)
        mask_bf = sb("mask_bf", [P, P], bf16)
        tri_bf = sb("tri_bf", [P, P], bf16)
        ones_bf = sb("ones_bf", [P, P], bf16)
        ones_e = sb("ones_e", [P, E1])

        big = sb("experts", [P, E0 * KD * 2 * F0 + E0 * KD * D])
        GU0 = E0 * KD * 2 * F0
        GU1 = E1 * KD * 2 * F1
        gu0_sb, dn0_sb = big[:, 0:GU0], big[:, GU0:]
        gu1_sb, dn1_sb = big[:, 0:GU1], big[0:F1, GU0:]
        wsgu_sb = big[:, GU1:GU1 + KD * 2 * SH].rearrange("p (k n) -> p k n", k=KD)
        off = GU1 + KD * 2 * SH
        wsdn_sb = big[:, off:off + 4 * D].rearrange("p (k n) -> p k n", k=4)
        off += 4 * D
        wo1_sb = big[:, off:off + KD * D].rearrange("p (k n) -> p k n", k=KD)
        off += KD * D
        lng_sb, bo1_sb = big[:, off:off + D], big[:, off + D:off + 2 * D]
        assert off + 2 * D <= GU0
        wqkv_sb = sb("wqkv", [P, KD, 3 * D])
        wo0_sb = sb("wo0", [P, KD, D])
        b768_sb = sb("b768", [P, 3 * D])
        lnb_sb = sb("lnb", [P, D])
        wr0_sb = sb("wr0", [P, KD, E0])
        wr1_sb = sb("wr1", [P, KD, E1])
        rb0_sb = sb("rb0", [P, E0])
        gub_bf = sb("gub_bf", [96, 2 * F0], bf16)
        dnb_bf = sb("dnb_bf", [96, D], bf16)

        xr = sb("xr", [P, NTT, D])
        xn = sb("xn", [P, NTT, D])

        att = sb("att", [P, 8192])
        til = sb("til", [P, 5120])
        qk_raw = att[:, 0:4096].rearrange("p (t n) -> p t n", t=NTT)
        v_rows = att[:, 4096:6144].rearrange("p (t n) -> p t n", t=NTT)
        xnT0 = att[:, 6144:8192].rearrange("p (k t) -> p k t", k=KD)
        parts = [a.rearrange("p (t w h n) -> p t w h n", t=2, w=2, h=HALF) for a in (att[:, 6144:8192], til[:, 0:2048])]
        ost = xn[:, 6:7, :].rearrange("p o (t n) -> p (o t) n", t=2)
        q1r, v1r, u1r = (att[:, 2048 * n:2048 * (n + 1)].rearrange("p (t n) -> p t n", t=NTT)
                         for n in range(3))
        kvb = til[:, 0:512].rearrange("p (s g n) -> p s g n", s=2, g=2)
        xnT1 = att[:, 6144:8192].rearrange("p (k t) -> p k t", k=KD)
        rows1 = att[:, 0:6144].rearrange("p (w t n) -> p w t n", w=3, t=NTT)
        rowsig = xn[:, 0:2, :]
        q1T = xn[:, :, :].rearrange("p t n -> p (t n)").rearrange("p (g t) -> p g t", g=2)

        xg = til[:, 0:1024].rearrange("p (s n) -> p s n", s=4)
        xgT = til[:, 1024:1536].rearrange("p (s k t) -> p s k t", s=2, k=KD)
        gbuf = til[:, 1536:2048].rearrange("p (s n) -> p s n", s=2)
        ubuf = til[:, 2048:2560].rearrange("p (s n) -> p s n", s=2)
        sig = til[:, 2560:3072].rearrange("p (s n) -> p s n", s=2)
        hbuf = til[:, 3072:3584].rearrange("p (s n) -> p s n", s=2)
        hT = til[:, 3584:4096].rearrange("p (s k t) -> p s k t", s=2, k=KD)
        ybuf = til[:, 4096:5120].rearrange("p (s n) -> p s n", s=4)
        pr = til[:, 2048:2816].rearrange("p (s n) -> p s n", s=2)
        prT = til[:, 2816:3584].rearrange("p (s n) -> p s n", s=2)
        otb = til[:, 3584:4096]
        oTs = xn[:, 4:6, :]
        fsum = til[:, 4608:5120].rearrange("p (t n) -> p t n", t=2)
        ftanh = xn[:, 0:2, :]
        fsil = xn[:, 2:4, :]
        shg = big[:, 6144:10240].rearrange("p (h m t) -> p h m t", h=2, m=4)
        shs = til[:, 2048:3072].rearrange("p (s t) -> p s t", s=2)
        a1T = til[:, 3072:3584].rearrange("p (s k t) -> p s k t", s=2, k=KD)
        fbuf = til[:, 3584:4096].rearrange("p (s n) -> p s n", s=2)
        fsig = til[:, 512:1024].rearrange("p (s n) -> p s n", s=2)

        rou = sb("rou", [P, 3584])
        oh = rou[:, 0:512].bitcast(bf16)
        sl4 = rou[:, 512:1536]
        eq4 = sl4.rearrange("p (s k n) -> p s k n", s=4, k=TOPK)
        amat = rou[:, 1536:3584].rearrange("p (s k n) -> p s k n", s=4, k=TOPK)
        bmat = til[:, 2048:4096].rearrange("p (s k n) -> p s k n", s=4, k=TOPK)
        cg = rou[:, 0:2048].rearrange("p (s k n) -> p s k n", s=2, k=TOPK)
        csum0 = til[:, 4096:4608]
        csum = rou[:, 2048:2560]
        vst = rou[:, 2048:3072].rearrange("p (s t h d) -> p s t h d", s=2, t=2, h=HALF)
        rtmp = rou[:, 3072:3584].rearrange("p (w h d) -> p w h d", w=2, d=DH)
        gub_f, dnb_f, bsp = til[0:96, 0:512], til[0:96, 512:768], til[0:96, 768:1024].bitcast(bf16)
        f1r = big[:, 0:2048].rearrange("p (t n) -> p t n", t=NTT)
        a1r = big[:, 2048:4096].rearrange("p (t n) -> p t n", t=NTT)
        qexp = big[:, 4096:6144].rearrange("p (t n) -> p t n", t=NTT)

        bnst = sb("bnst", [P, NTT, 6])
        mv = sb("mv", [P, NTT, 2])
        sd = sb("sd", [P, NTT])
        rstd = sb("rstd", [P, NTT])
        lgt = sb("lgt", [P, NTT * E1])
        top = sb("top", [P, NTT, 8])
        topi = sb("topi", [P, NTT, 8], u32)
        topf = sb("topf", [P, NTT, TOPK])
        wraw = sb("wraw", [P, NTT, TOPK])
        wsum = sb("wsum", [P, NTT])
        wtop = sb("wtop", [P, NTT, TOPK])
        mcnt = sb("mcnt", [P, NTT * E1], bf16)
        nti = sb("nti", [P, E1], i32)
        nts = sb("nts", [P, E1])
        enda = sb("enda", [P, E1])
        base = sb("base", [P, E1])
        slotf = sb("slotf", [P, NTT * TOPK])
        sloti = sb("sloti", [P, NTT * TOPK], i32)
        slotu = [sb(f"slotu{n}", [P, NTT * TOPK], u32) for n in (0, 1)]
        tq = sb("tq", [P, NTT * TOPK], i32)
        tqf = sb("tqf", [P, NTT * TOPK])
        smf = sb("smf", [P, NTT * TOPK])
        gidx = sb("gidx", [P, NT1], u32)
        wtile = sb("wtile", [P, NT1])
        texcol = sb("texcol", [P, 1])
        nmr = sb("nmr", [P, NTT])
        texi = sb("texi", [P, P], i32)
        selc = sb("selc", [96, NT0], bf16)
        idxs = sb("idxs", [P, 4], u32)
        idx4 = sb("idx4", [P, 2, TOPK], u32)
        stk = sb("stk", [P, 2, 2, SEQ])
        mxs = sb("mxs", [P, 4, 2])
        rec = sb("rec", [P, 2, HALF])

        ps = ctx.enter_context(nc.psum_tensor("ps", [P, 8, 512], f32))
        psf = ps[:, :, :].rearrange("p b n -> p (b n)")

        s_x = [sem(f"x_in{h}") for h in range(2)]
        s_cst, s_wr, s_bias, s_wqkv, s_wo0, s_w0, s_w1, s_wqvu1, s_small1, s_tab1 = map(sem, (
            "cst_in", "wr_in", "bias_in", "wqkv_in", "wo_in", "experts0_in", "experts1_in", "wqvu1_in",
            "small1_in", "tables1_in"))
        s_cbf = sem("casts_done")
        s_bsp = sem("bias_split_done")
        s_pool = sem("pool_chain")
        s_dve = sem("dve_chain")
        s_out = sem("out_stored")

        class Layer:

            def __init__(self, n):
                self.n, self.E, self.F, self.NT = n, (E0, E1)[n], (F0, F1)[n], (NT0, NT1)[n]
                self.KF, self.FP = -(-self.F // P), min(self.F, P)
                self.xnT = (xnT0, xnT1)[n]
                self.wr = (wr0_sb, wr1_sb)[n]
                self.ve_ready = sem(f"variances{n}")
                self.sd_ready = sem(f"deviations{n}")
                self.xn_ready = sem(f"xn_ready{n}")
                self.xn_stored = sem(f"xn_stored{n}")
                self.xT_done = sem(f"xnT_done{n}")
                self.xnT_ready = sem(f"xnT_ready{n}")
                self.qkv_done = sem(f"projected{n}")
                self.qkv_read = sem(f"projected_read{n}")
                self.logits_done = sem(f"logits_done{n}")
                self.wexp_in = sem(f"top_logits{n}")
                self.wexp_out = sem(f"top_exps{n}")
                self.m_ready = sem(f"choices{n}")
                self.rank_done = sem(f"ranks_done{n}")
                self.eq_ready = sem(f"onehots_equal{n}")
                self.ab_ready = sem(f"onehots_ready{n}")
                self.ab_used = sem(f"onehots_used{n}")
                self.idx_ready = sem(f"tile_lists_ready{n}")
                self.icol = sem(f"index_column{n}")
                self.xg_full = [sem(f"gathered{n}_{j}") for j in range(4)]
                self.xgT_done = sem(f"gathered_turned{n}")
                self.xgT_ready = sem(f"xgT_ready{n}")
                self.gu_done = sem(f"gate_up_done{n}")
                if n == 0:
                    self.g_ready = sem("gate_ready")
                    self.u_ready = sem("up_ready")
                self.sig_ready = sem(f"sigmoid_ready{n}")
                self.h1_ready = sem(f"half_gated{n}")
                self.h_ready = sem(f"hidden_ready{n}")
                self.hT_done = sem(f"hidden_turned{n}")
                self.hT_ready = sem(f"hT_ready{n}")
                self.y_done = sem(f"down_done{n}")
                self.y_ready = sem(f"weighted_ready{n}")
                self.y_stored = [sem(f"weighted_stored{n}_{j}") for j in range(4)]
                self.icol4 = sem(f"index_rows{n}")
                self.cg_full = [sem(f"four_rows{n}_{j}") for j in range(2)]
                if n == 1:
                    self.cg_read = sem("four_rows_read")
                    self.f_ready = sem("expert_sum_ready")
                    self.fsig_ready = sem("expert_sum_sigmoid")
                    self.g_done = sem("block_rows_ready")

        L = [Layer(0), Layer(1)]
        (s_rope, s_hl, s_hi, s_vst, s_stkT, s_stk, s_sc, s_mx, s_exp, s_pT, s_pTr, s_pTa, s_pv, s_otr, s_oa, s_rec, s_on,
         s_oT, s_oTr, s_wo, s_s, s_fp, s_f, s_fe, s_sil) = map(sem, (
            "rope_done", "parts_ready", "high_parts_ready", "v_columns_ready", "stack_turned",
            "stack_ready", "scores_done", "min_ready", "probs_ready", "probsT_done", "probsT_ready", "probsT_ready_act", "half_attended",
            "attnT_read", "attn_turned_back", "recip_ready", "attn_ready", "attnT_done", "attnT_ready",
            "wo_done", "s_read", "pair_sums", "expert_sum", "half_tanh", "gated"))
        s_x1 = sem("x1_ready")
        s_x1n = sem("x1_stats")
        s_nmr = sem("shift_ready")
        s_a1h = sem("a1_normalised")
        s_rst = sem("rope_steps")
        s_here = sem("waits_taken")
        s_bn1, s_a1n, s_rowm, s_qe, s_f1, s_gate1 = map(sem, (
            "stats1_ready", "a1_gated", "rows_gated", "q_exp", "routed_sum", "gate1_ready"))
        s_z, s_e, s_row1, s_qT1, s_qT1r, s_kv, s_kvr, s_o1, s_a1, s_a1T, s_a1Tr, s_wo1, s_s1, s_shd, s_shsig, s_shr, s_sdn = map(sem, (
            "z_ready", "zfun_ready", "rows1_ready", "q1T_done", "q1T_ready", "kv_done", "kv_ready", "o1_done",
            "a1_ready", "a1T_done", "a1T_ready", "wo1_done", "s1_ready",
            "shared_up_done", "shared_sig", "shared_ready", "shared_down_done"))

        def ge(eng, s, v):
            if not isinstance(v, int) or v > 0:
                eng.wait_ge(s, v)

        def run_steps(eng, total, body, first, rounds, stages):
            def step(u, g):
                for lag, every, work in stages:
                    v = u - lag
                    if v % every or (g is None and not 0 <= v < total):
                        continue
                    count = body // every
                    if g is None:
                        work(v // every, v // every % count)
                    else:
                        assert 0 <= v and v + body * (rounds - 1) < total
                        work(g * count + v // every, v // every % count)

            lags = [lag for lag, _, _ in stages]
            for u in range(min(lags), first):
                step(u, None)
            with eng.Fori(0, rounds) as g:
                for c in range(body):
                    step(first + c, g)
            for u in range(first + body * rounds, total + max(lags)):
                step(u, None)

        def run_tiles(eng, s, stages, rows=()):
            def slot4(work):
                return lambda t, j: work(t, j % 4)

            body = 8 if s.n else 4
            tile_stages = [(lag, every, slot4(work)) for lag, every, work in stages]
            run_steps(eng, s.NT, body, 8, (s.NT - 8) // body, tile_stages + (list(rows) if s.n else []))

        def run_heads(eng, stages):
            run_steps(eng, BATCH * HEADS, HEADS, 12, BATCH - 1, stages)

        MIXED = (("up", 0), ("up", 1), ("keys", 0), ("up", 2), ("keys", 1), ("queries", 0), ("up", 3), ("keys", 2),
                 ("queries", 1), ("up", 4), ("keys", 3), ("queries", 2), ("up", 5), ("queries", 3))

        block = ctx.enter_context(nc.Block())

        @block.sync
        def _(sp):
            x_rows = x.rearrange("(t p) d -> p t d", p=P)
            for h, t in enumerate((slice(0, 4), slice(4, 8))):
                sp.dma_start(xr[:, t, :], x_rows[:, t, :]).then_inc(s_x[h], 16)
            sp.dma_start(cst[:, :], consts).then_inc(s_cst, 16)
            sp.dma_start(wr0_sb[:, :, :], wr0).then_inc(s_wr, 16)
            sp.dma_start(rb0_sb[:, :], rb0.partition_broadcast(P)).then_inc(s_wr, 16)
            for j in range(3):
                sp.dma_start(gub_f[32 * j:32 * j + E0, :], gub0).then_inc(s_bias, 16)
                sp.dma_start(dnb_f[32 * j:32 * j + E0, :], dnb0).then_inc(s_bias, 16)
            sp.dma_start(wqkv_sb[:, :, :], wqkv0).then_inc(s_wqkv, 16)

            def load_experts0(c):
                e = slice(c * 4, c * 4 + 4)
                sp.dma_start(gu0_sb.rearrange("p (e n) -> p e n", e=E0)[:, e, :], gu0[:, e, :]).then_inc(s_w0, 16)
                sp.dma_start(dn0_sb.rearrange("p (e n) -> p e n", e=E0)[:, e, :], dn0[:, e, :]).then_inc(s_w0, 16)

            load_experts0(0)
            load_experts0(1)

            def store_xn(s):
                for i in range(NTT):
                    sp.wait_ge(s.xn_ready, i + 1)
                    sp.dma_start(xn_dram[s.n][i * P:(i + 1) * P, :], xn[:, i, :]).then_inc(s.xn_stored, 16)

            def store_tiles(s):
                rows = ys_dram[s.n].rearrange("(t p) d -> t p d", p=P)

                def store(t, j):
                    sp.wait_ge(s.y_ready, t + 1)
                    sp.dma_start(rows[t], ybuf[:, j, :]).then_inc(s.y_stored[j], 16)

                with sp.Fori(0, s.NT // 4) as g:
                    for j in range(4):
                        store(g * 4 + j, j)
                for t in range(s.NT // 4 * 4, s.NT):
                    store(t, t % 4)

            store_xn(L[0])
            load_experts0(2)
            load_experts0(3)
            sp.wait_ge(L[0].gu_done, 1)
            sp.dma_start(wo0_sb[:, :, :], wo0).then_inc(s_wo0, 16)
            sp.dma_start(wr1_sb[:, :, :], wr1).then_inc(s_small1, 16)
            sp.dma_start(b768_sb[:, :], b768.partition_broadcast(P)).then_inc(s_small1, 16)
            sp.dma_start(lnb_sb[:, :], lnrow[1:2, :].partition_broadcast(P)).then_inc(s_small1, 16)
            sp.wait_ge(L[0].qkv_done, NTT)
            sp.dma_start(wqkv_sb[:, :, :], wqvu1).then_inc(s_wqvu1, 16)
            store_tiles(L[0])
            sp.wait_ge(L[0].y_done, NT0)
            for c in range(8):
                sp.wait_ge(s_f, c + 3)
                e = slice(c * 4, c * 4 + 4)
                sp.dma_start(gu1_sb.rearrange("p (e n) -> p e n", e=E1)[:, e, :], gu1[:, e, :]).then_inc(s_w1, 16)
                sp.dma_start(dn1_sb.rearrange("p (e n) -> p e n", e=E1)[:, e, :], dn1[:, e, :]).then_inc(s_w1, 16)
            sp.dma_start(wsgu_sb, wsgu).then_inc(s_tab1, 16)
            sp.dma_start(wsdn_sb, wsdn).then_inc(s_tab1, 16)
            sp.dma_start(wo1_sb, wo1).then_inc(s_tab1, 16)
            sp.dma_start(lng_sb, lnrow[0:1, :].partition_broadcast(P)).then_inc(s_tab1, 16)
            sp.dma_start(bo1_sb, bo1.partition_broadcast(P)).then_inc(s_tab1, 16)
            store_xn(L[1])
            store_tiles(L[1])
            for i in range(NTT):
                sp.wait_ge(L[1].g_done, i + 1)
                sp.dma_start(out[i * P:(i + 1) * P, :], xr[:, i, :]).then_inc(s_out, 16)
            sp.wait_ge(s_out, 16 * NTT)

        @block.gpsimd
        def _(po):
            chain = [0]

            def link(ins):
                chain[0] += 1
                ins.then_inc(s_pool, 1)
                po.wait_ge(s_pool, chain[0])

            def here():
                po.sem_inc(s_here, 1)

            def onehots(s):
                for i in range(NTT):
                    po.wait_ge(s.eq_ready, i + 1)
                    eq = eq4[:, i % 4, :, 0:s.NT]
                    po.tensor_tensor(bmat[:, i % 4, :, s.NT:2 * s.NT], eq, wtop[:, i, :].unsqueeze(2).broadcast_to([P, TOPK, s.NT]), ALU.mult)
                    po.tensor_tensor(bmat[:, i % 4, :, 0:s.NT], eq, tokid[:, i:i + 1].unsqueeze(2).broadcast_to([P, TOPK, s.NT]), ALU.mult)\
                      .then_inc(s.ab_ready, 1)

            def gather_tiles(s):
                ge(po, s.xn_stored, 16 * NTT)
                po.wait_ge(s.idx_ready, 1)

                def one(t, j):
                    if not isinstance(t, int) or t >= 4:
                        po.wait_ge(s.xgT_done, t - 3)
                    po.tensor_copy(idxs[:, j:j + 1], gidx[:, bass.ds(t, 1)]).then_inc(s.icol, 1)
                    po.wait_ge(s.icol, t + 1)
                    here()
                    po.indirect_dma_start(xg[:, j, :], None, xn_dram[s.n],
                                          bass.IndirectOffsetOnAxis(ap=idxs[:, j:j + 1], axis=0))\
                      .then_inc(s.xg_full[j], 16)

                def four(g):
                    for j in range(4):
                        one(g * 4 + j, j)

                four(0)
                mixed = BATCH if s.n == 0 else 0
                if s.n == 0:
                    po.memset(vst[:, :, :, :, DH:DH + 1], 1.0)
                    po.memset(vst[:, :, :, :, DH + 1:], 0.0)
                    po.wait_ge(s.qkv_read, 2 * NTT)
                    here()
                    with po.Fori(0, mixed) as g:
                        four(g * 2 + 1)
                        rotate(g * 2, 0, g * 2)
                        four(g * 2 + 2)
                        rotate(g * 2 + 1, 1, g * 2 + 1)
                with po.Fori(0, s.NT // 4 - 1 - 2 * mixed) as g:
                    four(g + 1 + 2 * mixed)
                for t in range(s.NT // 4 * 4, s.NT):
                    one(t, t % 4)

            def rotate(i, tt, n):
                ct, st = (cst[:, c + 2 * DH * tt:c + 2 * DH * (tt + 1)].rearrange("p (w d) -> p w d", w=2) for c in (C_COS, C_SIN))
                raw = qk_raw[:, bass.ds(i, 1), :].rearrange("p o (w h d) -> p (o w) h d", w=2, d=DH)
                half = DH // 2

                def wide(a, lo, hi):
                    return a[:, :, lo:hi].unsqueeze(2).broadcast_to([P, 2, HEADS, hi - lo])

                po.tensor_tensor(rtmp[:, :, :, 0:half], raw[:, :, :, half:DH], wide(st, 0, half), ALU.mult).then_inc(s_rst, 1)
                po.tensor_tensor(rtmp[:, :, :, half:DH], raw[:, :, :, 0:half], wide(st, half, DH), ALU.mult).then_inc(s_rst, 1)
                po.wait_ge(s_rst, n * 3 + 2)
                here()
                po.tensor_tensor(raw, raw, wide(ct, 0, DH), ALU.mult).then_inc(s_rst, 1)
                po.wait_ge(s_rst, n * 3 + 3)
                here()
                po.tensor_tensor(raw, raw, rtmp[:, :, :, :], ALU.add).then_inc(s_rope, 1)
                po.wait_ge(s_rope, n + 1)
                here()

            def gather_back(s, i, j):
                po.tensor_copy(idx4[:, j, :], slotu[s.n][:, bass.ds(i * TOPK, TOPK)]).then_inc(s.icol4, 1)
                po.wait_ge(s.icol4, i + 1)
                here()
                for k in range(TOPK):
                    po.indirect_dma_start(cg[:, j, k, :], None, ys_dram[s.n],
                                          bass.IndirectOffsetOnAxis(ap=idx4[:, j, k:k + 1], axis=0))\
                      .then_inc(s.cg_full[j], 16)

            def tiles_stored(s):
                for j in range(4):
                    po.wait_ge(s.y_stored[j], 16 * ((s.NT - j + 3) // 4))

            link(po.memset(gub_bf[:, :], 0.0))
            link(po.memset(dnb_bf[:, :], 0.0))
            po.wait_ge(s_bias, 96)
            po.wait_ge(s_dve, 1)
            for full, part, n in ((gub_f, gub_bf, 2 * F0), (dnb_f, dnb_bf, D)):
                for j in range(3):
                    rows = slice(32 * j, 32 * j + E0)
                    for m in range(j):
                        link(po.tensor_tensor(bsp[rows, 0:n], full[rows, :], ones_e[rows, 0:1].broadcast_to([E0, n]), ALU.mult))
                        link(po.tensor_tensor(full[rows, :], full[rows, :], bsp[rows, 0:n], ALU.subtract))
                    link(po.tensor_tensor(part[rows, :], full[rows, :], ones_e[rows, 0:1].broadcast_to([E0, n]), ALU.mult))
            po.engine_nop().then_inc(s_bsp, 1)

            onehots(L[0])
            gather_tiles(L[0])

            def one(shape):
                a = ones_e[:, 0:1]
                for _ in shape[2:]:
                    a = a.unsqueeze(1)
                return a.broadcast_to(shape)

            def split(b, j):
                if not isinstance(b, int):
                    po.wait_ge(s_stkT, b * 8 + 4 * j - 4)
                    here()
                raw = [qk_raw[:, bass.ds(b * 2 + tt, 1), :].rearrange("p o (w h d) -> p (o w) h d", w=2, d=DH)
                       [:, :, HALF * j:HALF * (j + 1), :] for tt in range(2)]

                def places(tt, w, part):
                    a = parts[j][:, tt, w, :, :]
                    if w == 0:
                        return a.rearrange("p h (r c d) -> p h r c d", r=2, c=2)[:, :, :, part, :]
                    return a.rearrange("p h (c r d) -> p h c r d", r=2, c=2)[:, :, part, :, :]

                def twice(a):
                    return a.unsqueeze(2).broadcast_to([P, HALF, 2, DH])

                for tt in range(2):
                    for w in range(2):
                        po.tensor_tensor(places(tt, w, 0).bitcast(f32r), twice(raw[tt][:, w, :, :]), one([P, HALF, 2, DH]), ALU.mult)\
                          .then_inc(s_hi, 1)
                po.wait_ge(s_hi, b * 8 + 4 * j + 4)
                here()
                for tt in range(2):
                    for w in range(2):
                        ins = po.tensor_tensor(places(tt, w, 1).bitcast(f32r), twice(raw[tt][:, w, :, :]),
                                               places(tt, w, 0), ALU.subtract)
                ins.then_inc(s_hl, 1)

            def fetch(b, j):
                if not isinstance(b, int):
                    po.wait_ge(s_f, b * 2 + j + 1)
                po.tensor_copy(idx4[:, j, :], slotu[0][:, bass.ds(b * 2 * TOPK + j * TOPK, TOPK)]).then_inc(L[0].icol4, 1)
                po.wait_ge(L[0].icol4, b * 2 + j + 1)
                here()
                for k in range(TOPK):
                    po.indirect_dma_start(cg[:, j, k, :], None, ys_dram[0],
                                          bass.IndirectOffsetOnAxis(ap=idx4[:, j, k:k + 1], axis=0)).then_inc(L[0].cg_full[j], 16)

            split(0, 0)
            po.wait_ge(L[0].y_ready, NT0)
            split(0, 1)
            tiles_stored(L[0])
            with po.Fori(0, BATCH - 1) as b:
                fetch(b, 0)
                fetch(b, 1)
                split(b + 1, 0)
                split(b + 1, 1)
            po.wait_ge(s_f, 2 * BATCH)
            fetch(BATCH - 1, 0)
            fetch(BATCH - 1, 1)

            onehots(L[1])
            gather_tiles(L[1])
            tiles_stored(L[1])
            gather_back(L[1], 0, 0)
            for i in range(NTT):
                j = i % 2
                if i + 1 < NTT:
                    gather_back(L[1], i + 1, 1 - j)
                po.wait_ge(L[1].cg_full[j], 64 * (i // 2 + 1))
                po.tensor_tensor(csum.rearrange("p (k n) -> p k n", k=2), cg[:, j, 0:2, :], cg[:, j, 2:4, :], ALU.add)\
                  .then_inc(L[1].cg_read, 1)
                po.wait_ge(L[1].cg_read, i + 1)
                po.tensor_tensor(f1r[:, i, :], csum[:, 0:D], csum[:, D:2 * D], ALU.add).then_inc(s_f1, 1)
                po.wait_ge(s_f1, i + 1)

        @block.scalar
        def _(ac):
            ac.wait_ge(s_dve, 1)
            ac.activation(rstd[:, 0:1], ones_e[:, 0:1], ACT.Sqrt)

            def norm_and_turn(s):
                ac.wait_ge(s.ve_ready, 1)
                ac.activation(sd[:, :], sd[:, :], ACT.Sqrt).then_inc(s.sd_ready, 1)
                for i in range(NTT):
                    ac.wait_ge(s.xT_done, i + 1)
                    ac.activation(s.xnT[:, :, i * P:(i + 1) * P],
                                  ps[:, i % 2, 0:D].rearrange("p (k t) -> p k t", k=KD), ACT.Copy)\
                      .then_inc(s.xnT_ready, 1)

            def top_exp(s):
                ac.wait_ge(s.wexp_in, 1)
                ac.activation(wraw[:, :, :], wraw[:, :, :], ACT.Exp).then_inc(s.wexp_out, 1)

            def tiles(s):
                ac.wait_ge(s.idx_ready, 1)

                def turn(t, j):
                    ac.wait_ge(s.xgT_done, t + 1)
                    if not isinstance(t, int) or t >= 2:
                        ac.wait_ge(s.gu_done, t - 1)
                    ac.activation(xgT[:, j % 2, :, :], ps[:, j % 2, 0:D].rearrange("p (k t) -> p k t", k=KD), ACT.Copy)\
                      .then_inc(s.xgT_ready, 1)

                def gate(t, j):
                    if s.n == 0:
                        ac.wait_ge(s.g_ready, t + 1)
                        ac.activation(sig[:, j % 2, 0:s.F], gbuf[:, j % 2, :], ACT.Sigmoid, scale=ALPHA)\
                          .then_inc(s.sig_ready, 1)
                    else:
                        ac.wait_ge(s.gu_done, t + 1)
                        if not isinstance(t, int) or t >= 2:
                            ac.wait_ge(s.h_ready, t - 1)
                        ac.activation(sig[:, j % 2, 0:s.F], ps[:, 2 + j % 2, 0:s.F], ACT.Sigmoid)\
                          .then_inc(s.sig_ready, 1)

                def weigh(t, j):
                    ac.wait_ge(s.y_done, t + 1)
                    if not isinstance(t, int) or t >= 4:
                        ac.wait_ge(s.y_stored[j], (t - j) * 4)
                    ac.activation(ybuf[:, j, :], ps[:, 6 + j % 2, 0:D], ACT.Copy, scale=wtile[:, bass.ds(t, 1)])\
                      .then_inc(s.y_ready, 1)

                def row_sigmoid(i, j):
                    ac.wait_ge(s_z, i * 3 + 3)
                    if not isinstance(i, int) or i >= 1:
                        ac.wait_ge(s_rowm, i)
                    ac.activation(rowsig, rows1[:, 1:3, bass.ds(i, 1), :].rearrange("p w o n -> p (w o) n"), ACT.Sigmoid)\
                      .then_inc(s_e, 1)

                if s.n == 1:
                    ac.wait_ge(s.xn_stored, 16 * NTT)
                run_tiles(ac, s, [(0, 1, turn), (4, 1, weigh), (1, 1, gate)], [(3, 8, row_sigmoid)])

            norm_and_turn(L[0])
            def qkv0(i):
                ac.wait_ge(L[0].qkv_done, i + 1)
                b0 = 4 + 2 * (i % 2)
                ac.activation(qk_raw[:, i, :], ps[:, b0, :], ACT.Copy).then_inc(L[0].qkv_read, 1)
                ac.activation(v_rows[:, i, :], ps[:, b0 + 1, 0:D], ACT.Copy).then_inc(L[0].qkv_read, 1)

            qkv0(0)
            top_exp(L[0])
            for i in range(1, NTT):
                qkv0(i)
            tiles(L[0])

            def stack(n, j):
                ac.wait_ge(s_stkT, n + 1)
                ac.activation(stk[:, j % 2, :, :].bitcast(f32r), ps[:, 0, :].rearrange("p (w t) -> p w t", w=2), ACT.Copy)\
                  .then_inc(s_stk, 1)

            def probs(h, j):
                ac.wait_ge(s_mx, h * 2 + 2)
                if not isinstance(h, int) or h >= 2:
                    ac.wait_ge(s_pT, h - 1)
                for tt, cols in ((0, slice(0, P)), (1, slice(P, 3 * P))):
                    ins = ac.activation(pr[:, j % 2, cols], ps[:, 1 + j % 2, cols], ACT.Exp,
                                        bias=mxs[:, j % 4, tt:tt + 1], scale=-1.0)
                ins.then_inc(s_exp, 1)

            def values(half):
                def work(b, j):
                    if not isinstance(b, int) or b > 0:
                        ac.wait_ge(s_pv, b * 2 + half)
                    ac.activation(vst[:, half, :, :, 0:DH], v_rows[:, bass.ds(b * 2, 2), HALF * DH * half:HALF * DH * (half + 1)]
                                  .rearrange("p t (h d) -> p t h d", d=DH), ACT.Copy).then_inc(s_vst, 1)
                return work

            def probs_turned_act(n, j):
                ac.wait_ge(s_pT, n * 4 + 4)
                ac.activation(prT[:, 1, :], ps[:, 4, 0:3 * P], ACT.Copy).then_inc(s_pTa, 1)

            def attended(n, j):
                ac.wait_ge(s_pv, n + 2)
                ac.activation(otb, ps[:, 5 + j, :], ACT.Copy).then_inc(s_otr, 1)

            def turned0(n, j):
                ac.wait_ge(s_oT, n + 1)
                ac.activation(oTs[:, j, :], ps[:, 7, 0:SEQ], ACT.Copy).then_inc(s_oTr, 1)

            def gate_tanh(b, j):
                ac.wait_ge(s_f, b * 2 + 4)
                ac.activation(ftanh, fsum, ACT.Tanh, scale=0.5).then_inc(s_fe, 1)

            run_heads(ac, [(-4, 2, stack), (-4, HEADS, values(0)), (4, HEADS, values(1)), (3, 4, probs_turned_act),
                           (-2, 1, probs), (HALF, HALF, attended), (12, HALF, turned0), (18, HEADS, gate_tanh)])

            norm_and_turn(L[1])

            def qvu1(i):
                ac.wait_ge(L[1].qkv_done, i + 1)
                b0 = 4 + 2 * (i % 2)
                ac.activation(att[:, 0:6144].rearrange("p (w t n) -> p w t n", w=3, t=NTT)[:, :, i, :],
                              psf[:, b0 * 512:b0 * 512 + 3 * D].rearrange("p (w n) -> p w n", w=3), ACT.Copy)\
                  .then_inc(L[1].qkv_read, 1)

            qvu1(0)
            top_exp(L[1])
            for i in range(1, NTT):
                qvu1(i)
            tiles(L[1])
            ac.wait_ge(s_z, 3 * NTT)
            for b in range(BATCH):
                ac.activation(qexp[:, 2 * b:2 * b + 2, :], q1r[:, 2 * b:2 * b + 2, :], ACT.Exp).then_inc(s_qe, 1)

            def shared(n):
                ac.wait_ge(s_shd, n + 1)
                if n >= 2:
                    ac.wait_ge(s_shr, n - 1)
                ac.activation(shs[:, n % 2, :], ps[:, n % 2, :], ACT.Sigmoid).then_inc(s_shsig, 1)

            for what, n in MIXED:
                if what == "up":
                    shared(n)
                elif what == "keys":
                    ac.wait_ge(s_qT1, n + 1)
                    ac.activation(q1T[:, :, n * SEQ:(n + 1) * SEQ], ps[:, 4 + n % 2, :].rearrange("p (g t) -> p g t", g=2), ACT.Copy)\
                      .then_inc(s_qT1r, 1)
                else:
                    ac.wait_ge(s_o1, n + 1)
                    ac.activation(a1r[:, 2 * n:2 * n + 2, :], ps[:, 6 + n % 2, :].rearrange("p (t n) -> p t n", t=2), ACT.Copy)\
                      .then_inc(s_a1, 1)
            ac.wait_ge(L[1].ve_ready, 2)
            ac.activation(sd[:, :], sd[:, :], ACT.Sqrt).then_inc(L[1].sd_ready, 1)
            shared(6)
            ac.wait_ge(s_nmr, 1)
            for i in range(NTT):
                ac.activation(a1r[:, i, :], a1r[:, i, :], ACT.Identity, bias=nmr[:, i:i + 1], scale=rstd[:, i:i + 1])\
                  .then_inc(s_a1h, 1)
                if i == 1:
                    shared(7)
            for i in range(NTT):
                ac.wait_ge(s_a1T, i + 1)
                if i >= 2:
                    ac.wait_ge(s_wo1, i - 1)
                ac.activation(a1T[:, i % 2, :, :], ps[:, 6 + i % 2, 0:D].rearrange("p (k t) -> p k t", k=KD), ACT.Copy)\
                  .then_inc(s_a1Tr, 1)
                ac.wait_ge(L[1].f_ready, i + 1)
                if i >= 2:
                    ac.wait_ge(s_gate1, i - 1)
                ac.activation(fsig[:, i % 2, :], f1r[:, i, :], ACT.Sigmoid).then_inc(L[1].fsig_ready, 1)

        @block.tensor
        def _(pe):
            now = [pe.alloc_register(f"expert_now{j}") for j in range(4)]
            before = [pe.alloc_register(f"expert_before{j}") for j in range(4)]

            def turn_and_route(s):
                pe.wait_ge(s_cst, 16)
                pe.wait_ge(s_wr if s.n == 0 else s_small1, 32 if s.n == 0 else 48)
                for i in range(NTT + 1):
                    if i < NTT:
                        pe.wait_ge(s.xn_ready, i + 1)
                        if i >= 2:
                            pe.wait_ge(s.xnT_ready, i - 1)
                        for k in range(KD):
                            mm = pe.transpose(ps[:, i % 2, k * P:(k + 1) * P], xn[:, i, k * P:(k + 1) * P], ident)
                        mm.then_inc(s.xT_done, 1)
                    if i >= 1:
                        pe.wait_ge(s.xnT_ready, i)
                        for k in range(KD):
                            mm = pe.matmul(ps[:, 2, (i - 1) * s.E:i * s.E], s.xnT[:, k, (i - 1) * P:i * P],
                                           s.wr[:, k, :], start=(k == 0), stop=(k == KD - 1))
                mm.then_inc(s.logits_done, 1)

            def project(s, i):
                if i == 0:
                    if s.n == 0:
                        pe.wait_ge(s_wqkv, 16)
                    else:
                        pe.wait_ge(s_wqvu1, 16)
                if i >= 2:
                    pe.wait_ge(s.qkv_read, (i - 1) * (2 if s.n == 0 else 1))
                b0 = 4 + 2 * (i % 2)
                for n0, n1 in ((0, 512), (512, 768)):
                    for k in range(KD):
                        mm = pe.matmul(psf[:, b0 * 512 + n0:b0 * 512 + n1], s.xnT[:, k, i * P:(i + 1) * P],
                                       wqkv_sb[:, k, n0:n1], start=(k == 0), stop=(k == KD - 1))
                mm.then_inc(s.qkv_done, 1)

            def rank(s):
                pe.wait_ge(s.m_ready, 1)
                pe.wait_ge(s_cbf, 4)
                cnt = mcnt[:, 0:NTT * s.E].rearrange("p (t e) -> p t e", e=s.E)
                out3 = ps[:, 3, 0:NTT * s.E].rearrange("p (t e) -> p t e", e=s.E)
                pe.matmul(out3, tri_bf[:, :], cnt, start=True, stop=False)
                for j in range(NTT - 1):
                    n = NTT - 1 - j
                    pe.matmul(out3[:, j + 1:NTT, :], ones_bf[:, :], cnt[:, j, :].unsqueeze(1).broadcast_to([P, n, s.E]),
                              start=False, stop=(j == NTT - 2))
                for j in range(NTT):
                    mm = pe.matmul(ps[:, 3, 256:256 + s.E], ones_bf[:, :], cnt[:, j, :], start=(j == 0), stop=(j == NTT - 1))
                mm.then_inc(s.rank_done, 1)

            def tile_experts(s):
                pe.wait_ge(s.m_ready, 2)
                pe.matmul(ps[:, 3, 384:384 + P], texcol[:, :].broadcast_to([P, P]), ident, start=True, stop=True).then_inc(s.rank_done, 1)

            def place(s, i):
                pe.wait_ge(s.ab_ready, i + 1)
                for k in range(TOPK):
                    mm = pe.matmul(ps[:, 2, 0:2 * s.NT], amat[:, i % 4, k, :], bmat[:, i % 4, k, 0:2 * s.NT],
                                   start=(i == 0 and k == 0), stop=(i == NTT - 1 and k == TOPK - 1))
                mm.then_inc(s.ab_used, 1)

            def tiles(s):
                pe.wait_ge(s.idx_ready, 1)
                if s.n == 0:
                    pe.wait_ge(s_w0, 128)
                    pe.wait_ge(s_bsp, 1)
                else:
                    pe.wait_ge(s_w1, 256)
                    pe.wait_ge(s_tab1, 80)
                gu, dn = ((gu0_sb, dn0_sb), (gu1_sb, dn1_sb))[s.n]

                def experts(g, j):
                    if not isinstance(g, int) or g > 0:
                        for a, b in zip(before, now):
                            pe.reg_mov(a, b)
                    pe.load(now, texi[0:1, bass.ds(g * 4, 4)])

                def turn(t, j):
                    pe.wait_ge(s.xg_full[j], (t + (4 - j)) * 4)
                    if not isinstance(t, int) or t >= 2:
                        pe.wait_ge(s.xgT_ready, t - 1)
                    for k in range(KD):
                        mm = pe.transpose(ps[:, j % 2, k * P:(k + 1) * P], xg[:, j, k * P:(k + 1) * P], ident)
                    mm.then_inc(s.xgT_done, 1)

                def up(t, j):
                    e = pe.snap(now[j], min_val=0, max_val=s.E - 1)
                    if not isinstance(t, int) or t >= 2:
                        pe.wait_ge(s.h_ready, t - 1)
                    b0, w = 2 + j % 2, 2 * s.F
                    if s.n == 0:
                        pe.matmul(ps[:, b0, 0:w], selc[:, bass.ds(t, 1)].broadcast_to([96, P]), gub_bf[:, :],
                                  start=True, stop=False)
                    pe.wait_ge(s.xgT_ready, t + 1)
                    for k in range(KD):
                        mm = pe.matmul(ps[:, b0, 0:w], xgT[:, j % 2, k, :], gu[:, bass.ds(e * (KD * w) + k * w, w)],
                                       start=(s.n == 1 and k == 0), stop=(k == KD - 1))
                    mm.then_inc(s.gu_done, 1)

                def turn_h(t, j):
                    if isinstance(t, int) and t == 0:
                        pe.wait_ge(s.qkv_read, NTT * (2 if s.n == 0 else 1))
                    pe.wait_ge(s.h_ready, t + 1)
                    if not isinstance(t, int) or t >= 2:
                        pe.wait_ge(s.hT_ready, t - 1)
                    for k in range(s.KF):
                        mm = pe.transpose(ps[0:s.FP, 4 + j % 2, k * P:(k + 1) * P], hbuf[:, j % 2, k * s.FP:(k + 1) * s.FP], ident)
                    mm.then_inc(s.hT_done, 1)

                def down(t, j):
                    e = pe.snap((now if j == 0 else before)[j], min_val=0, max_val=s.E - 1)
                    if not isinstance(t, int) or t >= 2:
                        pe.wait_ge(s.y_ready, t - 1)
                    if s.n == 0:
                        pe.matmul(ps[:, 6 + j % 2, 0:D], selc[:, bass.ds(t, 1)].broadcast_to([96, P]), dnb_bf[:, :],
                                  start=True, stop=False)
                    pe.wait_ge(s.hT_ready, t + 1)
                    for k in range(s.KF):
                        mm = pe.matmul(ps[:, 6 + j % 2, 0:D], hT[0:s.FP, j % 2, k, :],
                                       dn[0:s.FP, bass.ds(e * (s.KF * D) + k * D, D)],
                                       start=(s.n == 1 and k == 0), stop=(k == s.KF - 1))
                    mm.then_inc(s.y_done, 1)

                run_tiles(pe, s, [(0, 1, turn), (1, 1, up), (0, 4, experts), (2, 1, turn_h), (3, 1, down)])

            turn_and_route(L[0])
            project(L[0], 0)
            project(L[0], 1)
            rank(L[0])
            for i in range(2, 4):
                project(L[0], i)
            tile_experts(L[0])
            for i in range(NTT):
                place(L[0], i)
            for i in range(4, NTT):
                project(L[0], i)
            tiles(L[0])

            pe.wait_ge(s_wo0, 16)
            pe.sem_inc(s_pv, 1)

            def stack_ready(n, j):
                pe.wait_ge(s_hl, n + 1)

            def turn_stack(n, j):
                if not isinstance(n, int) or n >= 1:
                    pe.wait_ge(s_stk, n)
                half, h = j // 4, 2 * (j % 4)
                for tt in range(2):
                    q, k = (parts[half][:, tt, w, h:h + 2, :].rearrange("p h n -> p (h n)") for w in range(2))
                    pe.transpose(ps[:, 0, tt * P:(tt + 1) * P], q, ident)
                    mm = pe.transpose(ps[:, 0, SEQ + tt * P:SEQ + (tt + 1) * P], k, ident)
                mm.then_inc(s_stkT, 1)

            def stack_in(n, j):
                pe.wait_ge(s_stk, n + 1)

            def scores(h, j):
                if not isinstance(h, int) or h >= 2:
                    pe.wait_ge(s_exp, h - 1)
                bank = ps[:, 1 + j % 2, :]
                rows = slice(64 * (j % 2), 64 * (j % 2) + 64)
                q, k = (stk[rows, j // 2 % 2, w, :].bitcast(f32r) for w in range(2))
                pe.matmul(bank[:, 0:P], q[:, 0:P], k[:, 0:P], start=True, stop=False)
                pe.matmul(bank[:, 0:P], ident_bf[:, :], mask_bf[:, :], start=False, stop=True)
                pe.matmul(bank[:, P:3 * P], q[:, P:2 * P], k[:, :], start=True, stop=False)
                pe.matmul(bank[:, 2 * P:3 * P], ident_bf[:, :], mask_bf[:, :], start=False, stop=True).then_inc(s_sc, 1)

            def turn_probs(h, j):
                if isinstance(h, int) and h >= BATCH * HEADS - 2:
                    pe.wait_ge(s_exp, h + 1)
                for n in range(3):
                    mm = pe.transpose(ps[:, 3 + j % 2, n * P:(n + 1) * P], pr[:, j % 2, n * P:(n + 1) * P], ident)
                mm.then_inc(s_pT, 1)

            def values_in(n, j):
                if isinstance(n, int) and n == 0:
                    pe.wait_ge(L[0].y_ready, NT0)
                pe.wait_ge(s_vst, n + 1)

            def turned_in(r):
                def work(n, j):
                    if r < 3:
                        pe.wait_ge(s_pTr, n * 3 + r + 1)
                    else:
                        pe.wait_ge(s_pTa, n + 1)
                return work

            def attend(h, j):
                half, m = j // HALF, j % HALF
                o = ps[32 * (m % 4):32 * (m % 4) + 32, 5 + half, (m // 4) * SEQ:(m // 4 + 1) * SEQ]
                pe.matmul(o, vst[:, half, 0, m, :], prT[:, j % 2, 0:SEQ], start=True, stop=False)
                mm = pe.matmul(o[:, P:SEQ], vst[:, half, 1, m, :], prT[:, j % 2, SEQ:3 * P], start=False, stop=True)
                if m == HALF - 1:
                    mm.then_inc(s_pv, 1)

            def residual_read(b, j):
                pe.wait_ge(s_s, b + 1)

            def turn_back(n, j):
                pe.wait_ge(s_otr, n + 1)
                if not isinstance(n, int) or n >= 1:
                    pe.wait_ge(s_oTr, n)
                for tt in range(2):
                    for g in range(2):
                        mm = pe.transpose(ps[:, 7, tt * SEQ + g * P:tt * SEQ + (g + 1) * P], otb[:, g * SEQ + tt * P:g * SEQ + (tt + 1) * P], ident)
                mm.then_inc(s_oa, 1)

            def turn_rows(n, j):
                pe.wait_ge(s_on, n + 1)
                for tt in range(2):
                    mm = pe.transpose(ps[:, 7, tt * P:(tt + 1) * P], ost[:, tt, :], ident)
                mm.then_inc(s_oT, 1)

            def project0(tt):
                def work(b, j):
                    if tt == 0:
                        pe.wait_ge(s_oTr, b * 2 + 2)
                    for k in range(KD):
                        mm = pe.matmul(ps[:, 7, tt * D:(tt + 1) * D], oTs[:, k, tt * P:(tt + 1) * P], wo0_sb[:, k, :],
                                       start=(k == 0), stop=(k == KD - 1))
                    if tt == 1:
                        mm.then_inc(s_wo, 1)
                return work

            run_heads(pe, [(-4, HALF, stack_ready), (-4, 2, turn_stack), (-2, 2, stack_in), (-2, 1, scores), (0, 1, turn_probs),
                           (1, HALF, values_in),
                           (1, 4, turned_in(0)), (2, 4, turned_in(1)), (3, 4, turned_in(2)), (4, 4, turned_in(3)),
                           (1, 1, attend), (26, HEADS, residual_read), (10, HALF, turn_back),
                           (12, HALF, turn_rows), (22, HEADS, project0(0)), (23, HEADS, project0(1))])

            pe.wait_ge(s_s, BATCH)
            turn_and_route(L[1])
            project(L[1], 0)
            project(L[1], 1)
            rank(L[1])
            for i in range(2, 5):
                project(L[1], i)
            tile_experts(L[1])
            for i in range(NTT):
                place(L[1], i)
            for i in range(5, NTT):
                project(L[1], i)
            tiles(L[1])


            def shared_up(n):
                h, m = n // 4, n % 4
                if n >= 2:
                    pe.wait_ge(s_shr, n - 1)
                for w in range(2):
                    for k in range(KD):
                        mm = pe.matmul(ps[:, n % 2 + 2 * w, :], wsgu_sb[:, k, w * SH + m * P:w * SH + (m + 1) * P],
                                       L[1].xnT[:, k, h * 512:(h + 1) * 512], start=(k == 0), stop=(k == KD - 1))
                mm.then_inc(s_shd, 1)

            def shared_down(i):
                if i == 0 or i == 4:
                    pe.wait_ge(s_shr, i + 4)
                if i >= 2:
                    pe.wait_ge(L[1].f_ready, i - 1)
                for m in range(4):
                    mm = pe.matmul(ps[:, 4 + i % 2, 0:D], shg[:, i // 4, m, (i % 4) * P:(i % 4 + 1) * P], wsdn_sb[:, m, :],
                                   start=(m == 0), stop=(m == 3))
                mm.then_inc(s_sdn, 1)

            def keys_values(b):
                if b == 0:
                    pe.wait_ge(L[1].y_ready, NT1)
                pe.wait_ge(s_row1, b + 1)
                if b >= 2:
                    pe.wait_ge(s_qT1r, b - 1)
                    pe.wait_ge(s_a1, b - 1)
                    pe.wait_ge(s_bn1, b - 1)
                for g in range(2):
                    for tt in range(2):
                        mm = pe.transpose(ps[:, 4 + b % 2, g * SEQ + tt * P:g * SEQ + (tt + 1) * P],
                                          q1r[:, 2 * b + tt, g * P:(g + 1) * P], ident)
                mm.then_inc(s_qT1, 1)
                for g in range(2):
                    for tt in range(2):
                        i = 2 * b + tt
                        mm = pe.matmul(ps[:, 6 + b % 2, g * P:(g + 1) * P], q1r[:, i, g * P:(g + 1) * P], v1r[:, i, g * P:(g + 1) * P],
                                       start=(tt == 0), stop=(tt == 1))
                mm.then_inc(s_kv, 1)

            def queries(b):
                pe.wait_ge(s_kvr, b + 1)
                pe.wait_ge(s_qT1r, b + 1)
                for tt in range(2):
                    for g in range(2):
                        mm = pe.matmul(ps[:, 6 + b % 2, tt * D + g * P:tt * D + (g + 1) * P],
                                       q1T[:, g, b * SEQ + tt * P:b * SEQ + (tt + 1) * P], kvb[:, b % 2, g, :], start=True, stop=True)
                mm.then_inc(s_o1, 1)

            for what, n in MIXED:
                if what == "up":
                    shared_up(n)
                elif what == "keys":
                    keys_values(n)
                else:
                    queries(n)
            shared_up(6)
            shared_up(7)
            for i in range(NTT + 1):
                if i < NTT:
                    shared_down(i)
                    pe.wait_ge(s_a1n, i + 1)
                    if i >= 2:
                        pe.wait_ge(s_a1Tr, i - 1)
                    for k in range(KD):
                        mm = pe.transpose(ps[:, 6 + i % 2, k * P:(k + 1) * P], a1r[:, i, k * P:(k + 1) * P], ident)
                    mm.then_inc(s_a1T, 1)
                if i >= 1:
                    pe.wait_ge(s_a1Tr, i)
                    if i == 1:
                        pe.wait_ge(s_shr, 8)
                    if i >= 3:
                        pe.wait_ge(s_s1, i - 2)
                    for k in range(KD):
                        mm = pe.matmul(ps[:, (i - 1) % 2, 0:D], a1T[:, (i - 1) % 2, k, :], wo1_sb[:, k, :],
                                       start=(k == 0), stop=(k == KD - 1))
                    mm.then_inc(s_wo1, 1)

        @block.vector
        def _(ve):
            chain = [0]

            def link(ins):
                chain[0] += 1
                ins.then_inc(s_dve, 1)
                ve.wait_ge(s_dve, chain[0])

            def normalise(s):
                if s.n == 0:
                    for i in range(NTT):
                        if i % 4 == 0:
                            ve.wait_ge(s_x[i // 4], 16)
                        ins = ve.bn_stats(bnst[:, i, :], xr[:, i, :])
                    link(ins)
                for i in range(NTT):
                    ins = ve.bn_aggr(mv[:, i, :], bnst[:, i, :])
                link(ins)
                ve.tensor_scalar(sd[:, :], mv[:, :, 1], EPS, None, ALU.add).then_inc(s.ve_ready, 1)
                if s.n == 0:
                    ve.wait_ge(s_cst, 16)
                    for dst, c in ((ident_bf, C_ID), (mask_bf, C_MASK), (tri_bf, C_TRI)):
                        ve.tensor_copy(dst[:, :], cst[:, c:c + P]).then_inc(s_cbf, 1)
                ve.wait_ge(s.sd_ready, 1)
                link(ve.reciprocal(rstd[:, :], sd[:, :]))
                for i in range(NTT):
                    ve.tensor_scalar(xn[:, i, :], xr[:, i, :], mv[:, i, 0:1], rstd[:, i:i + 1], ALU.subtract, ALU.mult)\
                      .then_inc(s.xn_ready, 1)

            def route(s):
                E, NT = s.E, s.NT
                lg = lgt[:, 0:NTT * E].rearrange("p (t e) -> p t e", e=E)
                ohv = oh[:, 0:NTT * TOPK * E].rearrange("p (t k e) -> p t k e", t=NTT, e=E) if NTT * TOPK * E <= 1024 else None
                s4 = sl4[:, 0:NTT * TOPK * E].rearrange("p (t k e) -> p t k e", t=NTT, e=E)
                if s.n == 0:
                    ve.wait_ge(s_wr, 32)
                ve.wait_ge(s.logits_done, 1)
                out_l = ps[:, 2, 0:NTT * E].rearrange("p (t e) -> p t e", e=E)
                if s.n == 0:
                    link(ve.tensor_tensor(lg, out_l, rb0_sb[:, :].unsqueeze(1).broadcast_to([P, NTT, E]), ALU.add))
                else:
                    link(ve.tensor_copy(lg, out_l))
                for i in range(NTT):
                    ins = ve.max(top[:, i, :], lg[:, i, :])
                link(ins)
                ve.tensor_tensor(wraw[:, :, :], top[:, :, 0:TOPK], top[:, :, 0:1].broadcast_to([P, NTT, TOPK]), ALU.subtract)\
                  .then_inc(s.wexp_in, 1)
                for i in range(NTT):
                    ins = ve.max_index(topi[:, i, :], top[:, i, :], lg[:, i, :])
                link(ins)
                link(ve.tensor_copy(topf[:, :, :], topi[:, :, 0:TOPK]))
                oh2 = oh[:, 0:NTT * TOPK * E].rearrange("p (n e) -> p n e", e=E)
                link(ve.tensor_tensor(oh2, iota[:, 0:E].unsqueeze(1).broadcast_to([P, NTT * TOPK, E]),
                                      topf[:, :, :].rearrange("p t k -> p (t k)").unsqueeze(2).broadcast_to([P, NTT * TOPK, E]),
                                      ALU.is_equal))
                with nc.allow_low_precision("zeros and ones: a token's four experts differ"):
                    ve.tensor_reduce(mcnt[:, 0:NTT * E].rearrange("p (t e) -> p t e", e=E), ohv.rearrange("p t k e -> p t e k"),
                                     AX.X, ALU.add).then_inc(s.m_ready, 1)
                ve.wait_ge(s.wexp_out, 1)
                link(ve.tensor_reduce(wsum[:, :], wraw[:, :, :], AX.X, ALU.add))
                link(ve.reciprocal(wsum[:, :], wsum[:, :]))
                link(ve.tensor_tensor(wtop[:, :, :], wraw[:, :, :], wsum[:, :].unsqueeze(2).broadcast_to([P, NTT, TOPK]), ALU.mult))
                ve.wait_ge(s.rank_done, 1)
                link(ve.tensor_scalar(nti[:, 0:E], ps[:, 3, 256:256 + E], float(P - 1), None, ALU.add))
                link(ve.tensor_scalar(nti[:, 0:E], nti[:, 0:E], 7, 7, ALU.arith_shift_right, ALU.logical_shift_left))
                link(ve.tensor_copy(nts[:, 0:E], nti[:, 0:E]))
                link(ve.tensor_tensor_scan(enda[:, 0:E], ones_e[:, 0:E], nts[:, 0:E], 0.0, ALU.mult, ALU.add))
                link(ve.tensor_tensor(base[:, 0:E], enda[:, 0:E], nts[:, 0:E], ALU.subtract))
                link(ve.tensor_tensor(lg, ps[:, 3, 0:NTT * E].rearrange("p (t e) -> p t e", e=E),
                                      base[:, 0:E].unsqueeze(1).broadcast_to([P, NTT, E]), ALU.add))
                link(ve.tensor_tensor(s4, ohv, lg.unsqueeze(2).broadcast_to([P, NTT, TOPK, E]), ALU.mult))
                link(ve.tensor_reduce(slotf[:, :], s4.rearrange("p t k e -> p (t k) e"), AX.X, ALU.add))
                ve.tensor_copy(slotu[s.n][:, :], slotf[:, :])
                link(ve.tensor_copy(sloti[:, :], slotf[:, :]))
                ve.tensor_scalar(tq[:, :], sloti[:, :], 7, None, ALU.arith_shift_right)
                link(ve.tensor_scalar(sloti[:, :], sloti[:, :], P - 1, None, ALU.bitwise_and))
                ve.tensor_copy(tqf[:, :], tq[:, :])
                link(ve.tensor_copy(smf[:, :], sloti[:, :]))
                link(ve.tensor_scalar(nts[:, 0:E], enda[:, 0:E], 1.0 / P, tokid[:, 0:1], ALU.mult, ALU.is_le))
                link(ve.tensor_reduce(texcol[:, :], nts[:, 0:E], AX.X, ALU.add))
                ve.tensor_scalar(texcol[:, :], texcol[:, :], float(E - 1), None, ALU.min).then_inc(s.m_ready, 1)
                for i in range(NTT):
                    if i >= 4:
                        ve.wait_ge(s.ab_used, i - 3)
                    pick = slice(i * TOPK, (i + 1) * TOPK)
                    ve.tensor_tensor(amat[:, i % 4, :, :], iota.unsqueeze(1).broadcast_to([P, TOPK, P]),
                                     smf[:, pick].unsqueeze(2).broadcast_to([P, TOPK, P]), ALU.is_equal)
                    ve.tensor_tensor(eq4[:, i % 4, :, 0:NT], iota[:, 0:NT].unsqueeze(1).broadcast_to([P, TOPK, NT]),
                                     tqf[:, pick].unsqueeze(2).broadcast_to([P, TOPK, NT]), ALU.is_equal).then_inc(s.eq_ready, 1)
                ve.wait_ge(s.rank_done, 2)
                ve.tensor_copy(texi[:, :], ps[:, 3, 384:384 + P])
                if s.n == 0:
                    link(ve.tensor_scalar(selc[:, :], ps[0:96, 3, 384:384 + NT], pmod[0:96, :], None, ALU.is_equal))
                ve.wait_ge(s.ab_used, NTT)
                link(ve.tensor_copy(gidx[:, 0:NT], ps[:, 2, 0:NT]))
                ve.tensor_copy(wtile[:, 0:NT], ps[:, 2, NT:2 * NT]).then_inc(s.idx_ready, 1)

            def tiles(s):
                F = s.F

                def gate(t, j):
                    ve.wait_ge(s.gu_done, t + 1)
                    g, u = ps[:, 2 + j % 2, 0:F], ps[:, 2 + j % 2, F:2 * F]
                    if s.n == 0:
                        ve.tensor_scalar(gbuf[:, j % 2, :], g, LIMIT, None, ALU.min).then_inc(s.g_ready, 1)
                        ve.tensor_scalar(ubuf[:, j % 2, :], u, LIMIT, -LIMIT, ALU.min, ALU.max).then_inc(s.u_ready, 1)
                        ve.wait_ge(s.u_ready, t + 1)
                        ve.scalar_tensor_tensor(out=ubuf[:, j % 2, :], in0=ubuf[:, j % 2, :], scalar=1.0, in1=gbuf[:, j % 2, :],
                                                op0=ALU.add, op1=ALU.mult).then_inc(s.h1_ready, 1)
                        ve.wait_ge(s.h1_ready, t + 1)
                        ve.wait_ge(s.sig_ready, t + 1)
                    else:
                        ve.wait_ge(s.sig_ready, t + 1)
                        ve.tensor_tensor(gbuf[:, j % 2, 0:F], sig[:, j % 2, 0:F], g, ALU.mult).then_inc(s.h1_ready, 1)
                        ve.wait_ge(s.h1_ready, t + 1)
                    if not isinstance(t, int) or t >= 2:
                        ve.wait_ge(s.hT_done, t - 1)
                    if s.n == 0:
                        ve.tensor_tensor(hbuf[:, j % 2, :], ubuf[:, j % 2, :], sig[:, j % 2, :], ALU.mult).then_inc(s.h_ready, 1)
                    else:
                        ve.tensor_tensor(hbuf[:, j % 2, 0:F], gbuf[:, j % 2, 0:F], u, ALU.mult).then_inc(s.h_ready, 1)

                def turned(t, j):
                    ve.wait_ge(s.hT_done, t + 1)
                    if not isinstance(t, int) or t >= 2:
                        ve.wait_ge(s.y_done, t - 1)
                    ve.tensor_copy(hT[0:s.FP, j % 2, 0:s.KF, :],
                                   ps[0:s.FP, 4 + j % 2, 0:s.KF * P].rearrange("p (k t) -> p k t", t=P)).then_inc(s.hT_ready, 1)

                def row_bias(w):
                    def work(i, j):
                        row = rows1[:, w, bass.ds(i, 1), :].rearrange("p o n -> p (o n)")
                        ve.tensor_tensor(row, row, b768_sb[:, w * D:(w + 1) * D], ALU.add).then_inc(s_z, 1)
                    return work

                def row_silu(i, j):
                    ve.wait_ge(s_e, i + 1)
                    vu = rows1[:, 1:3, bass.ds(i, 1), :].rearrange("p w o n -> p (w o) n")
                    ve.tensor_tensor(vu, vu, rowsig, ALU.mult).then_inc(s_rowm, 1)

                if s.n == 1:
                    ve.wait_ge(s.qkv_read, NTT)
                run_tiles(ve, s, [(2, 1, turned), (1, 1, gate)],
                          [(0, 8, row_bias(0)), (1, 8, row_bias(1)), (2, 8, row_bias(2)), (5, 8, row_silu)])

            link(ve.memset(ones_e[:, :], 1.0))
            ve.memset(ones_bf[:, :], 1.0).then_inc(s_cbf, 1)
            normalise(L[0])
            route(L[0])
            tiles(L[0])

            def smallest(h, j):
                ve.wait_ge(s_sc, h + 1)
                for tt, cols in ((0, slice(0, P)), (1, slice(P, 3 * P))):
                    ve.tensor_reduce(mxs[:, j % 4, tt:tt + 1], ps[:, 1 + j % 2, cols], AX.X, ALU.min).then_inc(s_mx, 1)

            def probs_turned(r):
                def work(n, j):
                    ve.wait_ge(s_pT, n * 4 + r + 1)
                    ve.tensor_copy(prT[:, r % 2, :], ps[:, 3 + r % 2, 0:3 * P]).then_inc(s_pTr, 1)
                return work

            def scale_rows(n, j):
                ve.wait_ge(s_oa, n + 1)
                o = ps[:, 7, :].rearrange("p (t h d) -> p t h d", t=2, d=32)
                ve.reciprocal(rec[:, :, :], o[:, :, :, DH]).then_inc(s_rec, 1)
                ve.wait_ge(s_rec, n + 1)
                ve.tensor_tensor(ost.rearrange("p t (h d) -> p t h d", d=DH), o[:, :, :, 0:DH],
                                 rec[:, :, :].unsqueeze(3).broadcast_to([P, 2, HALF, DH]), ALU.mult).then_inc(s_on, 1)

            def total(j):
                def work(b, _):
                    ve.wait_ge(L[0].cg_full[j], b * 64 + 64)
                    ve.wait_ge(s_f, b * 2 + j + 2)
                    ve.tensor_tensor(csum0.rearrange("p (k n) -> p k n", k=2), cg[:, j, 0:2, :], cg[:, j, 2:4, :], ALU.add)\
                      .then_inc(s_fp, 1)
                    ve.wait_ge(s_fp, b * 2 + j + 1)
                    ve.tensor_tensor(fsum[:, j, :], csum0[:, 0:D], csum0[:, D:2 * D], ALU.add).then_inc(s_f, 1)
                return work

            def gate0(b, j):
                ve.wait_ge(s_fe, b + 1)
                ve.scalar_tensor_tensor(out=fsil, in0=ftanh, scalar=1.0, in1=fsum, op0=ALU.add, op1=ALU.mult).then_inc(s_sil, 1)

            def residual(b, j):
                ve.wait_ge(s_sil, b + 1)
                ve.wait_ge(s_wo, b + 1)
                ve.scalar_tensor_tensor(out=fsil, in0=fsil, scalar=0.5, in1=ps[:, 7, :].rearrange("p (t n) -> p t n", t=2),
                                        op0=ALU.mult, op1=ALU.mult).then_inc(s_s, 1)

            def add_residual(b, j):
                ve.wait_ge(s_s, b + 1)
                rows = xr[:, bass.ds(b * 2, 2), :]
                ve.tensor_tensor(rows, rows, fsil, ALU.add).then_inc(s_x1, 1)

            def row_stats(b, j):
                ve.wait_ge(s_x1, b + 1)
                for tt in range(2):
                    ve.bn_stats(bnst[:, bass.ds(b * 2 + tt, 1), :].rearrange("p o n -> p (o n)"),
                                xr[:, bass.ds(b * 2 + tt, 1), :].rearrange("p o n -> p (o n)")).then_inc(s_x1n, 1)

            ve.sem_inc(s_f, 2)
            run_heads(ve, [(-2, 1, smallest), (0, 4, probs_turned(0)), (1, 4, probs_turned(1)), (2, 4, probs_turned(2)),
                           (12, HEADS, total(0)), (16, HEADS, total(1)), (10, HALF, scale_rows), (21, HEADS, gate0),
                           (23, HEADS, residual), (24, HEADS, add_residual), (25, HEADS, row_stats)])
            ve.wait_ge(s_x1n, NTT)
            normalise(L[1])
            route(L[1])
            tiles(L[1])

            def elu(b):
                two = slice(2 * b, 2 * b + 2)
                ve.wait_ge(s_qe, b + 1)
                link(ve.tensor_scalar(qexp[:, two, :], qexp[:, two, :], 1.0, -1.0, ALU.min, ALU.add))
                ve.scalar_tensor_tensor(out=q1r[:, two, :], in0=q1r[:, two, :], scalar=0.0, in1=qexp[:, two, :],
                                        op0=ALU.max, op1=ALU.add).then_inc(s_row1, 1)

            def shared(n):
                ve.wait_ge(s_shsig, n + 1)
                link(ve.tensor_tensor(shs[:, n % 2, :], shs[:, n % 2, :], ps[:, n % 2, :], ALU.mult))
                ve.tensor_tensor(shg[:, n // 4, n % 4, :], shs[:, n % 2, :], ps[:, 2 + n % 2, :], ALU.mult).then_inc(s_shr, 1)

            elu(0)
            elu(1)
            for what, n in MIXED:
                if what == "up":
                    shared(n)
                    if n < 2:
                        elu(n + 2)
                elif what == "keys":
                    ve.wait_ge(s_kv, n + 1)
                    if n >= 2:
                        ve.wait_ge(s_o1, n - 1)
                    ve.tensor_tensor(kvb[:, n % 2, :, :], ps[:, 6 + n % 2, 0:D].rearrange("p (g n) -> p g n", g=2),
                                     bdiag.unsqueeze(1).broadcast_to([P, 2, P]), ALU.mult).then_inc(s_kvr, 1)
                else:
                    ve.wait_ge(s_a1, n + 1)
                    for tt in range(2):
                        ins = ve.bn_stats(bnst[:, 2 * n + tt, :], a1r[:, 2 * n + tt, :])
                    ins.then_inc(s_bn1, 1)
            ve.wait_ge(s_bn1, BATCH)
            for i in range(NTT):
                ins = ve.bn_aggr(mv[:, i, :], bnst[:, i, :])
            link(ins)
            ve.tensor_scalar(sd[:, :], mv[:, :, 1], EPS, None, ALU.add).then_inc(L[1].ve_ready, 1)
            ve.wait_ge(L[1].sd_ready, 2)
            link(ve.reciprocal(rstd[:, :], sd[:, :]))

            ve.scalar_tensor_tensor(out=nmr[:, :], in0=mv[:, :, 0], scalar=-1.0, in1=rstd[:, :], op0=ALU.mult, op1=ALU.mult)\
              .then_inc(s_nmr, 1)

            def mark(ins):
                chain[0] += 1
                ins.then_inc(s_dve, 1)
                return chain[0]

            done = {}

            def affine_scale(i):
                ve.wait_ge(s_a1h, i + 1)
                done["scale", i] = mark(ve.tensor_tensor(a1r[:, i, :], a1r[:, i, :], lng_sb, ALU.mult))

            def affine_shift(i):
                ve.wait_ge(s_dve, done["scale", i])
                done["shift", i] = mark(ve.tensor_tensor(a1r[:, i, :], a1r[:, i, :], lnb_sb[:, :], ALU.add))

            def affine_gate(i):
                ve.wait_ge(s_dve, done["shift", i])
                ve.tensor_tensor(a1r[:, i, :], a1r[:, i, :], u1r[:, i, :], ALU.mult).then_inc(s_a1n, 1)

            def finish_bias(i):
                ve.wait_ge(s_wo1, i + 1)
                ve.tensor_tensor(fbuf[:, i % 2, :], ps[:, i % 2, 0:D], bo1_sb, ALU.add).then_inc(s_s1, 1)

            def finish_gate(i):
                ve.wait_ge(s_s1, i + 1)
                ve.wait_ge(s_gate1, i + 1)
                done["gate", i] = mark(ve.tensor_tensor(fbuf[:, i % 2, :], fbuf[:, i % 2, :], f1r[:, i, :], ALU.mult))

            def finish_add(i):
                ve.wait_ge(s_dve, done["gate", i])
                ve.tensor_tensor(xr[:, i, :], xr[:, i, :], fbuf[:, i % 2, :], ALU.add).then_inc(L[1].g_done, 1)

            for i in (0, 2):
                shared(6 + i // 2)
                for step in (affine_scale, affine_shift, affine_gate):
                    step(i)
                    step(i + 1)
            for i in range(NTT + 2):
                if i < NTT:
                    ve.wait_ge(s_sdn, i + 1)
                    ve.wait_ge(s_f1, i + 1)
                    ve.tensor_tensor(f1r[:, i, :], f1r[:, i, :], ps[:, 4 + i % 2, 0:D], ALU.add).then_inc(L[1].f_ready, 1)
                if 1 <= i <= NTT:
                    ve.wait_ge(L[1].fsig_ready, i)
                    ve.tensor_tensor(f1r[:, i - 1, :], f1r[:, i - 1, :], fsig[:, (i - 1) % 2, :], ALU.mult).then_inc(s_gate1, 1)
                for affine, finish in ((affine_scale, finish_bias), (affine_shift, finish_gate), (affine_gate, finish_add)):
                    if i + 4 < NTT:
                        affine(i + 4)
                    if i >= 2:
                        finish(i - 2)


def kernel(**inputs):
    import numpy as np
    import concourse.bacc as bacc
    from concourse.bass_utils import run_bass_kernel_spmd

    a = {k: np.asarray(v) for k, v in inputs.items()}

    def rows(w):
        return np.ascontiguousarray(w.reshape(-1, P, w.shape[-1]).transpose(1, 0, 2))

    def experts(w):
        e, h, n = w.shape
        p = min(h, P)
        return np.ascontiguousarray(w.reshape(e, h // p, p, n).transpose(2, 0, 1, 3).reshape(p, e, -1))

    def apart(w):
        return np.concatenate([w[..., ::2], w[..., 1::2]], axis=-1)

    arrays = dict(
        x=a["L0_attn_x"].reshape(TOK, D),
        consts=constants(),
        wqkv0=rows(np.concatenate([a["L0_attn_Wq"].T, a["L0_attn_Wk"].T, a["L0_attn_Wv"].T], axis=1)),
        wo0=rows(a["L0_attn_Wo"].T),
        wr0=rows(a["L0_ffn_router_weight"].T),
        rb0=a["L0_ffn_router_bias"].reshape(1, E0),
        gub0=apart(a["L0_ffn_gate_up_proj_bias"]),
        dnb0=a["L0_ffn_down_proj_bias"],
        gu0=experts(apart(a["L0_ffn_gate_up_proj"])),
        dn0=experts(a["L0_ffn_down_proj"]),
        wqvu1=rows(np.concatenate([a["L1_attn_Wqk"], a["L1_attn_Wv"], a["L1_attn_Wu"]], axis=1)),
        b768=np.concatenate([a["L1_attn_bqk"], a["L1_attn_bv"], a["L1_attn_bu"]]).reshape(1, 3 * D),
        wo1=rows(a["L1_attn_Wo"]),
        lnrow=np.stack([a["L1_attn_ln_g"], a["L1_attn_ln_b"]]),
        bo1=a["L1_attn_bo"].reshape(1, D),
        wr1=rows(a["L1_ffn_router_w"]),
        gu1=experts(np.concatenate([a["L1_ffn_w_gate"], a["L1_ffn_w_up"]], axis=-1)),
        dn1=experts(a["L1_ffn_w_down"]),
        wsgu=rows(np.concatenate([a["L1_ffn_ws_gate"], a["L1_ffn_ws_up"]], axis=1)),
        wsdn=rows(a["L1_ffn_ws_down"]),
    )
    arrays = {k: np.ascontiguousarray(v) for k, v in arrays.items()}
    nc = bacc.Bacc("TRN2", target_bir_lowering=False, num_devices=1)
    args = [nc.dram_tensor("in_" + k, v.shape, mybir.dt.from_np(v.dtype), kind="ExternalInput").ap() for k, v in arrays.items()]
    args.append(nc.dram_tensor("out", (TOK, D), mybir.dt.float32, kind="ExternalOutput").ap())
    build_program(nc, *args)
    r = run_bass_kernel_spmd(nc, [{"in_" + k: v for k, v in arrays.items()}], core_ids=[0])
    return r.results[0]["out"].reshape(BATCH, SEQ, D)
```
